# Optimizing a Trainium2 kernel written in Bass

```python
import numpy as np
import jax
import jax.numpy as jnp

def _softmax(x, axis=-1):
    return jax.nn.softmax(x, axis=axis)

def _gelu(x):
    return jax.nn.gelu(x, approximate=True)

def _silu(x):
    return jax.nn.silu(x)

def _sigmoid(x):
    return jax.nn.sigmoid(x)

def _layernorm(x, axis=-1, eps=1e-05):
    m = jnp.mean(x, axis=axis, keepdims=True)
    v = jnp.var(x, axis=axis, keepdims=True)
    return (x - m) / jnp.sqrt(v + eps)

def _scatter_add(tgt, idx, src, axis=0):
    return tgt.at[idx].add(src)

def _segment_sum(src, seg, n):
    return jax.ops.segment_sum(src, seg, n)
kernel_name = 'mk_gps_d1_gnn_r8_cb3bcf'

def setup_inputs(seed: int=0):
    np.random.seed(seed)
    _w = jnp.asarray

    def _rec_inputs():
        import jax
        import jax.numpy as jnp
        _gk = jax.random.key(seed)
        x = -0.0006008 + 1.001 * jax.random.normal(jax.random.fold_in(_gk, 1), (6250, 256), jnp.float32)
        src = jax.random.randint(jax.random.fold_in(_gk, 2), (100000,), 0, 6250, jnp.int32)
        dst = jnp.minimum((6250 * jax.random.uniform(jax.random.fold_in(_gk, 3), (100000,)) ** 2.0).astype(jnp.int32), 49999)
        _o = jnp.argsort(dst, stable=True)
        src = src[_o]
        dst = dst[_o]
        edge_attr_20 = jax.random.uniform(jax.random.fold_in(_gk, 11), (100000, 20), jnp.float32, 0.0, 1)
        return (x, src, dst, edge_attr_20)
    x, src, dst, edge_attr_20 = _rec_inputs()

    def _L0_gnn_setup():
        import jax, jax.numpy as jnp
        import numpy as np
        N, E, HDIM, NG = (1250, 40000, 256, 20)
        BN_EPS = 1e-05
        key = jax.random.key(seed)
        ks = jax.random.split(key, 12)
        inp = {'x': jax.random.normal(ks[0], (N, HDIM), dtype=jnp.float32), 'rbf': jax.random.uniform(ks[1], (E, NG), dtype=jnp.float32), 'ei': jax.random.randint(ks[2], (2, E), 0, N, dtype=jnp.int64), 'Wf1': jax.random.normal(ks[3], (NG, HDIM), dtype=jnp.float32) / np.sqrt(NG), 'bf1': jnp.zeros((HDIM,), dtype=jnp.float32), 'Wf2': jax.random.normal(ks[4], (HDIM, HDIM), dtype=jnp.float32) / np.sqrt(HDIM), 'bf2': jnp.zeros((HDIM,), dtype=jnp.float32), 'Wu1': jax.random.normal(ks[5], (HDIM, HDIM), dtype=jnp.float32) / np.sqrt(HDIM), 'bu1': jnp.zeros((HDIM,), dtype=jnp.float32), 'Wu2': jax.random.normal(ks[6], (HDIM, HDIM), dtype=jnp.float32) / np.sqrt(HDIM), 'bu2': jnp.zeros((HDIM,), dtype=jnp.float32), 'gamma': jnp.ones((HDIM,), dtype=jnp.float32), 'beta': jnp.zeros((HDIM,), dtype=jnp.float32)}
        return inp
    _L0_gnn_all = _L0_gnn_setup()
    _L0_gnn_in = {k: v for k, v in _L0_gnn_all.items() if k in ('Wf1', 'bf1', 'Wf2', 'bf2', 'Wu1', 'bu1', 'Wu2', 'bu2', 'gamma', 'beta')}
    del _L0_gnn_all

    def _L0_mix_setup():
        import jax, jax.numpy as jnp
        import numpy as np
        B, N, C, H = (8, 2048, 256, 8)
        D = C // H
        GH = C // 4
        key = jax.random.key(seed)
        ks = jax.random.split(key, 6)
        s = 0.02
        return {'x': jax.random.normal(ks[0], (B, N, C), dtype=jnp.float32), 'Wqkv': jax.random.normal(ks[1], (C, 3 * C), dtype=jnp.float32) * s, 'Wproj': jax.random.normal(ks[2], (C, C), dtype=jnp.float32) * s, 'bproj': jnp.zeros((C,), dtype=jnp.float32), 'ln_g': jnp.ones((C,), dtype=jnp.float32), 'ln_b': jnp.zeros((C,), dtype=jnp.float32), 'Wg1': jax.random.normal(ks[3], (C, GH), dtype=jnp.float32) * s, 'bg1': jnp.zeros((GH,), dtype=jnp.float32), 'Wg2': jax.random.normal(ks[4], (GH, C), dtype=jnp.float32) * s, 'bg2': jnp.zeros((C,), dtype=jnp.float32)}
    _L0_mix_all = _L0_mix_setup()
    _L0_mix_in = {k: v for k, v in _L0_mix_all.items() if k in ('Wqkv', 'Wproj', 'bproj', 'ln_g', 'ln_b', 'Wg1', 'bg1', 'Wg2', 'bg2')}
    del _L0_mix_all

    def _L0_ffn_setup():
        import jax, jax.numpy as jnp
        import numpy as np
        DIM = 256
        H = 8
        D = 64
        G = 64
        INNER = H * D
        SCALE = D ** (-0.5)
        key = jax.random.key(seed)
        ks = jax.random.split(key, 12)
        B, N = (4, 2048)
        x = jax.random.normal(ks[0], (B, N, DIM), dtype=jnp.float32)
        s = lambda fan_in: 1.0 / np.sqrt(fan_in)
        W_fx = jax.random.normal(ks[1], (DIM, INNER), dtype=jnp.float32) * s(DIM)
        b_fx = jnp.zeros((INNER,), dtype=jnp.float32)
        W_x = jax.random.normal(ks[2], (DIM, INNER), dtype=jnp.float32) * s(DIM)
        b_x = jnp.zeros((INNER,), dtype=jnp.float32)
        A = jax.random.normal(ks[3], (G, D), dtype=jnp.float32)
        Q, _ = jnp.linalg.qr(A.T)
        W_slice = Q[:, :G].astype(jnp.float32)
        b_slice = jnp.zeros((G,), dtype=jnp.float32)
        W_q = jax.random.normal(ks[4], (D, D), dtype=jnp.float32) * s(D)
        W_k = jax.random.normal(ks[5], (D, D), dtype=jnp.float32) * s(D)
        W_v = jax.random.normal(ks[6], (D, D), dtype=jnp.float32) * s(D)
        W_out = jax.random.normal(ks[7], (INNER, DIM), dtype=jnp.float32) * s(INNER)
        b_out = jnp.zeros((DIM,), dtype=jnp.float32)
        temperature = jnp.ones((1, H, 1, 1), dtype=jnp.float32) * 0.5
        return {'x': x, 'W_fx': W_fx, 'b_fx': b_fx, 'W_x': W_x, 'b_x': b_x, 'W_slice': W_slice, 'b_slice': b_slice, 'W_q': W_q, 'W_k': W_k, 'W_v': W_v, 'W_out': W_out, 'b_out': b_out, 'temperature': temperature}
    _L0_ffn_all = _L0_ffn_setup()
    _L0_ffn_in = {k: v for k, v in _L0_ffn_all.items() if k in ('W_fx', 'b_fx', 'W_x', 'b_x', 'W_slice', 'b_slice', 'W_q', 'W_k', 'W_v', 'W_out', 'b_out', 'temperature')}
    del _L0_ffn_all
    return {'x': x, 'src': src, 'dst': dst, 'edge_attr_20': edge_attr_20, 'L0_gnn_Wf1': _L0_gnn_in['Wf1'], 'L0_gnn_bf1': _L0_gnn_in['bf1'], 'L0_gnn_Wf2': _L0_gnn_in['Wf2'], 'L0_gnn_bf2': _L0_gnn_in['bf2'], 'L0_gnn_Wu1': _L0_gnn_in['Wu1'], 'L0_gnn_bu1': _L0_gnn_in['bu1'], 'L0_gnn_Wu2': _L0_gnn_in['Wu2'], 'L0_gnn_bu2': _L0_gnn_in['bu2'], 'L0_gnn_gamma': _L0_gnn_in['gamma'], 'L0_gnn_beta': _L0_gnn_in['beta'], 'L0_mix_Wqkv': _L0_mix_in['Wqkv'], 'L0_mix_Wproj': _L0_mix_in['Wproj'], 'L0_mix_bproj': _L0_mix_in['bproj'], 'L0_mix_ln_g': _L0_mix_in['ln_g'], 'L0_mix_ln_b': _L0_mix_in['ln_b'], 'L0_mix_Wg1': _L0_mix_in['Wg1'], 'L0_mix_bg1': _L0_mix_in['bg1'], 'L0_mix_Wg2': _L0_mix_in['Wg2'], 'L0_mix_bg2': _L0_mix_in['bg2'], 'L0_ffn_W_fx': _L0_ffn_in['W_fx'], 'L0_ffn_b_fx': _L0_ffn_in['b_fx'], 'L0_ffn_W_x': _L0_ffn_in['W_x'], 'L0_ffn_b_x': _L0_ffn_in['b_x'], 'L0_ffn_W_slice': _L0_ffn_in['W_slice'], 'L0_ffn_b_slice': _L0_ffn_in['b_slice'], 'L0_ffn_W_q': _L0_ffn_in['W_q'], 'L0_ffn_W_k': _L0_ffn_in['W_k'], 'L0_ffn_W_v': _L0_ffn_in['W_v'], 'L0_ffn_W_out': _L0_ffn_in['W_out'], 'L0_ffn_b_out': _L0_ffn_in['b_out'], 'L0_ffn_temperature': _L0_ffn_in['temperature']}

def reference(x, src, dst, edge_attr_20, L0_gnn_Wf1, L0_gnn_bf1, L0_gnn_Wf2, L0_gnn_bf2, L0_gnn_Wu1, L0_gnn_bu1, L0_gnn_Wu2, L0_gnn_bu2, L0_gnn_gamma, L0_gnn_beta, L0_mix_Wqkv, L0_mix_Wproj, L0_mix_bproj, L0_mix_ln_g, L0_mix_ln_b, L0_mix_Wg1, L0_mix_bg1, L0_mix_Wg2, L0_mix_bg2, L0_ffn_W_fx, L0_ffn_b_fx, L0_ffn_W_x, L0_ffn_b_x, L0_ffn_W_slice, L0_ffn_b_slice, L0_ffn_W_q, L0_ffn_W_k, L0_ffn_W_v, L0_ffn_W_out, L0_ffn_b_out, L0_ffn_temperature):
    import jax
    import jax.numpy as jnp

    def _L0_gnn_ref(x, rbf, Wf1, bf1, Wf2, bf2, Wu1, bu1, Wu2, bu2, gamma, beta, ei):
        import jax, jax.numpy as jnp
        import numpy as np
        N, E, HDIM, NG = (1250, 40000, 256, 20)
        BN_EPS = 1e-05
        row, col = (ei[0], ei[1])
        filt = jax.nn.silu(rbf @ Wf1 + bf1) @ Wf2 + bf2
        msg = x[col] * filt
        agg = jax.ops.segment_sum(msg, row, num_segments=x.shape[0])
        h = jax.nn.silu(agg @ Wu1 + bu1) @ Wu2 + bu2
        mean = jnp.mean(h, axis=0)
        var = jnp.mean(jnp.square(h - mean), axis=0)
        bn = gamma * (h - mean) * jax.lax.rsqrt(var + BN_EPS) + beta
        return x + bn

    def _L0_mix_ref(x, Wqkv, Wproj, bproj, ln_g, ln_b, Wg1, bg1, Wg2, bg2):
        import jax, jax.numpy as jnp
        import numpy as np
        B, N, C, H = (8, 2048, 256, 8)
        D = C // H
        GH = C // 4
        b, n, c = x.shape
        h, d = (H, D)
        qkv = (x @ Wqkv).reshape(b, n, 3, h, d)
        q, k, v = (qkv[:, :, 0], qkv[:, :, 1], qkv[:, :, 2])
        k = jax.nn.softmax(k, axis=1)
        context = jnp.einsum('bnhd,bnhv->bhdv', k, v)
        out = jnp.einsum('bnhd,bhdv->bnhv', q, context).reshape(b, n, c)
        mu = jnp.mean(x, axis=-1, keepdims=True)
        var = jnp.var(x, axis=-1, keepdims=True)
        xn = (x - mu) * jax.lax.rsqrt(var + 1e-05) * ln_g + ln_b
        hgate = jax.nn.gelu(xn @ Wg1 + bg1, approximate=False)
        gate = jax.nn.sigmoid(hgate @ Wg2 + bg2)
        return out * gate @ Wproj + bproj

    def _L0_ffn_ref(x, W_fx, b_fx, W_x, b_x, W_slice, b_slice, W_q, W_k, W_v, W_out, b_out, temperature):
        import jax, jax.numpy as jnp
        import numpy as np
        DIM = 256
        H = 8
        D = 64
        G = 64
        INNER = H * D
        SCALE = D ** (-0.5)
        B, N, _ = x.shape
        fx_mid = (x @ W_fx + b_fx).reshape(B, N, H, D).transpose(0, 2, 1, 3)
        x_mid = (x @ W_x + b_x).reshape(B, N, H, D).transpose(0, 2, 1, 3)
        temp = jnp.clip(temperature, 0.1, 5.0)
        slice_weights = jax.nn.softmax((x_mid @ W_slice + b_slice) / temp, axis=-1)
        slice_norm = slice_weights.sum(axis=2)
        slice_token = jnp.einsum('bhnc,bhng->bhgc', fx_mid, slice_weights)
        slice_token = slice_token / (slice_norm[..., None] + 1e-05)
        q = slice_token @ W_q
        k = slice_token @ W_k
        v = slice_token @ W_v
        attn = jax.nn.softmax(jnp.einsum('bhgc,bhkc->bhgk', q, k) * SCALE, axis=-1)
        out_slice = jnp.einsum('bhgk,bhkc->bhgc', attn, v)
        out_x = jnp.einsum('bhgc,bhng->bhnc', out_slice, slice_weights)
        out_x = out_x.transpose(0, 2, 1, 3).reshape(B, N, INNER)
        return out_x @ W_out + b_out
    edge_index = jnp.stack([src, dst])
    xn = _layernorm(x, axis=-1)
    x = x + _L0_gnn_ref(xn, edge_attr_20, L0_gnn_Wf1, L0_gnn_bf1, L0_gnn_Wf2, L0_gnn_bf2, L0_gnn_Wu1, L0_gnn_bu1, L0_gnn_Wu2, L0_gnn_bu2, L0_gnn_gamma, L0_gnn_beta, edge_index) + _L0_mix_ref(xn[None], L0_mix_Wqkv, L0_mix_Wproj, L0_mix_bproj, L0_mix_ln_g, L0_mix_ln_b, L0_mix_Wg1, L0_mix_bg1, L0_mix_Wg2, L0_mix_bg2)[0]
    x = x + _L0_ffn_ref(_layernorm(x, axis=-1)[None], L0_ffn_W_fx, L0_ffn_b_fx, L0_ffn_W_x, L0_ffn_b_x, L0_ffn_W_slice, L0_ffn_b_slice, L0_ffn_W_q, L0_ffn_W_k, L0_ffn_W_v, L0_ffn_W_out, L0_ffn_b_out, L0_ffn_temperature)[0]
    return x

_drawn_inputs = setup_inputs


def setup_inputs(seed=0):
    import zlib

    import numpy as np

    out = dict(_drawn_inputs(seed))
    spreads = {'L0_gnn_bf1': (0.0, 0.568),
     'L0_gnn_bf2': (0.0, 0.292),
     'L0_gnn_bu1': (0.0, 2.0),
     'L0_gnn_bu2': (0.0, 2.0),
     'L0_gnn_gamma': (1.0, 0.6),
     'L0_gnn_beta': (0.0, 0.8),
     'L0_mix_bproj': (0.0, 0.8),
     'L0_mix_ln_g': (1.0, 0.6),
     'L0_mix_ln_b': (0.0, 0.8),
     'L0_mix_bg1': (0.0, 0.8),
     'L0_mix_bg2': (0.0, 0.8),
     'L0_ffn_b_fx': (0.0, 0.562),
     'L0_ffn_b_x': (0.0, 2.0),
     'L0_ffn_b_slice': (0.0, 2.0),
     'L0_ffn_b_out': (0.0, 0.8),
     'L0_ffn_temperature': (0.5, 0.6)}
    factors = {'L0_mix_Wqkv': 8.0,
     'L0_mix_Wproj': 8.0,
     'L0_mix_Wg1': 8.0,
     'L0_mix_Wg2': 8.0,
     'L0_ffn_W_x': 23.668,
     'L0_ffn_W_slice': 24.134,
     'L0_ffn_W_q': 22.761,
     'L0_ffn_W_k': 22.462,
     'L0_ffn_W_fx': 2.892}
    for name, (base, spread) in spreads.items():
        noise = np.random.default_rng([zlib.crc32(name.encode()), seed]).standard_normal(out[name].shape)
        drawn = base * np.exp(spread * noise) if base else spread * noise
        out[name] = jnp.asarray(drawn.astype(out[name].dtype))
    for name, factor in factors.items():
        out[name] = (out[name] * factor).astype(out[name].dtype)
    return out
```

```python
from contextlib import ExitStack

import concourse.bass as bass
from concourse import mybir
from concourse.alu_op_type import AluOpType as ALU

F32 = mybir.dt.float32
F32R = mybir.dt.float32r
I32 = mybir.dt.int32
ACT = mybir.ActivationFunctionType
X = mybir.AxisListType.X
ds = bass.ds

P = 128
NODES, C = 6250, 256
CB = C // P
NT = -(-NODES // P)
TAIL = NODES - (NT - 1) * P
NPAD = NT * P
GT = 7
NG = NT // GT
GC = GT * P
HC = GC // 2
EDGES, EF = 100000, 20
ET = 8
EC = ET * P
NCH = 2 * -(-EDGES // (2 * EC))
EPAD = NCH * EC
TRASH = NODES
PAD_SRC = NODES + P
ROWS = -(-(PAD_SRC + 1) // P) * P
TABLES = 2
MH, MD = 8, 32
GH = C // 4
FH, FD, FG = 8, 64, 64
HG = FH * FG
HGB = HG // P
EPS = 1e-5
XW = C + 2


def tail_cols(s, h):
    return max(0, min(HC, NODES - (NG - 1) * GC - h * HC))


def rows_of(t):
    return TAIL if isinstance(t, int) and t == NT - 1 else P


def split_rows(dram, t0, n):
    return dram[t0 * P:(t0 + n) * P, :].rearrange("(t p) c -> p t c", p=P)


class Shared:
    pass


class Moments:

    def __init__(self, sb, name):
        self.raw = sb(name + "_raw", [P, NT, 6], F32)
        self.mean = sb(name + "_mean", [P, NT], F32)
        self.rstd = sb(name + "_rstd", [P, NT], F32)
        self.tmp = sb(name + "_tmp", [P, 3, NT], F32)


def combine_moments(nc, dve, m, t0, n, step, base):
    half = lambda k: m.raw[:, ds(t0, n), k]
    cut = lambda b: b[:, ds(t0, n)]
    s, d, q = (m.tmp[:, k, ds(t0, n)] for k in range(3))
    nc.vector.tensor_tensor(s, half(1), half(4), ALU.add).then_inc(step, 1)
    nc.vector.tensor_tensor(d, half(1), half(4), ALU.subtract).then_inc(step, 1)
    nc.vector.tensor_tensor(q, half(2), half(5), ALU.add).then_inc(step, 1)
    dve.wait_ge(step, base + 3)
    nc.vector.tensor_scalar(cut(m.mean), s, 0.5, None, ALU.mult).then_inc(step, 1)
    nc.vector.scalar_tensor_tensor(out=d, in0=d, scalar=0.25, in1=d, op0=ALU.mult,
                                   op1=ALU.mult).then_inc(step, 1)
    nc.vector.tensor_scalar(q, q, 1.0 / C, EPS, ALU.mult, ALU.add).then_inc(step, 1)
    dve.wait_ge(step, base + 6)
    nc.vector.tensor_tensor(cut(m.rstd), q, d, ALU.add).then_inc(step, 1)


MOMENT_STEPS = 7


def first_layernorm(nc, sem, sb, g):
    parts = [(12 * k, 12) for k in range(4)] + [(NT - 1, 1)]
    zeros = g.zeros
    x_in = [sem(f"x_in{k}") for k in range(len(parts))]
    tail_clear = sem("a_tail_clear")
    stats = sem("a_stats")
    step = sem("a_step")
    var_ready = sem("a_var_ready")
    std_ready = sem("a_std_ready")
    rstd_ready = sem("a_rstd_ready")
    xn_ready = sem("a_xn_ready")
    xn_out = sem("a_xn_out")
    zero_ready = sem("a_zero_ready")
    tables_clear = sem("a_tables_clear")
    filled = sem("a_filled")
    ones_filled = sem("a_ones_filled")
    m = g.mom
    last = len(parts) - 1

    with nc.Block() as block:
        @block.sync
        def _(sp):
            for k, (t0, n) in enumerate(parts[:-1]):
                sp.dma_start(g.x[:, t0:t0 + n, :], split_rows(g.x_dram, t0, n)).then_inc(x_in[k], 16)
            sp.wait_ge(tail_clear, 1)
            sp.dma_start(g.x[0:TAIL, NT - 1, :], g.x_dram[(NT - 1) * P:NODES, :]).then_inc(x_in[last], 16)
            for k, (t0, n) in enumerate(parts):
                sp.wait_ge(xn_ready, t0 + n)
                sp.dma_start(split_rows(g.xn_dram, t0, n), g.xn[:, t0:t0 + n, :]).then_inc(xn_out, 16)
            sp.wait_ge(xn_out, 16 * len(parts))

        @block.gpsimd
        def _(pool):
            nc.gpsimd.memset(zeros[:], 0.0).then_inc(zero_ready, 1)
            nc.gpsimd.memset(g.ident[:], 0.0).then_inc(filled, 1)
            nc.gpsimd.memset(g.earlier[:], 1.0).then_inc(filled, 1)
            pool.wait_ge(filled, 2)
            nc.gpsimd.affine_select(out=g.ident[:], in_=g.ident[:], compare_op=ALU.not_equal, fill=1.0,
                                    base=0, pattern=[[-1, P]], channel_multiplier=1)
            nc.gpsimd.affine_select(out=g.earlier[:], in_=g.earlier[:], compare_op=ALU.is_gt, fill=0.0,
                                    base=0, pattern=[[-1, P]], channel_multiplier=1)
            nc.gpsimd.iota(g.trash_i[:], pattern=[[0, 1]], base=TRASH, channel_multiplier=1)

        @block.scalar
        def _(act):
            act.wait_ge(zero_ready, 1)
            width = zeros.shape[1]
            for table in g.sums_dram:
                flat = table.rearrange("(p r) c -> p (r c)", p=P)
                for k in range(ROWS // P * C // width):
                    act.dma_start(flat[:, k * width:(k + 1) * width], zeros[:]).then_inc(tables_clear, 16)
            for k in range(len(parts)):
                t0, n = parts[k]
                act.wait_ge(var_ready, k + 1)
                nc.scalar.activation(m.rstd[:, t0:t0 + n], m.rstd[:, t0:t0 + n], ACT.Sqrt).then_inc(std_ready, 1)
            act.wait_ge(tables_clear, 16 * TABLES * (ROWS // P * C // width))

        @block.vector
        def _(dve):
            nc.vector.memset(g.x[:, NT - 1, :], 0.0).then_inc(tail_clear, 1)
            nc.vector.memset(g.ones_f[:], 1.0).then_inc(ones_filled, 1)
            dve.wait_ge(ones_filled, 1)
            nc.vector.tensor_copy(g.ones[:], g.ones_f[:])

            def gather_stats(k):
                t0, n = parts[k]
                dve.wait_ge(x_in[k], 16)
                for t in range(t0, t0 + n):
                    nc.vector.bn_stats(m.raw[:, t, :], g.x[:, t, :]).then_inc(stats, 1)
                dve.wait_ge(stats, t0 + n)
                combine_moments(nc, dve, m, t0, n, step, MOMENT_STEPS * k)
                dve.wait_ge(step, MOMENT_STEPS * (k + 1))
                dve.sem_inc(var_ready, 1)

            def normalise(k):
                t0, n = parts[k]
                dve.wait_ge(std_ready, k + 1)
                nc.vector.reciprocal(m.rstd[:, t0:t0 + n], m.rstd[:, t0:t0 + n]).then_inc(rstd_ready, 1)
                dve.wait_ge(rstd_ready, k + 1)
                for t in range(t0, t0 + n):
                    nc.vector.tensor_scalar(g.xn[:, t, :], g.x[:, t, :], m.mean[:, t:t + 1],
                                            m.rstd[:, t:t + 1], ALU.subtract, ALU.mult).then_inc(xn_ready, 1)

            for k in range(len(parts)):
                gather_stats(k)
                if k:
                    normalise(k - 1)
            normalise(last)


def load_weights(nc, sem, g, name, todo, split):
    loaded = sem(name + "_loaded")
    halved = sem(name + "_halved")
    with nc.Block() as block:
        @block.sync
        def _(sp):
            with nc.allow_non_contiguous_dma(reason="bias columns: a few hundred elements"):
                for t, src in todo:
                    sp.dma_start(t[:], src).then_inc(loaded, 16)
            sp.wait_ge(loaded, 16 * len(todo))

        @block.vector
        def _(dve):
            dve.wait_ge(loaded, 16 * len(todo))
            for k, (parts, whole) in enumerate(split):
                nc.vector.tensor_copy(parts[:, 0, :], whole[:]).then_inc(halved, 1)
                dve.wait_ge(halved, k + 1)
                nc.vector.tensor_tensor(parts[:, 1, :], whole[:], parts[:, 0, :].bitcast(F32), ALU.subtract)


def in_blocks(a):
    return a.rearrange("(b p) n -> p b n", p=P)


def as_columns(a):
    return a.rearrange("(b p) -> p b", p=P)


def as_row(a):
    return a.rearrange("(a n) -> a n", a=1)


def mix_weights(nc, sem, sb, g):
    w = g.w
    g.wqkv = sb("wqkv", [P, CB, 3 * C], F32)
    g.wq_t = sb("wq_t", [P, CB, C], F32)
    g.wproj = sb("wproj", [P, CB, C], F32)
    g.wg1 = sb("wg1", [P, CB, GH], F32)
    g.wg2 = sb("wg2", [GH, C], F32)
    g.ln_g = sb("ln_g", [P, CB], F32)
    g.ln_b = sb("ln_b", [P, CB], F32)
    g.bg1 = sb("bg1", [GH, 1], F32)
    g.bg2 = sb("bg2", [P, CB], F32)
    g.bproj = sb("bproj", [P, C], F32)
    load_weights(nc, sem, g, "mix", [
        (g.wqkv, in_blocks(w["mix_Wqkv"])), (g.wq_t, in_blocks(w["mix_WqT"])), (g.wproj, in_blocks(w["mix_Wproj"])),
        (g.wg1, in_blocks(w["mix_Wg1"])), (g.wg2, w["mix_Wg2"]), (g.ln_g, as_columns(w["mix_ln_g"])),
        (g.ln_b, as_columns(w["mix_ln_b"])), (g.bg1, w["mix_bg1"].rearrange("(p a) -> p a", a=1)),
        (g.bg2, as_columns(w["mix_bg2"])), (g.bproj, as_row(w["mix_bproj"]).to_broadcast([P, C]))], [])


def gnn_weights(nc, sem, sb, g):
    w = g.w
    g.wf1 = sb("wf1", [EF, C], F32)
    g.wf2 = sb("wf2", [P, CB, C], F32)
    g.wu1 = sb("wu1", [P, CB, C], F32)
    g.wu2 = sb("wu2", [P, CB, C], F32)
    g.bf1 = sb("bf1", [P, CB], F32)
    g.bu1 = sb("bu1", [P, CB], F32)
    g.bu2 = sb("bu2", [P, CB], F32)
    g.gamma = sb("gamma", [P, CB], F32)
    g.beta = sb("beta", [P, CB], F32)
    g.bf2 = sb("bf2", [1, C], F32)
    g.bf2_parts = sb("bf2_parts", [1, 2, C], F32R)
    load_weights(nc, sem, g, "gnn", [
        (g.wf1, w["gnn_Wf1"]), (g.wf2, in_blocks(w["gnn_Wf2"])), (g.wu1, in_blocks(w["gnn_Wu1"])),
        (g.wu2, in_blocks(w["gnn_Wu2"])), (g.bf1, as_columns(w["gnn_bf1"])), (g.bu1, as_columns(w["gnn_bu1"])),
        (g.bu2, as_columns(w["gnn_bu2"])), (g.gamma, as_columns(w["gnn_gamma"])), (g.beta, as_columns(w["gnn_beta"])),
        (g.bf2, as_row(w["gnn_bf2"]))], [(g.bf2_parts, g.bf2)])


def ffn_weights(nc, sem, sb, g):
    g.b_out = sb("b_out", [1, C], F32)
    g.b_out_parts = sb("b_out_parts", [1, 2, C], F32R)
    load_weights(nc, sem, g, "ffn", [(g.b_out, as_row(g.w["ffn_b_out"]))], [(g.b_out_parts, g.b_out)])


def mix_scores(nc, sem, sb, g):
    turned = sem("b_turned")
    turn_free = sem("b_turn_free")
    k_made = sem("b_k_made")
    k_free = sem("b_k_free")
    stats = sem("b_stats")
    step = sem("b_step")
    var_ready = sem("b_var_ready")
    std_ready = sem("b_std_ready")
    folded = sem("b_folded")
    bias_made = sem("b_bias_made")
    maxed = sem("b_maxed")
    m = g.mom
    turn = [g.ps[b] for b in range(4)]
    kps = [g.ps[b] for b in range(4, 8)]

    with nc.Block() as block:
        @block.tensor
        def _(pe):
            def group(s):
                for t in range(GT):
                    if t % 2 == 0:
                        pe.wait_ge(turn_free, s * 4 + t // 2 + 1)
                    for b in range(CB):
                        mm = nc.tensor.transpose(turn[t // 2][:, ds((t % 2 * CB + b) * P, P)],
                                                 g.xn[:, s * GT + t, ds(b * P, P)], g.ident[:])
                    if t % 2 or t == GT - 1:
                        mm.then_inc(turned, 1)
                for h in range(2):
                    for f in range(CB):
                        j = h * CB + f
                        pe.wait_ge(turn_free, s * 4 + 4 + 4)
                        pe.wait_ge(k_free, s * 4 + j + 1)
                        for b in range(CB):
                            mm = nc.tensor.matmul(kps[j][:, 0:HC], g.wqkv[:, b, ds(C + f * P, P)],
                                                  g.xT[:, b, ds(s * GC + h * HC, HC)],
                                                  start=b == 0, stop=b == CB - 1)
                        mm.then_inc(k_made, 1)

            for s in range(NG):
                group(s)
            pe.wait_ge(folded, 1)
            pe.wait_ge(turn_free, NG * 4 + 4)
            for b in range(CB):
                mm = nc.tensor.matmul(turn[0][0:GH, 0:1], g.wg1[:, b, :], g.ln_b[:, b:b + 1],
                                      start=b == 0, stop=b == CB - 1)
            mm.then_inc(bias_made, 1)

        @block.scalar
        def _(act):
            act.sem_inc(turn_free, 4)
            with act.Fori(0, NG) as s:
                for k in range(4):
                    n = 2 if k < 3 else 1
                    act.wait_ge(turned, s * 4 + k + 1)
                    nc.scalar.activation(
                        g.xT[:, :, ds(s * GC + k * 2 * P, n * P)].rearrange("p f (t n) -> p f t n", n=P),
                        turn[k][:, 0:n * C].rearrange("p (t f n) -> p f t n", f=CB, n=P),
                        ACT.Copy).then_inc(turn_free, 1)
            act.wait_ge(var_ready, 1)
            nc.scalar.activation(m.rstd[:], m.rstd[:], ACT.Sqrt).then_inc(std_ready, 1)

        @block.vector
        def _(dve):
            dve.sem_inc(k_free, 4)
            with dve.Fori(0, NG - 1) as s:
                for j in range(4):
                    dve.wait_ge(k_made, s * 4 + j + 1)
                    nc.vector.tensor_reduce(g.k_max[:, j % CB, ds(2 * s + j // CB, 1)], kps[j][:, 0:HC],
                                            X, ALU.max).then_inc(k_free, 1)
            s = NG - 1
            for j in range(4):
                dve.wait_ge(k_made, s * 4 + j + 1)
                nc.vector.tensor_reduce(g.k_max[:, j % CB, 2 * s + j // CB:2 * s + j // CB + 1],
                                        kps[j][:, 0:tail_cols(s, j // CB)], X, ALU.max).then_inc(k_free, 1)
            dve.wait_ge(k_free, 4 + 4 * NG)
            for f in range(CB):
                nc.vector.tensor_reduce(g.neg_k_max[:, f:f + 1], g.k_max[:, f, :], X, ALU.max,
                                        negate=True).then_inc(maxed, 1)
            with dve.Fori(0, NT) as t:
                nc.vector.bn_stats(m.raw[:, t, :], g.xn[:, t, :]).then_inc(stats, 1)
            dve.wait_ge(stats, NT)
            combine_moments(nc, dve, m, 0, NT, step, 0)
            dve.wait_ge(step, MOMENT_STEPS)
            dve.sem_inc(var_ready, 1)
            dve.wait_ge(std_ready, 1)
            nc.vector.reciprocal(m.rstd[:], m.rstd[:])
            dve.sem_inc(folded, 1)
            dve.wait_ge(bias_made, 1)
            nc.vector.tensor_tensor(g.bg1f[:], turn[0][0:GH, 0:1], g.bg1[:], ALU.add)
            for b in range(CB):
                nc.vector.tensor_scalar(g.wg1f[:, b, :], g.wg1[:, b, :], g.ln_g[:, b:b + 1], None, ALU.mult)
            nc.vector.memset(g.head_mask[:], 0.0).then_inc(folded, 1)
            dve.wait_ge(folded, 2)
            for h in range(P // MD):
                nc.vector.memset(g.head_mask[ds(h * MD, MD), ds(h * MD, MD)], 1.0)


def mix_context(nc, sem, sb, g):
    k_made = sem("c_k_made")
    exp_made = sem("c_exp_made")
    e_turned = sem("c_e_turned")
    e_ready = sem("c_e_ready")
    e_used = sem("c_e_used")
    gram_made = sem("c_gram_made")
    stage = sem("c_stage")
    eT = [sb(f"eT{p}", [P, CB, HC * 2], F32) for p in range(2)]
    e_node = sb("e_node", [P, 2, C], F32)
    gramT = sb("gramT", [P, CB, C], F32)
    ctx_m = sb("ctx_m", [P, CB, P], F32)
    kps = [g.ps[b] for b in range(4)]
    eps = [g.ps[4], g.ps[5]]
    gps = [g.ps[6], g.ps[7]]

    with nc.Block() as block:
        @block.tensor
        def _(pe):
            def scores(s):
                for h in range(2):
                    for f in range(CB):
                        j = h * CB + f
                        pe.wait_ge(exp_made, 4 * s + j + 1)
                        for b in range(CB):
                            mm = nc.tensor.matmul(kps[j][:, 0:HC], g.wqkv[:, b, ds(C + f * P, P)],
                                                  g.xT[:, b, ds(s * GC + h * HC, HC)],
                                                  start=b == 0, stop=b == CB - 1)
                        mm.then_inc(k_made, 1)

            def turn(s, t, par):
                pe.wait_ge(exp_made, 4 + 4 * s + 4)
                pe.wait_ge(e_ready, s * GT + t + 1)
                rows = rows_of(s * GT + t)
                for f in range(CB):
                    mm = nc.tensor.transpose(eps[(s * GT + t) % 2][0:rows, ds(f * P, P)],
                                             eT[par][:, f, ds(t * P, rows)], g.ident[:])
                mm.then_inc(e_turned, 1)

            def gram(s, t, start=False, stop=False):
                pe.wait_ge(e_ready, 2 + s * GT + t + 1)
                rows = rows_of(s * GT + t)
                for b in range(CB):
                    mm = nc.tensor.matmul(gps[b][:, 0:C], g.xn[0:rows, s * GT + t, ds(b * P, P)],
                                          e_node[0:rows, (s * GT + t) % 2, :], start=start, stop=stop)
                mm.then_inc(e_used, 1)

            for s in range(NG):
                if s == 0:
                    scores(0)
                if s + 1 < NG:
                    scores(s + 1)
                for t in range(GT):
                    turn(s, t, s % 2)
                    if s or t:
                        u = s * GT + t - 1
                        gram(u // GT, u % GT, start=u == 0)
            gram(NG - 1, GT - 1, stop=True)
            nc_last = nc.tensor.matmul(kps[0][0:1, 0:1], g.ident[:, 0:1], g.ident[:, 0:1], start=True, stop=True)
            nc_last.then_inc(gram_made, 1)

            pe.wait_ge(stage, 2)
            for f in range(CB):
                for b in range(CB):
                    mm = nc.tensor.matmul(kps[1][:, ds(f * P, P)], gramT[:, b, ds(f * P, P)],
                                          g.wqkv[:, b, ds(2 * C + f * P, P)], start=b == 0, stop=b == CB - 1)
            mm.then_inc(gram_made, 1)
            pe.wait_ge(stage, 6)
            for b in range(CB):
                for f in range(CB):
                    mm = nc.tensor.matmul(kps[2][:, ds(b * C + f * P, P)], g.wq_t[:, f, ds(b * P, P)],
                                          ctx_m[:, f, :], start=True, stop=True)
            mm.then_inc(gram_made, 1)

        @block.scalar
        def _(act):
            act.sem_inc(exp_made, 4)
            for s in range(NG):
                for j in range(4):
                    h, f = j // CB, j % CB
                    n = HC if s < NG - 1 else tail_cols(s, h)
                    act.wait_ge(k_made, 4 * s + j + 1)
                    if s >= 2:
                        act.wait_ge(e_turned, (s - 1) * GT)
                    nc.scalar.activation(eT[s % 2][:, f, ds(h * HC, n)], kps[j][:, 0:n], ACT.Exp,
                                         bias=g.neg_k_max[:, f:f + 1],
                                         accum_out=g.k_sum[:, f, 2 * s + h:2 * s + h + 1]).then_inc(exp_made, 1)

        @block.vector
        def _(dve):
            dve.sem_inc(e_ready, 2)
            for u in range(NT):
                dve.wait_ge(e_turned, u + 1)
                if u >= 2:
                    dve.wait_ge(e_used, u - 1)
                rows = rows_of(u)
                nc.vector.tensor_copy(e_node[0:rows, u % 2, :], eps[u % 2][0:rows, 0:C]).then_inc(e_ready, 1)
            dve.wait_ge(gram_made, 1)
            for b in range(CB):
                nc.vector.tensor_copy(gramT[:, b, :], gps[b][:, 0:C]).then_inc(stage, 1)
            dve.wait_ge(exp_made, 4 + 4 * NG)
            nc.vector.tensor_reduce(g.k_tot[:], g.k_sum[:], X, ALU.add).then_inc(stage, 1)
            dve.wait_ge(stage, 3)
            nc.vector.reciprocal(g.k_inv[:], g.k_tot[:]).then_inc(stage, 1)
            dve.wait_ge(stage, 4)
            dve.wait_ge(gram_made, 2)
            for f in range(CB):
                nc.vector.scalar_tensor_tensor(out=ctx_m[:, f, :], in0=kps[1][:, ds(f * P, P)],
                                               scalar=g.k_inv[:, f:f + 1], in1=g.head_mask[:],
                                               op0=ALU.mult, op1=ALU.mult).then_inc(stage, 1)
            dve.wait_ge(gram_made, 3)
            nc.vector.tensor_copy(g.wqm[:], kps[2][:, 0:CB * C].rearrange("p (b n) -> p b n", b=CB))


def mix_output(nc, sem, sb, g):
    xhat_ready = sem("d_xhat_ready")
    turned = sem("d_turned")
    turn_copied = sem("d_turn_copied")
    hid_made = sem("d_hid_made")
    hid_ready = sem("d_hid_ready")
    gate_made = sem("d_gate_made")
    gate_ready = sem("d_gate_ready")
    att_made = sem("d_att_made")
    prod_ready = sem("d_prod_ready")
    proj_made = sem("d_proj_made")
    res_ready = sem("d_res_ready")
    xhat = sb("xhat", [P, GT, C], F32)
    xhatT = sb("xhatT", [P, CB, GC], F32)
    hid = sb("hid", [GH, GC], F32)
    gate = sb("gate", [P, CB, GC], F32)
    prod = gate
    m = g.mom
    turn = [g.ps[0], g.ps[1]]
    hps = g.ps[2]
    gps = [g.ps[3], g.ps[4]]
    aps = g.ps[5]
    pps = [g.ps[6], g.ps[7]]

    with nc.Block() as block:
        @block.tensor
        def _(pe):
            with pe.Fori(0, NG) as s:
                for k in range(4):
                    pe.wait_ge(xhat_ready, s * GT + min(2 * k + 2, GT))
                    pe.wait_ge(turn_copied, s * 4 + k + 1)
                    for t in range(2 * k, min(2 * k + 2, GT)):
                        for b in range(CB):
                            mm = nc.tensor.transpose(turn[k % 2][:, ds((t % 2 * CB + b) * P, P)],
                                                     xhat[:, t, ds(b * P, P)], g.ident[:])
                    mm.then_inc(turned, 1)
                pe.wait_ge(turn_copied, s * 4 + 2 + 4)
                for h in range(2):
                    pe.wait_ge(hid_ready, s * 2 + h + 1)
                    for b in range(CB):
                        mm = nc.tensor.matmul(hps[0:GH, 0:HC], g.wg1f[:, b, :], xhatT[:, b, ds(h * HC, HC)],
                                              start=b == 0, stop=b == CB - 1)
                    mm.then_inc(hid_made, 1)
                for h in range(2):
                    pe.wait_ge(hid_ready, s * 2 + 1 + h + 1)
                    for f in range(CB):
                        j = h * CB + f
                        pe.wait_ge(gate_ready, s * 4 + j + 1)
                        nc.tensor.matmul(gps[f][:, 0:HC], g.wg2[:, ds(f * P, P)], hid[:, ds(h * HC, HC)],
                                         start=True, stop=True).then_inc(gate_made, 1)
                for j in range(4):
                    h, f = j // CB, j % CB
                    pe.wait_ge(prod_ready, s * 4 + j + 1)
                    for b in range(CB):
                        mm = nc.tensor.matmul(aps[:, 0:HC], g.wqm[:, b, ds(f * P, P)],
                                              g.xT[:, b, ds(s * GC + h * HC, HC)],
                                              start=b == 0, stop=b == CB - 1)
                    mm.then_inc(att_made, 1)
                pe.wait_ge(prod_ready, s * 4 + 1 + 4)
                for k in range(4):
                    pe.wait_ge(res_ready, s * 4 + k + 1)
                    for t in range(2 * k, min(2 * k + 2, GT)):
                        for f in range(CB):
                            mm = nc.tensor.matmul(pps[k % 2][:, ds(t % 2 * C, C)], prod[:, f, ds(t * P, P)],
                                                  g.wproj[:, f, :], start=f == 0, stop=f == CB - 1)
                    mm.then_inc(proj_made, 1)

        @block.scalar
        def _(act):
            act.sem_inc(turn_copied, 2)
            act.sem_inc(hid_ready, 1)
            act.sem_inc(gate_ready, 2)
            with act.Fori(0, NG) as s:
                for k in range(4):
                    n = 2 if k < 3 else 1
                    act.wait_ge(turned, s * 4 + k + 1)
                    if k == 0:
                        act.wait_ge(hid_made, s * 2)
                    nc.scalar.activation(
                        xhatT[:, :, ds(k * 2 * P, n * P)].rearrange("p f (t n) -> p f t n", n=P),
                        turn[k % 2][:, 0:n * C].rearrange("p (t f n) -> p f t n", f=CB, n=P),
                        ACT.Copy).then_inc(turn_copied, 1)
                for h in range(2):
                    act.wait_ge(hid_made, s * 2 + h + 1)
                    act.wait_ge(gate_made, s * 4)
                    nc.scalar.activation(hid[:, ds(h * HC, HC)], hps[0:GH, 0:HC], ACT.Gelu,
                                         bias=g.bg1f[:, 0:1]).then_inc(hid_ready, 1)
                for j in range(4):
                    h, f = j // CB, j % CB
                    act.wait_ge(gate_made, s * 4 + j + 1)
                    act.wait_ge(proj_made, s * 4)
                    nc.scalar.activation(gate[:, f, ds(h * HC, HC)], gps[f][:, 0:HC], ACT.Sigmoid,
                                         bias=g.bg2[:, f:f + 1]).then_inc(gate_ready, 1)

        @block.vector
        def _(dve):
            dve.sem_inc(prod_ready, 1)
            dve.sem_inc(res_ready, 2)
            with dve.Fori(0, NG) as s:
                for t in range(GT):
                    dve.wait_ge(turned, s * 4)
                    nc.vector.tensor_scalar(xhat[:, t, :], g.xn[:, s * GT + t, :],
                                            m.mean[:, ds(s * GT + t, 1)], m.rstd[:, ds(s * GT + t, 1)],
                                            ALU.subtract, ALU.mult).then_inc(xhat_ready, 1)
                for j in range(4):
                    h, f = j // CB, j % CB
                    dve.wait_ge(att_made, s * 4 + j + 1)
                    dve.wait_ge(gate_ready, s * 4 + 2 + j + 1)
                    nc.vector.tensor_tensor(prod[:, f, ds(h * HC, HC)], aps[:, 0:HC],
                                            gate[:, f, ds(h * HC, HC)], ALU.mult).then_inc(prod_ready, 1)
                for k in range(4):
                    n = 2 if k < 3 else 1
                    dve.wait_ge(proj_made, s * 4 + k + 1)
                    here = g.res[:, ds(s * GT + 2 * k, n), :]
                    nc.vector.tensor_tensor(here, pps[k % 2][:, 0:n * C].rearrange("p (t c) -> p t c", c=C),
                                            here, ALU.add).then_inc(res_ready, 1)


def residual_start(nc, sem, g):
    added = sem("res_added")
    with nc.Block() as block:
        @block.vector
        def _(dve):
            with dve.Fori(0, NT) as t:
                nc.vector.tensor_tensor(g.x[:, t, :], g.x[:, t, :], g.xn[:, t, :], ALU.add).then_inc(added, 1)
            dve.wait_ge(added, NT)
            with dve.Fori(0, NT) as t:
                nc.vector.tensor_tensor(g.x[:, t, :], g.x[:, t, :], g.bproj[:], ALU.add)


def edge_messages(nc, sem, sb, g):
    HE = EC // 2
    attr = sb("attr", [EF, 2, EC], F32)
    src_row = sb("src_row", [P, 2, EC], I32)
    src_i = sb("src_i", [P, NCH * ET], I32)
    src_f = sb("src_f", [P, NCH * ET], F32)
    to_trash = sb("to_trash", [P, NCH * ET], F32)
    trash_f = sb("trash_f", [P, 1], F32)
    dst_all = sb("dst_all", [P, NCH * ET], I32)
    dst_idx = [sb(f"dst_idx{p}", [P, ET], I32) for p in range(2)]
    out_idx = [sb(f"out_idx{p}", [P, ET], I32) for p in range(2)]
    hidT = sb("hidT", [P, 2, CB, HE], F32)
    gathered = [sb(f"gathered{p}", [P, ET, C], F32) for p in range(2)]
    msg = sb("msg", [P, 2, 2, C], F32)
    same = sb("same", [P, 2, ET, P], F32)
    rank = sb("rank", [P, ET], F32)
    rank_scr = sb("rank_scr", [P, ET, P], mybir.dt.bfloat16)
    redirect = sb("redirect", [P, ET], F32)
    summed = [sb(f"summed{p}", [P, ET, C], F32) for p in range(2)]
    hps = [g.ps[0], g.ps[1]]
    fps = [g.ps[2], g.ps[3]]
    sps = [g.ps[4], g.ps[5]]

    cols_in = sem("e_cols_in")
    cols_ready = sem("e_cols_ready")
    attr_in = [sem(f"e_attr_in{p}") for p in range(2)]
    row_in = [sem(f"e_row_in{p}") for p in range(2)]
    hid_made = sem("e_hid_made")
    hid_ready = sem("e_hid_ready")
    filt_made = sem("e_filt_made")
    idx_ready = sem("e_idx_ready")
    rows_in = [sem(f"e_rows_in{p}") for p in range(2)]
    msg_ready = sem("e_msg_ready")
    same_ready = sem("e_same_ready")
    redirected = sem("e_redirected")
    out_ready = sem("e_out_ready")
    sum_made = sem("e_sum_made")
    sum_ready = sem("e_sum_ready")
    added = [sem(f"e_added{k}") for k in range(TABLES)]
    passed = sem("e_passed")
    PAIRS = ET // 2
    PER = ET // TABLES

    def both_ways(eng, step):
        step(0, 0, True, False)
        step(0, 1, False, False)
        with eng.Fori(1, NCH // 2 - 1) as i:
            step(i, 0, False, False)
            step(i, 1, False, False)
        step(NCH // 2 - 1, 0, False, False)
        step(NCH // 2 - 1, 1, False, True)

    with nc.Block() as block:
        @block.sync
        def _(sp):
            sp.dma_start(src_i[:], g.src_cols).then_inc(cols_in, 16)
            sp.dma_start(dst_all[:], g.dst_cols).then_inc(cols_in, 16)

            def load(i, p, first, last):
                c = 2 * i + p
                if not (isinstance(i, int) and i == 0):
                    sp.wait_ge(hid_made, 2 * c - 2)
                sp.dma_start(attr[:, p, :], g.attr_T[:, ds(c * EC, EC)]).then_inc(attr_in[p], 16)
                if not (isinstance(i, int) and i == 0):
                    sp.wait_ge(same_ready, PAIRS * (c - 1))
                sp.dma_start(src_row[:, p, :],
                             g.src_rows[ds(c, 1), :].to_broadcast([P, EC])).then_inc(row_in[p], 16)

            both_ways(sp, load)

        @block.gpsimd
        def _(pool):
            def gather(i, p):
                c = 2 * i + p
                pool.wait_ge(idx_ready, c + 1)
                if not (isinstance(i, int) and i == 0):
                    pool.wait_ge(msg_ready, PAIRS * (c - 1))
                pool.sem_inc(passed, 1)
                for t in range(ET):
                    yield nc.gpsimd.indirect_dma_start(
                        gathered[p][:, t, :], None, g.xn_dram,
                        bass.IndirectOffsetOnAxis(ap=dst_idx[p][:, t:t + 1], axis=0)).then_inc(rows_in[p], 16)

            def step(i, p, first, last):
                c = 2 * i + p
                ahead = None
                if not last:
                    ahead = gather(i + p, 1 - p)
                pool.wait_ge(out_ready, c + 1)
                for t in range(ET):
                    if ahead is not None:
                        next(ahead)
                    if t % 2 == 0:
                        pool.wait_ge(sum_ready, PAIRS * c + t // 2 + 1)
                    k = t % TABLES
                    if not (first and p == 0 and t < TABLES):
                        pool.wait_ge(added[k], 16 * (PER * c + t // TABLES))
                    pool.sem_inc(passed, 1)
                    nc.gpsimd.indirect_dma_start(
                        g.sums_dram[k], bass.IndirectOffsetOnAxis(ap=out_idx[p][:, t:t + 1], axis=0),
                        summed[p][:, t, :], None, compute_op=ALU.add).then_inc(added[k], 16)

            for _g in gather(0, 0):
                pass
            both_ways(pool, step)
            for k in range(TABLES):
                pool.wait_ge(added[k], 16 * PER * NCH)

        @block.tensor
        def _(pe):
            def hidden(i, p, h):
                c = 2 * i + p
                if h == 0:
                    pe.wait_ge(attr_in[p], 16 * i + 16)
                for f in range(CB):
                    if not (isinstance(i, int) and c == 0 and h == 0):
                        pe.wait_ge(hid_ready, 2 * (2 * c + h) - 1 + f)
                    mm = nc.tensor.matmul(hps[f][:], g.wf1[:, ds(f * P, P)], attr[:, p, ds(h * HE, HE)], start=True, stop=True)
                mm.then_inc(hid_made, 1)

            def filt(i, p, j):
                c = 2 * i + p
                h = j // 2
                if j % 2 == 0:
                    pe.wait_ge(hid_ready, 4 * c + 2 * h + 2)
                if not (isinstance(i, int) and c == 0 and j < 2):
                    pe.wait_ge(msg_ready, PAIRS * c + j - 1)
                for t in range(2):
                    out = fps[j % 2][:, ds(t * C, C)]
                    nc.tensor.matmul(out, g.ones[:], g.bf2_parts[:, 0, :], start=True, stop=False)
                    nc.tensor.matmul(out, g.ones[:], g.bf2_parts[:, 1, :], start=False, stop=False)
                    for f in range(CB):
                        mm = nc.tensor.matmul(out, hidT[:, h, f, ds((2 * (j % 2) + t) * P, P)], g.wf2[:, f, :],
                                              start=False, stop=f == CB - 1)
                mm.then_inc(filt_made, 1)

            def merge(i, p, j):
                c = 2 * i + p
                pe.wait_ge(msg_ready, PAIRS * c + j + 1)
                pe.wait_ge(same_ready, PAIRS * c + j + 1)
                if not (isinstance(i, int) and c == 0 and j < 2):
                    pe.wait_ge(sum_ready, PAIRS * c + j - 1)
                for t in range(2):
                    mm = nc.tensor.matmul(sps[j % 2][:, ds(t * C, C)], same[:, p, 2 * j + t, :],
                                          msg[:, j % 2, t, :], start=True, stop=True)
                mm.then_inc(sum_made, 1)

            def step(i, p, first, last):
                filt(i, p, 0)
                filt(i, p, 1)
                if not last:
                    hidden(i + p, 1 - p, 0)
                merge(i, p, 0)
                filt(i, p, 2)
                merge(i, p, 1)
                filt(i, p, 3)
                if not last:
                    hidden(i + p, 1 - p, 1)
                merge(i, p, 2)
                merge(i, p, 3)

            hidden(0, 0, 0)
            hidden(0, 0, 1)
            both_ways(pe, step)

        @block.scalar
        def _(act):
            def silu(i, p, h):
                c = 2 * i + p
                act.wait_ge(hid_made, 2 * c + h + 1)
                if not (isinstance(i, int) and c == 0):
                    act.wait_ge(filt_made, PAIRS * (c - 1) + 2 * h + 2)
                for f in range(CB):
                    nc.scalar.activation(hidT[:, h, f, :], hps[f][:], ACT.Silu,
                                         bias=g.bf1[:, f:f + 1]).then_inc(hid_ready, 1)

            def copy_sums(i, p, j):
                c = 2 * i + p
                act.wait_ge(sum_made, PAIRS * c + j + 1)
                if not (isinstance(i, int) and i == 0):
                    for k in range(TABLES):
                        act.wait_ge(added[k], 16 * PER * (c - 1))
                nc.scalar.activation(summed[p][:, ds(2 * j, 2), :],
                                     sps[j % 2][:].rearrange("p (t c) -> p t c", c=C),
                                     ACT.Copy).then_inc(sum_ready, 1)

            def step(i, p, first, last):
                if not last:
                    silu(i + p, 1 - p, 0)
                copy_sums(i, p, 0)
                copy_sums(i, p, 1)
                if not last:
                    silu(i + p, 1 - p, 1)
                copy_sums(i, p, 2)
                copy_sums(i, p, 3)

            silu(0, 0, 0)
            silu(0, 0, 1)
            both_ways(act, step)

        @block.vector
        def _(dve):
            dve.wait_ge(cols_in, 32)
            nc.vector.tensor_copy(src_f[:], src_i[:]).then_inc(cols_ready, 1)
            nc.vector.tensor_copy(trash_f[:], g.trash_i[:]).then_inc(cols_ready, 1)
            dve.wait_ge(cols_ready, 2)
            nc.vector.tensor_scalar(to_trash[:], src_f[:], trash_f[:, 0:1], -1.0, ALU.subtract,
                                    ALU.mult).then_inc(cols_ready, 1)
            dve.wait_ge(cols_ready, 3)

            def dst_columns(i, p):
                c = 2 * i + p
                nc.vector.tensor_copy(dst_idx[p][:], dst_all[:, ds(c * ET, ET)]).then_inc(idx_ready, 1)

            def equal(i, p, j):
                c = 2 * i + p
                if j == 0:
                    dve.wait_ge(row_in[p], 16 * i + 16)
                    if not (isinstance(i, int) and i == 0):
                        dve.wait_ge(sum_made, PAIRS * (c - 1))
                for t in range(2 * j, 2 * j + 2):
                    row = src_row[:, p, ds(t * P, P)]
                    col = src_f[:, ds(c * ET + t, 1)]
                    nc.vector.tensor_scalar(same[:, p, t, :], row, col, None, ALU.is_equal)
                    mm = nc.vector.scalar_tensor_tensor(out=rank_scr[:, t, :], in0=row, scalar=col, in1=g.earlier[:],
                                                        op0=ALU.is_equal, op1=ALU.mult,
                                                        accum_out=rank[:, t:t + 1])
                mm.then_inc(same_ready, 1)

            def out_rows(i, p):
                c = 2 * i + p
                dve.wait_ge(same_ready, PAIRS * c + PAIRS)
                nc.vector.scalar_tensor_tensor(out=redirect[:], in0=rank[:], scalar=0.0,
                                               in1=to_trash[:, ds(c * ET, ET)], op0=ALU.is_gt,
                                               op1=ALU.mult).then_inc(redirected, 1)
                dve.wait_ge(redirected, c + 1)
                if not (isinstance(i, int) and i == 0):
                    for k in range(TABLES):
                        dve.wait_ge(added[k], 16 * PER * (c - 1))
                nc.vector.tensor_tensor(out_idx[p][:], redirect[:], src_f[:, ds(c * ET, ET)],
                                        ALU.add).then_inc(out_ready, 1)

            def message(i, p, j):
                c = 2 * i + p
                if j == 0:
                    dve.wait_ge(rows_in[p], 16 * ET * i + 16 * ET)
                dve.wait_ge(filt_made, PAIRS * c + j + 1)
                if not (isinstance(i, int) and c == 0 and j < 2):
                    dve.wait_ge(sum_made, PAIRS * c + j - 1)
                nc.vector.tensor_tensor(msg[:, j % 2, :, :], fps[j % 2][:].rearrange("p (t c) -> p t c", c=C),
                                        gathered[p][:, ds(2 * j, 2), :], ALU.mult).then_inc(msg_ready, 1)

            def step(i, p, first, last):
                for j in range(PAIRS):
                    message(i, p, j)
                    if j == 0 and not last and not (first and p == 0):
                        dst_columns(i + p, 1 - p)
                    if not last:
                        equal(i + p, 1 - p, j)
                if not last:
                    out_rows(i + p, 1 - p)

            dst_columns(0, 0)
            dst_columns(0, 1)
            for j in range(PAIRS):
                equal(0, 0, j)
            out_rows(0, 0)
            both_ways(dve, step)


def update_nodes(nc, sem, sb, g):
    parts_in = [sem(f"u_parts_in{p}") for p in range(2)]
    agg_ready = sem("u_agg_ready")
    turned = sem("u_turned")
    turn_copied = sem("u_turn_copied")
    hid_made = sem("u_hid_made")
    hid_ready = sem("u_hid_ready")
    h_made = sem("u_h_made")
    h_ready = sem("u_h_ready")
    stats = sem("u_stats")
    chain = sem("u_chain")
    norm_ready = sem("u_norm_ready")
    back_made = sem("u_back_made")
    back_ready = sem("u_back_ready")
    part = [[sb(f"part{p}{k}", [P, GT, C], F32) for k in range(TABLES)] for p in range(2)]
    aggT = sb("aggT", [P, CB, GC], F32)
    hidT = sb("u_hidT", [P, CB, GC], F32)
    hT = sb("hT", [P, CB, NPAD], F32)
    raw = sb("bn_raw", [P, CB, 2 * NG, 6], F32)
    mv = sb("bn_mv", [P, CB, 2], F32)
    sd = sb("bn_sd", [P, CB], F32)
    scale = sb("bn_scale", [P, CB], F32)
    shift = sb("bn_shift", [P, CB], F32)
    turn = [g.ps[0], g.ps[1]]
    ups = [g.ps[2], g.ps[3]]
    hps = [g.ps[4], g.ps[5]]
    bps = [g.ps[6], g.ps[7]]

    with nc.Block() as block:
        @block.sync
        def _(sp):
            for s in range(NG):
                if s >= 2:
                    sp.wait_ge(turned, 4 * (s - 1))
                for k in range(TABLES):
                    sp.dma_start(part[s % 2][k][:], split_rows(g.sums_dram[k], s * GT, GT)).then_inc(parts_in[s % 2], 16)

        @block.tensor
        def _(pe):
            for s in range(NG):
                pe.wait_ge(agg_ready, s + 1)
                for k in range(4):
                    if 4 * s + k >= 2:
                        pe.wait_ge(turn_copied, 4 * s + k - 1)
                    for t in range(2 * k, min(2 * k + 2, GT)):
                        for b in range(CB):
                            mm = nc.tensor.transpose(turn[k % 2][:, ds((t % 2 * CB + b) * P, P)],
                                                     part[s % 2][0][:, t, ds(b * P, P)], g.ident[:])
                    mm.then_inc(turned, 1)
                pe.wait_ge(turn_copied, 4 * s + 4)
                for w, src, bank, made, ready in ((g.wu1, aggT, ups, hid_made, hid_ready),
                                                  (g.wu2, hidT, hps, h_made, h_ready)):
                    if w is g.wu2:
                        pe.wait_ge(hid_ready, 4 * s + 4)
                    for j in range(4):
                        h, f = j // CB, j % CB
                        if 4 * s + j >= 2:
                            pe.wait_ge(ready, 4 * s + j - 1)
                        for b in range(CB):
                            mm = nc.tensor.matmul(bank[f][:, 0:HC], w[:, b, ds(f * P, P)], src[:, b, ds(h * HC, HC)],
                                                  start=b == 0, stop=b == CB - 1)
                        mm.then_inc(made, 1)
            for s in range(NG):
                pe.wait_ge(norm_ready, CB * (s + 1))
                for k in range(4):
                    if 4 * s + k >= 2:
                        pe.wait_ge(back_ready, 4 * s + k - 1)
                    for t in range(2 * k, min(2 * k + 2, GT)):
                        for f in range(CB):
                            mm = nc.tensor.transpose(bps[k % 2][:, ds((t % 2 * CB + f) * P, P)],
                                                     hT[:, f, ds(s * GC + t * P, P)], g.ident[:])
                    mm.then_inc(back_made, 1)

        @block.scalar
        def _(act):
            for s in range(NG):
                for k in range(4):
                    n = 2 if k < 3 else 1
                    act.wait_ge(turned, 4 * s + k + 1)
                    if s:
                        act.wait_ge(hid_made, 4 * s)
                    nc.scalar.activation(
                        aggT[:, :, ds(k * 2 * P, n * P)].rearrange("p f (t n) -> p f t n", n=P),
                        turn[k % 2][:, 0:n * C].rearrange("p (t f n) -> p f t n", f=CB, n=P),
                        ACT.Copy).then_inc(turn_copied, 1)
                for j in range(4):
                    h, f = j // CB, j % CB
                    act.wait_ge(hid_made, 4 * s + j + 1)
                    if s:
                        act.wait_ge(h_made, 4 * s)
                    nc.scalar.activation(hidT[:, f, ds(h * HC, HC)], ups[f][:, 0:HC], ACT.Silu,
                                         bias=g.bu1[:, f:f + 1]).then_inc(hid_ready, 1)
            act.wait_ge(chain, 3)
            nc.scalar.activation(sd[:], sd[:], ACT.Sqrt).then_inc(chain, 1)
            act.wait_ge(chain, 8)
            for s in range(NG):
                for f in range(CB):
                    cols = hT[:, f, ds(s * GC, GC)]
                    nc.scalar.activation(cols, cols, ACT.Identity, bias=shift[:, f:f + 1],
                                         scale=scale[:, f:f + 1]).then_inc(norm_ready, 1)

        @block.vector
        def _(dve):
            def gather_sums(s):
                dve.wait_ge(parts_in[s % 2], 32 * (s // 2 + 1))
                a, b = part[s % 2]
                nc.vector.tensor_tensor(a[:], a[:], b[:], ALU.add).then_inc(agg_ready, 1)

            gather_sums(0)
            for s in range(NG):
                if s + 1 < NG:
                    gather_sums(s + 1)
                for j in range(4):
                    h, f = j // CB, j % CB
                    dve.wait_ge(h_made, 4 * s + j + 1)
                    nc.vector.tensor_scalar(hT[:, f, ds(s * GC + h * HC, HC)], hps[f][:, 0:HC],
                                            g.bu2[:, f:f + 1], None, ALU.add).then_inc(h_ready, 1)
                    dve.wait_ge(h_ready, 4 * s + j + 1)
                    n = HC if s < NG - 1 else tail_cols(s, h)
                    nc.vector.bn_stats(raw[:, f, 2 * s + h, :],
                                       hT[:, f, ds(s * GC + h * HC, n)]).then_inc(stats, 1)
            dve.wait_ge(stats, 4 * NG)
            for f in range(CB):
                nc.vector.bn_aggr(mv[:, f, :], raw[:, f, :, :]).then_inc(chain, 1)
            dve.wait_ge(chain, 2)
            nc.vector.tensor_scalar(sd[:], mv[:, :, 1], EPS, None, ALU.add).then_inc(chain, 1)
            dve.wait_ge(chain, 4)
            nc.vector.reciprocal(sd[:], sd[:]).then_inc(chain, 1)
            dve.wait_ge(chain, 5)
            nc.vector.tensor_tensor(scale[:], g.gamma[:], sd[:], ALU.mult).then_inc(chain, 1)
            dve.wait_ge(chain, 6)
            nc.vector.tensor_tensor(shift[:], mv[:, :, 0], scale[:], ALU.mult).then_inc(chain, 1)
            dve.wait_ge(chain, 7)
            nc.vector.tensor_tensor(shift[:], g.beta[:], shift[:], ALU.subtract).then_inc(chain, 1)
            for s in range(NG):
                for k in range(4):
                    n = 2 if k < 3 else 1
                    dve.wait_ge(back_made, 4 * s + k + 1)
                    here = g.res[:, ds(s * GT + 2 * k, n), :]
                    nc.vector.tensor_tensor(here, bps[k % 2][:, 0:n * C].rearrange("p (t c) -> p t c", c=C),
                                            here, ALU.add).then_inc(back_ready, 1)


def slice_weights(nc, sem, sb, g):
    w = g.w
    wx_t = sb("wx_t", [FD, FH, C], F32)
    w_slice = sb("w_slice", [FD, FG], F32)
    b_x = sb("b_x", [FD, FH], F32)
    b_slice = sb("b_slice", [1, FG], F32)
    temp = sb("temp", [P, FH], F32)
    inv_temp = sb("inv_temp", [P, FH], F32)
    bias = sb("slice_bias", [1, HG], F32)
    loaded = sem("f_loaded")
    chain = sem("f_chain")
    made = sem("f_made")
    stats = sem("f_stats")
    step = sem("f_step")
    m = g.mom

    with nc.Block() as block:
        @block.sync
        def _(sp):
            sp.dma_start(wx_t[:], w["ffn_W_xT"]).then_inc(loaded, 16)
            sp.dma_start(w_slice[:], w["ffn_W_slice"]).then_inc(loaded, 16)
            with nc.allow_non_contiguous_dma(reason="512 elements of bias"):
                sp.dma_start(b_x[:], w["ffn_b_x"].rearrange("(h d) -> d h", h=FH)).then_inc(loaded, 16)
            sp.dma_start(b_slice[:], w["ffn_b_slice"].rearrange("(a n) -> a n", a=1)).then_inc(loaded, 16)
            sp.dma_start(temp[:], w["ffn_temperature"].rearrange("a h b c -> (a b c) h").to_broadcast([P, FH]))\
              .then_inc(loaded, 16)

        @block.tensor
        def _(pe):
            pe.wait_ge(loaded, 80)
            for b in range(CB):
                for h in range(FH):
                    nc.tensor.matmul(g.ps[b][:, ds(h * FG, FG)], wx_t[:, h, ds(b * P, P)], w_slice[:],
                                     start=True, stop=True)
            for h in range(FH):
                mm = nc.tensor.matmul(g.ps[2][0:1, ds(h * FG, FG)], b_x[:, h:h + 1], w_slice[:], start=True, stop=True)
            mm.then_inc(made, 1)

        @block.scalar
        def _(act):
            act.wait_ge(step, MOMENT_STEPS)
            nc.scalar.activation(m.rstd[:], m.rstd[:], ACT.Sqrt).then_inc(step, 1)

        @block.vector
        def _(dve):
            heads = lambda ap: ap.rearrange("p (h n) -> p h n", h=FH)
            wide = lambda ap, n: ap.unsqueeze(2).to_broadcast([n, FH, FG])
            dve.wait_ge(loaded, 80)
            nc.vector.tensor_scalar(temp[:], temp[:], 0.1, 5.0, ALU.max, ALU.min).then_inc(chain, 1)
            dve.wait_ge(chain, 1)
            nc.vector.reciprocal(inv_temp[:], temp[:]).then_inc(chain, 1)
            dve.wait_ge(chain, 2)
            dve.wait_ge(made, 1)
            for b in range(CB):
                nc.vector.tensor_tensor(heads(g.w_logit[:, b, :]), heads(g.ps[b][:]), wide(inv_temp[:], P), ALU.mult)
            nc.vector.tensor_tensor(heads(bias[:]), heads(g.ps[2][0:1, :]),
                                    b_slice[:].unsqueeze(1).to_broadcast([1, FH, FG]), ALU.add).then_inc(chain, 1)
            dve.wait_ge(chain, 3)
            nc.vector.tensor_tensor(heads(bias[:]), heads(bias[:]), wide(inv_temp[0:1, :], 1), ALU.mult).then_inc(chain, 1)
            dve.wait_ge(chain, 4)
            nc.vector.tensor_copy(g.bias_parts[:, 0, :], bias[:]).then_inc(chain, 1)
            dve.wait_ge(chain, 5)
            nc.vector.tensor_tensor(g.bias_parts[:, 1, :], bias[:], g.bias_parts[:, 0, :].bitcast(F32), ALU.subtract)
            with dve.Fori(0, NT) as t:
                nc.vector.bn_stats(m.raw[:, t, :], g.res[:, t, :]).then_inc(stats, 1)
            dve.wait_ge(stats, NT)
            combine_moments(nc, dve, m, 0, NT, step, 0)
            dve.wait_ge(step, MOMENT_STEPS + 1)
            nc.vector.reciprocal(m.rstd[:], m.rstd[:])


def slice_tokens(nc, sem, sb, g):
    x2_ready = sem("h_x2_ready")
    turned = sem("h_turned")
    x2T_ready = sem("h_x2T_ready")
    logit_made = sem("h_logit_made")
    max_ready = sem("h_max_ready")
    shifted = sem("h_shifted")
    exp_ready = sem("h_exp_ready")
    sum_ready = sem("h_sum_ready")
    inv_ready = sem("h_inv_ready")
    w_ready = sem("h_w_ready")
    w_turned = sem("h_w_turned")
    wT_ready = sem("h_wT_ready")
    tok_made = sem("h_tok_made")
    ones_ready = sem("h_ones_ready")
    x2 = [sb(f"x2_{p}", [P, XW], F32) for p in range(2)]
    x2T = [sb(f"x2T_{p}", [P, CB, P], F32) for p in range(2)]
    ex = [sb(f"ex_{p}", [P, HG], F32) for p in range(2)]
    neg_max = [sb(f"neg_max{p}", [P, FH], F32) for p in range(2)]
    tot = [sb(f"tot{p}", [P, FH], F32) for p in range(2)]
    m = g.mom
    tps = g.ps[0]
    lps = g.ps[1]
    wps = [g.ps[2], g.ps[3]]
    acc = g.ps[4:8]
    heads = lambda ap: ap.rearrange("p (h n) -> p h n", h=FH)
    wide = lambda ap: ap.unsqueeze(2).to_broadcast([P, FH, FG])

    def over_tiles(eng, step):
        step(0, 0)
        step(1, 1)
        with eng.Fori(1, NT // 2) as i:
            step(2 * i, 0)
            step(2 * i + 1, 1)
        step(NT - 1, 0)

    with nc.Block() as block:
        @block.tensor
        def _(pe):
            def turn_x(t, p):
                pe.wait_ge(x2_ready, t + 1)
                pe.wait_ge(x2T_ready, t + 1)
                for b in range(CB):
                    mm = nc.tensor.transpose(tps[:, ds(b * P, P)], x2[p][:, ds(b * P, P)], g.ident[:])
                mm.then_inc(turned, 1)

            def logits(t, p):
                pe.wait_ge(x2T_ready, t + 2)
                pe.wait_ge(shifted, t + 1)
                nc.tensor.matmul(lps[:], g.ones[:], g.bias_parts[:, 0, :], start=True, stop=False)
                nc.tensor.matmul(lps[:], g.ones[:], g.bias_parts[:, 1, :], start=False, stop=False)
                for b in range(CB):
                    mm = nc.tensor.matmul(lps[:], x2T[p][:, b, :], g.w_logit[:, b, :], start=False, stop=b == CB - 1)
                mm.then_inc(logit_made, 1)

            def use(t, p):
                pe.wait_ge(w_ready, t + 1)
                pe.wait_ge(wT_ready, t + 1)
                for q in range(HGB):
                    mm = nc.tensor.transpose(wps[p][:, ds(q * P, P)], ex[p][:, ds(q * P, P)], g.ident[:])
                mm.then_inc(w_turned, 1)
                rows = rows_of(t)
                for q in range(HGB):
                    mm = nc.tensor.matmul(acc[q][:, 0:XW], ex[p][0:rows, ds(q * P, P)], x2[p][0:rows, :],
                                          start=isinstance(t, int) and t == 0, stop=isinstance(t, int) and t == NT - 1)
                mm.then_inc(tok_made, 1)

            def step(t, p):
                turn_x(t, p)
                logits(t, p)
                if not (isinstance(t, int) and t == 0):
                    use(t - 1, 1 - p)

            over_tiles(pe, step)
            use(NT - 1, 0)

        @block.scalar
        def _(act):
            act.sem_inc(x2T_ready, 1)
            act.sem_inc(wT_ready, 2)

            def copy_x(t, p):
                act.wait_ge(turned, t + 1)
                if not (isinstance(t, int) and t < 2):
                    act.wait_ge(logit_made, t - 1)
                nc.scalar.activation(x2T[p][:], tps[:, 0:C].rearrange("p (b n) -> p b n", b=CB),
                                     ACT.Copy).then_inc(x2T_ready, 1)

            def expo(t, p):
                act.wait_ge(shifted, t + 2)
                nc.scalar.activation(ex[p][:], ex[p][:], ACT.Exp).then_inc(exp_ready, 1)

            def copy_w(t, p):
                act.wait_ge(w_turned, t + 1)
                nc.scalar.activation(g.wT[:, :, ds(t * P, P)], wps[p][:].rearrange("p (q n) -> p q n", q=HGB),
                                     ACT.Copy).then_inc(wT_ready, 1)

            def step(t, p):
                copy_x(t, p)
                if not (isinstance(t, int) and t == 0):
                    copy_w(t - 1, 1 - p)
                expo(t, p)

            over_tiles(act, step)
            copy_w(NT - 1, 0)

        @block.vector
        def _(dve):
            for p in range(2):
                nc.vector.memset(x2[p][:, C:C + 1], 1.0)
                nc.vector.memset(x2[p][:, C + 1:XW], 0.0)
            dve.sem_inc(shifted, 1)

            def normalise(t, p):
                if not (isinstance(t, int) and t < 2):
                    dve.wait_ge(tok_made, t - 1)
                nc.vector.tensor_scalar(x2[p][:, 0:C], g.res[:, t, :], m.mean[:, ds(t, 1)], m.rstd[:, ds(t, 1)],
                                        ALU.subtract, ALU.mult).then_inc(x2_ready, 1)

            def softmax(t, p):
                dve.wait_ge(logit_made, t + 1)
                nc.vector.tensor_reduce(neg_max[p][:], heads(lps[:]), X, ALU.max, negate=True).then_inc(max_ready, 1)
                dve.wait_ge(max_ready, t + 1)
                nc.vector.tensor_tensor(heads(ex[p][:]), heads(lps[:]), wide(neg_max[p][:]), ALU.add).then_inc(shifted, 1)
                dve.wait_ge(exp_ready, t + 1)
                nc.vector.tensor_reduce(tot[p][:], heads(ex[p][:]), X, ALU.add).then_inc(sum_ready, 1)
                dve.wait_ge(sum_ready, t + 1)
                nc.vector.reciprocal(tot[p][:], tot[p][:]).then_inc(inv_ready, 1)
                dve.wait_ge(inv_ready, t + 1)
                nc.vector.tensor_tensor(heads(ex[p][:]), heads(ex[p][:]), wide(tot[p][:]), ALU.mult).then_inc(w_ready, 1)

            def step(t, p):
                if not (isinstance(t, int) and t == NT - 1):
                    normalise(t + 1, 1 - p)
                softmax(t, p)

            normalise(0, 0)
            over_tiles(dve, step)


def slice_attention(nc, sem, sb, g):
    w = g.w
    w_fx = sb("w_fx", [P, CB, FH * FD], F32)
    b_fx = sb("b_fx", [1, FH * FD], F32)
    w_q = sb("w_q", [FD, FD], F32)
    w_k = sb("w_k", [FD, FD], F32)
    w_v = sb("w_v", [FD, FD], F32)
    w_out = sb("w_out", [FD, FH, C], F32)
    norm = sb("norm", [P, HGB, 2], F32)
    tok = sb("tok", [P, HGB, XW], F32)
    tokT = sb("tokT", [P, CB, HG], F32)
    share = sb("share", [1, HG], F32)
    fxT = sb("fxT", [FD, HG], F32)
    qT = sb("qT", [FD, HG], F32)
    kT = sb("kT", [FD, HG], F32)
    v = sb("v", [FG, FH * FD], F32)
    at = sb("at", [FG, HG], F32)
    atT = sb("atT", [FG, HG], F32)
    neg = sb("neg", [FG, FH], F32)
    tot = sb("a_tot", [FG, FH], F32)
    oT = sb("oT", [FD, HG], F32)
    loaded = sem("i_loaded")
    vec = sem("i_vec")
    mat = sem("i_mat")
    expo = sem("i_exp")
    acc = g.ps[4:8]
    heads = lambda ap: ap.rearrange("p (h n) -> p h n", h=FH)
    wide = lambda ap: ap.unsqueeze(2).to_broadcast([FG, FH, FG])

    with nc.Block() as block:
        @block.sync
        def _(sp):
            for t, src in ((w_fx, w["ffn_W_fx"].rearrange("(b p) n -> p b n", p=P)),
                           (b_fx, w["ffn_b_fx"].rearrange("(a n) -> a n", a=1)),
                           (w_q, w["ffn_W_q"]), (w_k, w["ffn_W_k"]), (w_v, w["ffn_W_v"]),
                           (w_out, w["ffn_W_out"].rearrange("(h d) n -> d h n", h=FH))):
                sp.dma_start(t[:], src).then_inc(loaded, 16)

        @block.vector
        def _(dve):
            V = nc.vector
            for q in range(HGB):
                V.tensor_scalar(norm[:, q, 0:1], acc[q][:, C:C + 1], EPS, None, ALU.add).then_inc(vec, 1)
            dve.wait_ge(vec, 4)
            V.reciprocal(norm[:, :, 1], norm[:, :, 0]).then_inc(vec, 1)
            dve.wait_ge(vec, 5)
            for q in range(HGB):
                V.tensor_scalar(tok[:, q, :], acc[q][:, 0:XW], norm[:, q, 1:2], None, ALU.mult).then_inc(vec, 1)
            dve.wait_ge(mat, 1)
            for b in range(CB):
                V.tensor_copy(tokT[:, b, :], g.ps[b][:]).then_inc(vec, 1)
            V.tensor_copy(share[:], g.ps[2][0:1, :]).then_inc(vec, 1)
            dve.wait_ge(mat, 2)
            V.tensor_copy(fxT[:], g.ps[3][0:FD, :]).then_inc(vec, 1)
            dve.wait_ge(mat, 3)
            V.tensor_copy(qT[:], g.ps[4][0:FD, :]).then_inc(vec, 1)
            V.tensor_copy(kT[:], g.ps[5][0:FD, :]).then_inc(vec, 1)
            V.tensor_copy(v[:], g.ps[6][0:FG, :]).then_inc(vec, 1)
            dve.wait_ge(mat, 4)
            V.tensor_reduce(neg[:], heads(g.ps[7][0:FG, :]), X, ALU.max, negate=True).then_inc(vec, 1)
            dve.wait_ge(vec, 17)
            V.tensor_tensor(heads(at[:]), heads(g.ps[7][0:FG, :]), wide(neg[:]), ALU.add).then_inc(vec, 1)
            dve.wait_ge(expo, 1)
            V.tensor_reduce(tot[:], heads(at[:]), X, ALU.add).then_inc(vec, 1)
            dve.wait_ge(vec, 19)
            V.reciprocal(tot[:], tot[:]).then_inc(vec, 1)
            dve.wait_ge(vec, 20)
            V.tensor_tensor(heads(at[:]), heads(at[:]), wide(tot[:]), ALU.mult).then_inc(vec, 1)
            dve.wait_ge(mat, 5)
            V.tensor_copy(atT[:], g.ps[0][0:FG, :]).then_inc(vec, 1)
            dve.wait_ge(mat, 6)
            V.tensor_copy(oT[:], g.ps[1][0:FD, :]).then_inc(vec, 1)
            dve.wait_ge(mat, 7)
            for q in range(HGB):
                V.tensor_copy(g.m_out[:, q, :], g.ps[2 + q][:, 0:C])

        @block.scalar
        def _(act):
            act.wait_ge(vec, 18)
            nc.scalar.activation(at[:], at[:], ACT.Exp, scale=float(FD) ** -0.5).then_inc(expo, 1)

        @block.tensor
        def _(pe):
            T = nc.tensor
            for q in range(HGB):
                pe.wait_ge(vec, 5 + q + 1)
                for b in range(CB):
                    T.transpose(g.ps[b][:, ds(q * P, P)], tok[:, q, ds(b * P, P)], g.ident[:])
                mm = T.transpose(g.ps[2][0:1, ds(q * P, P)], tok[:, q, C:C + 1], g.ident[:])
            mm.then_inc(mat, 1)
            pe.wait_ge(loaded, 96)
            pe.wait_ge(vec, 12)
            for h in range(FH):
                out = g.ps[3][0:FD, ds(h * FG, FG)]
                for b in range(CB):
                    T.matmul(out, w_fx[:, b, ds(h * FD, FD)], tokT[:, b, ds(h * FG, FG)], start=b == 0, stop=False)
                mm = T.matmul(out, b_fx[:, ds(h * FD, FD)], share[:, ds(h * FG, FG)], start=False, stop=True)
            mm.then_inc(mat, 1)
            pe.wait_ge(vec, 13)
            T.matmul(g.ps[4][0:FD, :], w_q[:], fxT[:], start=True, stop=True)
            T.matmul(g.ps[5][0:FD, :], w_k[:], fxT[:], start=True, stop=True)
            for h in range(FH):
                mm = T.matmul(g.ps[6][0:FG, ds(h * FD, FD)], fxT[:, ds(h * FG, FG)], w_v[:], start=True, stop=True)
            mm.then_inc(mat, 1)
            pe.wait_ge(vec, 16)
            for h in range(FH):
                mm = T.matmul(g.ps[7][0:FG, ds(h * FG, FG)], qT[:, ds(h * FG, FG)], kT[:, ds(h * FG, FG)],
                              start=True, stop=True)
            mm.then_inc(mat, 1)
            pe.wait_ge(vec, 21)
            for h in range(FH):
                mm = T.transpose(g.ps[0][0:FG, ds(h * FG, FG)], at[:, ds(h * FG, FG)], g.ident[0:FG, 0:FG])
            mm.then_inc(mat, 1)
            pe.wait_ge(vec, 22)
            for h in range(FH):
                mm = T.matmul(g.ps[1][0:FD, ds(h * FG, FG)], v[:, ds(h * FD, FD)], atT[:, ds(h * FG, FG)],
                              start=True, stop=True)
            mm.then_inc(mat, 1)
            pe.wait_ge(vec, 23)
            for h in range(FH):
                mm = T.matmul(g.ps[2 + h // 2][ds(h % 2 * FG, FG), 0:C], oT[:, ds(h * FG, FG)], w_out[:, h, :],
                              start=True, stop=True)
            mm.then_inc(mat, 1)


def slice_output(nc, sem, sb, g):
    made = sem("j_made")
    ready = sem("j_ready")
    stored = [sem(f"j_stored{p}") for p in range(2)]
    y = [sb(f"y{p}", [P, GT, C], F32) for p in range(2)]
    yps = g.ps[0:4]

    with nc.Block() as block:
        @block.tensor
        def _(pe):
            for u in range(NT):
                if u % 2 == 0 and u >= 8:
                    pe.wait_ge(ready, u // 2 - 3)
                out = yps[u // 2 % 4][:, ds(u % 2 * C, C)]
                nc.tensor.matmul(out, g.ones[:], g.b_out_parts[:, 0, :], start=True, stop=False)
                nc.tensor.matmul(out, g.ones[:], g.b_out_parts[:, 1, :], start=False, stop=False)
                for q in range(HGB):
                    mm = nc.tensor.matmul(out, g.wT[:, q, ds(u * P, P)], g.m_out[:, q, :], start=False, stop=q == HGB - 1)
                if u % 2 or u == NT - 1:
                    mm.then_inc(made, 1)

        @block.vector
        def _(dve):
            for k in range(-(-NT // 2)):
                n = min(2, NT - 2 * k)
                dve.wait_ge(made, k + 1)
                here = g.res[:, ds(2 * k, n), :]
                nc.vector.tensor_tensor(here, yps[k % 4][:, 0:n * C].rearrange("p (t c) -> p t c", c=C), here,
                                        ALU.add).then_inc(ready, 1)

        @block.sync
        def _(sp):
            done = 0
            whole = NT - 1
            for t0 in range(0, whole, 8):
                sp.wait_ge(ready, t0 // 2 + 4)
                sp.dma_start(split_rows(g.out_dram, t0, 8), g.res[:, t0:t0 + 8, :]).then_inc(stored[0], 16)
                done += 16
            sp.wait_ge(ready, -(-NT // 2))
            sp.dma_start(g.out_dram[whole * P:NODES, :], g.res[0:TAIL, whole, :]).then_inc(stored[1], 16)
            sp.wait_ge(stored[0], done)
            sp.wait_ge(stored[1], 16)


def gps_layer(nc, w, x, attr_T, src_rows, src_cols, dst_cols, out):
    with ExitStack() as ctx:
        def sem(name):
            return ctx.enter_context(nc.semaphore(name))

        def sb(name, shape, dt):
            return ctx.enter_context(nc.sbuf_tensor(name, shape, dt))

        def scoped(stage, *args):
            with ExitStack() as inner:
                stage(nc, sem, lambda *a: inner.enter_context(nc.sbuf_tensor(*a)), *args)

        g = Shared()
        g.w, g.x_dram, g.attr_T, g.out_dram = w, x, attr_T, out
        g.src_rows, g.src_cols, g.dst_cols = src_rows, src_cols, dst_cols
        g.xn_dram = nc.dram_tensor("xn_rows", [NPAD, C], F32).ap()
        g.sums_dram = [nc.dram_tensor(f"sums{k}", [ROWS, C], F32).ap() for k in range(TABLES)]
        g.ps = [ctx.enter_context(nc.psum_tensor(f"bank{b}", [P, 512], F32)) for b in range(8)]
        g.ident = sb("ident", [P, P], F32)
        g.earlier = sb("earlier", [P, P], F32)
        g.trash_i = sb("trash_i", [P, 1], I32)
        g.x = sb("x_res", [P, NT, C], F32)
        g.res = g.x
        g.mom = Moments(sb, "mom")
        g.ones_f = sb("ones_f", [1, P], F32)
        g.ones = sb("ones", [1, P], F32R)
        with ExitStack() as mixing:
            sb_mix = lambda *a: mixing.enter_context(nc.sbuf_tensor(*a))
            mix_weights(nc, sem, sb_mix, g)
            g.xT = sb_mix("xT", [P, CB, NPAD], F32)
            g.xn = sb_mix("xn", [P, NT, C], F32)
            g.k_max = sb_mix("k_max", [P, CB, 2 * NG], F32)
            g.neg_k_max = sb_mix("neg_k_max", [P, CB], F32)
            g.k_sum = sb_mix("k_sum", [P, CB, 2 * NG], F32)
            g.k_tot = sb_mix("k_tot", [P, CB], F32)
            g.k_inv = sb_mix("k_inv", [P, CB], F32)
            g.bg1f = sb_mix("bg1f", [GH, 1], F32)
            g.wg1f = sb_mix("wg1f", [P, CB, GH], F32)
            g.head_mask = sb_mix("head_mask", [P, P], F32)
            g.wqm = sb_mix("wqm", [P, CB, C], F32)
            with nc.sbuf_tensor("zeros", [P, 3200], F32) as g.zeros:
                first_layernorm(nc, sem, sb, g)
            residual_start(nc, sem, g)
            scoped(mix_scores, g)
            scoped(mix_context, g)
            scoped(mix_output, g)
        with ExitStack() as passing:
            gnn_weights(nc, sem, lambda *a: passing.enter_context(nc.sbuf_tensor(*a)), g)
            scoped(edge_messages, g)
            scoped(update_nodes, g)
        with ExitStack() as late:
            sb_late = lambda *a: late.enter_context(nc.sbuf_tensor(*a))
            g.w_logit = sb_late("w_logit", [P, CB, HG], F32)
            g.bias_parts = sb_late("bias_parts", [1, 2, HG], F32R)
            g.m_out = sb_late("m_out", [P, HGB, C], F32)
            g.wT = sb_late("wT", [P, HGB, NPAD], F32)
            ffn_weights(nc, sem, sb_late, g)
            scoped(slice_weights, g)
            scoped(slice_tokens, g)
            scoped(slice_attention, g)
            scoped(slice_output, g)


def kernel(**inputs):
    import numpy as np
    from concourse import bacc
    from concourse.bass_utils import run_bass_kernel_spmd

    a = {k: np.asarray(v) for k, v in inputs.items()}
    attr_T = np.zeros((EF, EPAD), np.float32)
    attr_T[:, :EDGES] = a["edge_attr_20"].T
    src = np.full((EPAD,), PAD_SRC, np.int32)
    src[:EDGES] = a["src"]
    dst = np.zeros((EPAD,), np.int32)
    dst[:EDGES] = a["dst"]
    arrays = {
        "x": a["x"], "attr_T": attr_T, "src_rows": src.reshape(NCH, EC),
        "src_cols": np.ascontiguousarray(src.reshape(-1, P).T),
        "dst_cols": np.ascontiguousarray(dst.reshape(-1, P).T),
    }
    weights = {k[3:]: v for k, v in a.items() if k.startswith("L0_")}
    weights["mix_WqT"] = np.ascontiguousarray(weights["mix_Wqkv"][:, :C].T)
    weights["ffn_W_xT"] = np.ascontiguousarray(weights.pop("ffn_W_x").reshape(C, FH, FD).transpose(2, 1, 0))

    nc = bacc.Bacc("TRN2", target_bir_lowering=False, num_devices=1)
    declare = lambda name, v: nc.dram_tensor(name, v.shape, mybir.dt.from_np(v.dtype), kind="ExternalInput").ap()
    io = {k: declare(k, v) for k, v in arrays.items()}
    w = {k: declare("w_" + k, v) for k, v in weights.items()}
    arrays.update({"w_" + k: v for k, v in weights.items()})
    out = nc.dram_tensor("out", (NODES, C), F32, kind="ExternalOutput").ap()
    gps_layer(nc, w, out=out, **io)
    r = run_bass_kernel_spmd(nc, [arrays], core_ids=[0])
    return r.results[0]["out"]
```

```python
from contextlib import ExitStack

import concourse.bass as bass
from concourse import mybir
from concourse.alu_op_type import AluOpType as ALU

F32 = mybir.dt.float32
F32R = mybir.dt.float32r
I32 = mybir.dt.int32
ACT = mybir.ActivationFunctionType
X = mybir.AxisListType.X
ds = bass.ds

P = 128
NODES, C = 6250, 256
CB = C // P
NT = -(-NODES // P)
TAIL = NODES - (NT - 1) * P
NPAD = NT * P
GT = 7
NG = NT // GT
GC = GT * P
HC = GC // 2
EDGES, EF = 100000, 20
ET = 8
EC = ET * P
NCH = 2 * -(-EDGES // (2 * EC))
EPAD = NCH * EC
TRASH = NODES
PAD_SRC = NODES + P
ROWS = -(-(PAD_SRC + 1) // P) * P
TABLES = 2
MH, MD = 8, 32
GH = C // 4
FH, FD, FG = 8, 64, 64
HG = FH * FG
HGB = HG // P
EPS = 1e-5
BIAS_ROWS = 33
XW = C + 2


def tail_cols(s, h):
    return max(0, min(HC, NODES - (NG - 1) * GC - h * HC))


def rows_of(t):
    return TAIL if isinstance(t, int) and t == NT - 1 else P


def split_rows(dram, t0, n):
    return dram[ds(t0 * P, n * P), :].rearrange("(t p) c -> p t c", p=P)


class Shared:
    pass


class Moments:

    def __init__(self, sb, name):
        self.raw = sb(name + "_raw", [P, NT, 6], F32)
        self.mean = sb(name + "_mean", [P, NT], F32)
        self.rstd = sb(name + "_rstd", [P, NT], F32)
        self.tmp = sb(name + "_tmp", [P, 3, NT], F32)


def combine_moments(nc, dve, m, t0, n, step, base):
    half = lambda k: m.raw[:, ds(t0, n), k]
    cut = lambda b: b[:, ds(t0, n)]
    s, d, q = (m.tmp[:, k, ds(t0, n)] for k in range(3))
    nc.vector.tensor_tensor(s, half(1), half(4), ALU.add).then_inc(step, 1)
    nc.vector.tensor_tensor(d, half(1), half(4), ALU.subtract).then_inc(step, 1)
    nc.vector.tensor_tensor(q, half(2), half(5), ALU.add).then_inc(step, 1)
    dve.wait_ge(step, base + 3)
    nc.vector.tensor_scalar(cut(m.mean), s, 0.5, None, ALU.mult).then_inc(step, 1)
    nc.vector.scalar_tensor_tensor(out=d, in0=d, scalar=0.25, in1=d, op0=ALU.mult,
                                   op1=ALU.mult).then_inc(step, 1)
    nc.vector.tensor_scalar(q, q, 1.0 / C, EPS, ALU.mult, ALU.add).then_inc(step, 1)
    dve.wait_ge(step, base + 6)
    nc.vector.tensor_tensor(cut(m.rstd), q, d, ALU.add).then_inc(step, 1)


MOMENT_STEPS = 7


def first_layernorm(nc, sem, sb, g):
    parts = [(12 * k, 12) for k in range(4)] + [(NT - 1, 1)]
    x = sb("x_rows_a", [P, NT, C], F32)
    xn = sb("xn_a", [P, NT, C], F32)
    ones_f = sb("ones_f", [BIAS_ROWS, P], F32)
    x_in = [sem(f"x_in{k}") for k in range(len(parts))]
    tail_clear = sem("a_tail_clear")
    stats = sem("a_stats")
    step = sem("a_step")
    var_ready = sem("a_var_ready")
    std_ready = sem("a_std_ready")
    rstd_ready = sem("a_rstd_ready")
    xn_ready = sem("a_xn_ready")
    xn_out = sem("a_xn_out")
    zero_ready = sem("a_zero_ready")
    filled = sem("a_filled")
    ones_filled = sem("a_ones_filled")
    weights_in = sem("a_weights_in")
    bias_clear = sem("a_bias_clear")
    bias_in = sem("a_bias_in")
    halved = sem("a_halved")
    width = g.zeros.shape[1]
    m = g.mom
    last = len(parts) - 1

    with nc.Block() as block:
        @block.sync
        def _(sp):
            for k, (t0, n) in enumerate(parts[:-1]):
                sp.dma_start(x[:, t0:t0 + n, :], split_rows(g.x_dram, t0, n)).then_inc(x_in[k], 16)
            sp.wait_ge(tail_clear, 1)
            sp.dma_start(x[0:TAIL, NT - 1, :], g.x_dram[(NT - 1) * P:NODES, :]).then_inc(x_in[last], 16)
            for k, (t0, n) in enumerate(parts):
                sp.wait_ge(xn_ready, t0 + n)
                sp.dma_start(split_rows(g.xn_dram, t0, n), xn[:, t0:t0 + n, :]).then_inc(xn_out, 16)
            sp.wait_ge(xn_out, 16 * len(parts))

        @block.gpsimd
        def _(pool):
            nc.gpsimd.memset(g.zeros[:], 0.0).then_inc(zero_ready, 1)
            nc.gpsimd.memset(g.ident[:], 0.0).then_inc(filled, 1)
            nc.gpsimd.memset(g.earlier[:], 1.0).then_inc(filled, 1)
            pool.wait_ge(filled, 2)
            nc.gpsimd.affine_select(out=g.ident[:], in_=g.ident[:], compare_op=ALU.not_equal, fill=1.0,
                                    base=0, pattern=[[-1, P]], channel_multiplier=1)
            nc.gpsimd.affine_select(out=g.earlier[:], in_=g.earlier[:], compare_op=ALU.is_gt, fill=0.0,
                                    base=0, pattern=[[-1, P]], channel_multiplier=1)
            nc.gpsimd.iota(g.trash_i[:], pattern=[[0, 1]], base=TRASH, channel_multiplier=1)

        @block.scalar
        def _(act):
            with nc.allow_non_contiguous_dma(reason="bias columns: a few hundred elements"):
                for t, src in g.weights:
                    act.dma_start(t[:], src).then_inc(weights_in, 16)
            act.wait_ge(bias_clear, len(g.biases))
            for whole, _, row in g.biases:
                for k in (0, BIAS_ROWS - 1):
                    act.dma_start(whole[k:k + 1, :], row).then_inc(bias_in, 16)
            act.wait_ge(zero_ready, 1)
            for table in g.sums_dram:
                flat = table.rearrange("(p r) c -> p (r c)", p=P)
                for k in range(ROWS // P * C // width):
                    act.dma_start(flat[:, k * width:(k + 1) * width], g.zeros[:]).then_inc(g.tables_clear, 16)
            for k in range(len(parts)):
                t0, n = parts[k]
                act.wait_ge(var_ready, k + 1)
                nc.scalar.activation(m.rstd[:, t0:t0 + n], m.rstd[:, t0:t0 + n], ACT.Sqrt).then_inc(std_ready, 1)
            act.wait_ge(weights_in, 16 * len(g.weights))

        @block.vector
        def _(dve):
            nc.vector.memset(x[:, NT - 1, :], 0.0).then_inc(tail_clear, 1)
            for whole, _, _ in g.biases:
                nc.vector.memset(whole[:], 0.0).then_inc(bias_clear, 1)
            nc.vector.memset(ones_f[:], 1.0).then_inc(ones_filled, 1)
            dve.wait_ge(ones_filled, 1)
            nc.vector.tensor_copy(g.ones2[:], ones_f[:])

            def gather_stats(k):
                t0, n = parts[k]
                dve.wait_ge(x_in[k], 16)
                for t in range(t0, t0 + n):
                    nc.vector.bn_stats(m.raw[:, t, :], x[:, t, :]).then_inc(stats, 1)
                dve.wait_ge(stats, t0 + n)
                combine_moments(nc, dve, m, t0, n, step, MOMENT_STEPS * k)
                dve.wait_ge(step, MOMENT_STEPS * (k + 1))
                dve.sem_inc(var_ready, 1)

            def normalise(k):
                t0, n = parts[k]
                dve.wait_ge(std_ready, k + 1)
                nc.vector.reciprocal(m.rstd[:, t0:t0 + n], m.rstd[:, t0:t0 + n]).then_inc(rstd_ready, 1)
                dve.wait_ge(rstd_ready, k + 1)
                for t in range(t0, t0 + n):
                    nc.vector.tensor_scalar(xn[:, t, :], x[:, t, :], m.mean[:, t:t + 1],
                                            m.rstd[:, t:t + 1], ALU.subtract, ALU.mult).then_inc(xn_ready, 1)

            for k in range(len(parts)):
                gather_stats(k)
                if k:
                    normalise(k - 1)
            normalise(last)
            dve.wait_ge(bias_in, 32 * len(g.biases))
            for k, (whole, halves, _) in enumerate(g.biases):
                low = slice(BIAS_ROWS - 1, BIAS_ROWS)
                nc.vector.tensor_copy(halves[:], whole[:]).then_inc(halved, 1)
                dve.wait_ge(halved, k + 1)
                nc.vector.tensor_tensor(halves[low, :], whole[low, :], halves[low, :].bitcast(F32), ALU.subtract)


def in_blocks(a):
    return a.rearrange("(b p) n -> p b n", p=P)


def as_columns(a):
    return a.rearrange("(b p) -> p b", p=P)


def as_row(a):
    return a.rearrange("(a n) -> a n", a=1)


def mixing_weights(sb, g):
    w = g.w
    g.wqkv = sb("wqkv", [P, CB, 3 * C], F32)
    g.wq_t = sb("wq_t", [P, CB, C], F32)
    g.wproj = sb("wproj", [P, CB, C], F32)
    g.wg1 = sb("wg1", [P, CB, GH], F32)
    g.wg2 = sb("wg2", [GH, C], F32)
    g.ln_g = sb("ln_g", [P, CB], F32)
    g.ln_b = sb("ln_b", [P, CB], F32)
    g.bg1 = sb("bg1", [GH, 1], F32)
    g.bg2 = sb("bg2", [P, CB], F32)
    g.wf2 = sb("wf2", [P, CB, C], F32)
    g.bf1 = sb("bf1", [P, CB], F32)
    return [
        (g.wqkv, in_blocks(w["mix_Wqkv"])), (g.wq_t, in_blocks(w["mix_WqT"])), (g.wproj, in_blocks(w["mix_Wproj"])),
        (g.wg1, in_blocks(w["mix_Wg1"])), (g.wg2, w["mix_Wg2"]), (g.ln_g, as_columns(w["mix_ln_g"])),
        (g.ln_b, as_columns(w["mix_ln_b"])), (g.bg1, w["mix_bg1"].rearrange("(p a) -> p a", a=1)),
        (g.bg2, as_columns(w["mix_bg2"])), (g.wf2, in_blocks(w["gnn_Wf2"])), (g.bf1, as_columns(w["gnn_bf1"]))]


def update_weights(sb, g):
    w = g.w
    g.wu1 = sb("wu1", [P, CB, C], F32)
    g.wu2 = sb("wu2", [P, CB, C], F32)
    g.bu1 = sb("bu1", [P, CB], F32)
    g.bu2 = sb("bu2", [P, CB], F32)
    g.gamma = sb("gamma", [P, CB], F32)
    g.beta = sb("beta", [P, CB], F32)
    return [
        (g.wu1, in_blocks(w["gnn_Wu1"])), (g.bu1, as_columns(w["gnn_bu1"])), (g.wu2, in_blocks(w["gnn_Wu2"])),
        (g.bu2, as_columns(w["gnn_bu2"])), (g.gamma, as_columns(w["gnn_gamma"])), (g.beta, as_columns(w["gnn_beta"]))]


def bias_row(sb, g, name):
    whole = sb(name + "_row", [BIAS_ROWS, C], F32)
    halves = sb(name + "_halves", [BIAS_ROWS, C], F32R)
    g.biases.append((whole, halves, as_row(g.w[name])))
    return halves


T_SCORES, K_SCORES = 0, 0
K_FOLD = K_SCORES + 4 * NG
T_GRAM, K_GRAM = T_SCORES + 4 * NG, K_FOLD + 1
T_CTX, K_CTX = T_GRAM + NT, K_GRAM + 4 * NG
T_OUT, K_OUT = T_CTX + 1, K_CTX + 1
T_OUT_PER, K_OUT_PER = 8, 10
SLOTS = 16
PAIRS_PER_PASS = 2 * NG


def is_first(v):
    return isinstance(v, int) and v == 0


def pair_tiles(k):
    return range(2 * k, min(2 * k + 2, GT))


def messages_and_attention(nc, sem, sb, g):
    HE = EC // 2
    PAIRS = ET // 2
    PER = ET // TABLES
    SPAN = 2 * 32 + EF
    attr = sb("attr", [SPAN, 2, HE], F32)
    attr_parts = sb("attr_parts", [SPAN, 2, HE], F32R)
    wf1_raw = sb("wf1_raw", [SPAN, C], F32)
    wf1_parts = sb("wf1_parts", [SPAN, C], F32R)
    src_row = sb("src_row", [P, 2, EC], I32)
    src_f = sb("src_f", [P, NCH * ET], F32)
    to_trash = sb("to_trash", [P, NCH * ET], F32)
    trash_f = sb("trash_f", [P, 1], F32)
    dst_all = sb("dst_all", [P, NCH * ET], I32)
    dst_idx = [sb(f"dst_idx{p}", [P, ET], I32) for p in range(2)]
    out_idx = [sb(f"out_idx{p}", [P, ET], I32) for p in range(2)]
    hidT = sb("hidT", [P, 2, CB, HE], F32)
    gathered = [sb(f"gathered{p}", [P, ET, C], F32) for p in range(2)]
    msg = sb("msg", [P, 2, 2, C], F32)
    same = sb("same", [P, 2, ET, P], F32)
    rank = sb("rank", [P, ET], F32)
    rank_scr = sb("rank_scr", [P, ET, P], mybir.dt.bfloat16)
    redirect = sb("redirect", [P, ET], F32)
    summed = [sb(f"summed{p}", [P, ET, C], F32) for p in range(2)]
    src_i = summed[0][:].rearrange("p t c -> p (t c)")[:, 0:NCH * ET].bitcast(I32)
    hps = [g.ps[0], g.ps[1]]
    fps = [g.ps[2], g.ps[3]]
    sps = g.ps[4]

    cols_in = sem("e_cols_in")
    cols_ready = sem("e_cols_ready")
    cleared = sem("e_cleared")
    wf1_in = sem("e_wf1_in")
    wf1_ready = sem("e_wf1_ready")
    attr_in = [sem(f"e_attr_in{h}") for h in range(2)]
    attr_rounded = sem("e_attr_rounded")
    attr_ready = sem("e_attr_ready")
    row_in = [sem(f"e_row_in{p}") for p in range(2)]
    hid_made = sem("e_hid_made")
    hid_ready = sem("e_hid_ready")
    filt_made = sem("e_filt_made")
    idx_ready = sem("e_idx_ready")
    rows_in = [[sem(f"e_rows_in{p}{h}") for h in range(2)] for p in range(2)]
    msg_ready = sem("e_msg_ready")
    same_ready = sem("e_same_ready")
    redirected = sem("e_redirected")
    out_ready = sem("e_out_ready")
    sum_made = sem("e_sum_made")
    sum_ready = sem("e_sum_ready")
    added = [sem(f"e_added{k}") for k in range(TABLES)]
    passed = sem("e_passed")

    xn = sb("xn_stage", [P, GT, C], F32)
    res = sb("res_stage", [P, GT, C], F32)
    turnedT = sb("turnedT", [P, CB, GC], F32)
    e_node = sb("e_node", [P, 2, C], F32)
    gramT = sb("gramT", [P, CB, C], F32)
    ctx_m = sb("ctx_m", [P, CB, P], F32)
    xhat = sb("xhat", [P, 2, 2, C], F32)
    hid = sb("hid", [GH, GC], F32)
    gate = sb("gate", [P, CB, GC], F32)
    bankT, bankK, bankG = g.ps[5], g.ps[6], g.ps[7]
    m = g.mom

    stage_in = sem("m_stage_in")
    t_made, t_free = sem("m_t_made"), sem("m_t_free")
    k_made, k_free = sem("m_k_made"), sem("m_k_free")
    stats = sem("m_stats")
    step = sem("m_step")
    var_ready = sem("m_var_ready")
    std_ready = sem("m_std_ready")
    rstd_ready = sem("m_rstd_ready")
    maxed = sem("m_maxed")
    folded = sem("m_folded")
    node_ready = sem("m_node_ready")
    gram_made = sem("m_gram_made")
    stage = sem("m_stage")
    x_in = sem("m_x_in")
    xhat_ready = sem("m_xhat_ready")
    presum_ready = sem("m_presum_ready")
    res_ready = sem("m_res_ready")
    res_out = sem("m_res_out")

    def along(eng, chunk, scores=None, gram=None, context=None, output=None):
        def group(base, s, share):
            for k in range(4):
                chunk(base + 2 * s + k // 2, k % 2, False,
                      (lambda q: share(s, 4 * k + q)) if share else (lambda q: None))

        def groups(base, share):
            group(base, 0, share)
            with eng.Fori(1, NG - 1) as s:
                group(base, s, share)
            group(base, NG - 1, share)

        groups(0, scores)
        groups(PAIRS_PER_PASS, gram)
        if context:
            context()
        groups(2 * PAIRS_PER_PASS, output)
        with eng.Fori(3 * PAIRS_PER_PASS, NCH // 2 - 1) as i:
            chunk(i, 0, False, lambda q: None)
            chunk(i, 1, False, lambda q: None)
        chunk(NCH // 2 - 1, 0, False, lambda q: None)
        chunk(NCH // 2 - 1, 1, True, lambda q: None)

    with nc.Block() as block:
        @block.sync
        def _(sp):
            def load_stage(s):
                sp.dma_start(xn[:], split_rows(g.xn_dram, s * GT, GT)).then_inc(stage_in, 16)

            def chunk(i, p, last, work):
                c = 2 * i + p
                for h in range(2):
                    if not is_first(c):
                        sp.wait_ge(attr_ready, 2 * (c - 1) + h + 1)
                    for copy in range(3):
                        sp.dma_start(attr[32 * copy:32 * copy + EF, h, :],
                                     g.attr_T[:, ds(c * EC + h * HE, HE)]).then_inc(attr_in[h], 16)
                if not is_first(i):
                    sp.wait_ge(same_ready, PAIRS * (c - 1))
                sp.dma_start(src_row[:, p, :],
                             g.src_rows[ds(c, 1), :].to_broadcast([P, EC])).then_inc(row_in[p], 16)
                work(0)

            def scores(s, slot):
                if slot == 12:
                    sp.wait_ge(t_made, T_SCORES + 4 * s + 4)
                    sp.wait_ge(stats, GT * s + GT)
                    load_stage(0 if isinstance(s, int) and s == NG - 1 else s + 1)

            def gram(s, slot):
                if slot == 12:
                    sp.wait_ge(gram_made, 1 + GT * s + GT)
                    load_stage(0 if isinstance(s, int) and s == NG - 1 else s + 1)

            def store_res(s):
                sp.wait_ge(res_ready, 4 * s + 4)
                sp.dma_start(split_rows(g.res_dram, s * GT, GT), res[:]).then_inc(res_out, 16)

            def load_x(s):
                if not is_first(s):
                    sp.wait_ge(res_out, 16 * s)
                if isinstance(s, int) and s == NG - 1:
                    sp.dma_start(res[:, 0:GT - 1, :], split_rows(g.x_dram, s * GT, GT - 1)).then_inc(x_in, 16)
                    sp.dma_start(res[0:TAIL, GT - 1, :], g.x_dram[(NT - 1) * P:NODES, :]).then_inc(x_in, 16)
                else:
                    sp.dma_start(res[:], split_rows(g.x_dram, s * GT, GT)).then_inc(x_in, 16)

            def output(s, slot):
                if slot == 4 and not is_first(s):
                    store_res(s - 1)
                    load_x(s)
                if slot == 12 and not (isinstance(s, int) and s == NG - 1):
                    sp.wait_ge(presum_ready, 4 * s + 4)
                    load_stage(s + 1)

            sp.dma_start(src_i, g.src_cols).then_inc(cols_in, 16)
            sp.dma_start(dst_all[:], g.dst_cols).then_inc(cols_in, 16)
            sp.wait_ge(cleared, 2)
            for copy in range(3):
                sp.dma_start(wf1_raw[32 * copy:32 * copy + EF, :], g.w["gnn_Wf1"]).then_inc(wf1_in, 16)
            load_stage(0)
            along(sp, chunk, scores, gram, lambda: load_x(0), output)
            store_res(NG - 1)
            sp.wait_ge(res_out, 16 * NG)

        @block.gpsimd
        def _(pool):
            def gather(i, p):
                c = 2 * i + p
                pool.wait_ge(idx_ready, c + 1)
                if not is_first(i):
                    pool.wait_ge(msg_ready, PAIRS * (c - 1))
                pool.sem_inc(passed, 1)
                for t in range(ET):
                    nc.gpsimd.indirect_dma_start(
                        gathered[p][:, t, :], None, g.xn_dram,
                        bass.IndirectOffsetOnAxis(ap=dst_idx[p][:, t:t + 1], axis=0)
                    ).then_inc(rows_in[p][t // PAIRS], 16)
                    yield

            def chunk(i, p, last, work):
                c = 2 * i + p
                ahead = None if last else gather(i + p, 1 - p)
                for t in range(ET):
                    if ahead:
                        next(ahead)
                    if t == 0:
                        pool.wait_ge(out_ready, c + 1)
                    if t % 2 == 0:
                        pool.wait_ge(sum_ready, PAIRS * c + t // 2 + 1)
                    k = t % TABLES
                    if not (is_first(c) and t < TABLES):
                        pool.wait_ge(added[k], 16 * (PER * c + t // TABLES))
                    pool.sem_inc(passed, 1)
                    nc.gpsimd.indirect_dma_start(
                        g.sums_dram[k], bass.IndirectOffsetOnAxis(ap=out_idx[p][:, t:t + 1], axis=0),
                        summed[p][:, t, :], None, compute_op=ALU.add).then_inc(added[k], 16)

            nc.gpsimd.memset(attr[:], 0.0).then_inc(cleared, 1)
            for _g in gather(0, 0):
                pass
            pool.wait_ge(g.tables_clear, g.clear_count)
            along(pool, chunk)
            for k in range(TABLES):
                pool.wait_ge(added[k], 16 * PER * NCH)

        @block.tensor
        def _(pe):
            T = nc.tensor

            def hidden(i, p, h):
                c = 2 * i + p
                pe.wait_ge(attr_ready, 2 * c + h + 1)
                for f in range(CB):
                    if not (is_first(c) and h == 0):
                        pe.wait_ge(hid_ready, 2 * (2 * c + h) - 1 + f)
                    mm = T.matmul(hps[f][:], wf1_parts[:, ds(f * P, P)], attr_parts[:, h, :], start=True, stop=True)
                mm.then_inc(hid_made, 1)

            def filt(i, p, j):
                c = 2 * i + p
                h = j // 2
                if j % 2 == 0:
                    pe.wait_ge(hid_ready, 4 * c + 2 * h + 2)
                if not (is_first(c) and j < 2):
                    pe.wait_ge(msg_ready, PAIRS * c + j - 1)
                for t in range(2):
                    out = fps[j % 2][:, ds(t * C, C)]
                    T.matmul(out, g.ones2[:], g.bf2[:], start=True, stop=False)
                    for f in range(CB):
                        mm = T.matmul(out, hidT[:, h, f, ds((2 * (j % 2) + t) * P, P)], g.wf2[:, f, :],
                                      start=False, stop=f == CB - 1)
                mm.then_inc(filt_made, 1)

            def merge(i, p, j):
                c = 2 * i + p
                pe.wait_ge(msg_ready, PAIRS * c + j + 1)
                pe.wait_ge(same_ready, PAIRS * c + j + 1)
                if not (is_first(c) and j == 0):
                    pe.wait_ge(sum_ready, PAIRS * c + j)
                for t in range(2):
                    mm = T.matmul(sps[:, ds(t * C, C)], same[:, p, 2 * j + t, :], msg[:, j % 2, t, :],
                                  start=True, stop=True)
                mm.then_inc(sum_made, 1)

            def chunk(i, p, last, work):
                filt(i, p, 0)
                if not is_first(2 * i + p):
                    merge(i + p - 1, 1 - p, 3)
                work(0)
                filt(i, p, 1)
                merge(i, p, 0)
                if not last:
                    hidden(i + p, 1 - p, 0)
                work(1)
                filt(i, p, 2)
                merge(i, p, 1)
                work(2)
                filt(i, p, 3)
                merge(i, p, 2)
                if not last:
                    hidden(i + p, 1 - p, 1)
                work(3)

            def turn_rows(out, rows, n_tiles):
                for t in range(n_tiles):
                    for b in range(CB):
                        mm = T.transpose(out[:, ds((t * CB + b) * P, P)], rows[:, t, ds(b * P, P)], g.ident[:])
                return mm

            def k_product(s, j):
                h, f = j // CB, j % CB
                for b in range(CB):
                    mm = T.matmul(bankK[:, 0:HC], g.wqkv[:, b, ds(C + f * P, P)],
                                  g.xT[:, b, ds(s * GC + h * HC, HC)], start=b == 0, stop=b == CB - 1)
                mm.then_inc(k_made, 1)

            def scores(s, slot):
                if slot < 4:
                    if slot == 0:
                        pe.wait_ge(stage_in, 16 * (s + 1))
                    pe.wait_ge(t_free, 1 + T_SCORES + 4 * s + slot)
                    tiles = pair_tiles(slot)
                    turn_rows(bankT, xn[:, tiles[0]:tiles[-1] + 1, :], len(tiles)).then_inc(t_made, 1)
                elif 5 <= slot < 9:
                    j = slot - 5
                    pe.wait_ge(t_free, 1 + T_SCORES + 4 * s + 4)
                    pe.wait_ge(k_free, 1 + K_SCORES + 4 * s + j)
                    k_product(s, j)
                if isinstance(s, int) and s == NG - 1 and slot == 10:
                    pe.wait_ge(k_free, 1 + K_FOLD)
                    for b in range(CB):
                        mm = T.matmul(bankK[0:GH, 0:1], g.wg1[:, b, :], g.ln_b[:, b:b + 1],
                                      start=b == 0, stop=b == CB - 1)
                    mm.then_inc(k_made, 1)

            def gram(s, slot):
                if slot < 4:
                    pe.wait_ge(k_free, 1 + K_GRAM + 4 * s + slot)
                    k_product(s, slot)
                if 4 <= slot < 4 + GT:
                    t = slot - 4
                    pe.wait_ge(k_free, 1 + K_GRAM + 4 * s + 4)
                    pe.wait_ge(t_free, 1 + T_GRAM + GT * s + t)
                    rows = rows_of(s * GT + t)
                    for f in range(CB):
                        mm = T.transpose(bankT[0:rows, ds(f * P, P)], turnedT[:, f, ds(t * P, rows)], g.ident[:])
                    mm.then_inc(t_made, 1)
                if 5 <= slot < 5 + GT:
                    t = slot - 5
                    if t == 0:
                        pe.wait_ge(stage_in, 16 * (NG + s + 1))
                    pe.wait_ge(node_ready, GT * s + t + 1)
                    rows = rows_of(s * GT + t)
                    for b in range(CB):
                        mm = T.matmul(bankG[:, ds(b * C, C)], xn[0:rows, t, ds(b * P, P)], e_node[0:rows, t % 2, :],
                                      start=is_first(s) and t == 0 and b == 0,
                                      stop=isinstance(s, int) and s == NG - 1 and t == GT - 1 and b == CB - 1,
                                      skip_group_check=True)
                    mm.then_inc(gram_made, 1)

            def context():
                pe.wait_ge(stage, 1)
                pe.wait_ge(k_free, 1 + K_CTX)
                for f in range(CB):
                    for b in range(CB):
                        mm = T.matmul(bankK[:, ds(f * P, P)], gramT[:, b, ds(f * P, P)],
                                      g.wqkv[:, b, ds(2 * C + f * P, P)], start=b == 0, stop=b == CB - 1)
                mm.then_inc(k_made, 1)
                pe.wait_ge(k_free, 1 + K_OUT)
                pe.wait_ge(t_free, 1 + T_CTX)
                for b in range(CB):
                    for f in range(CB):
                        mm = T.matmul(bankT[:, ds(b * C + f * P, P)], g.wq_t[:, f, ds(b * P, P)],
                                      ctx_m[:, f, :], start=True, stop=True)
                mm.then_inc(t_made, 1)

            def output(s, slot):
                t0, k0 = T_OUT + T_OUT_PER * s, K_OUT + K_OUT_PER * s
                if 1 <= slot < 5:
                    k = slot - 1
                    pe.wait_ge(xhat_ready, 4 * s + k + 1)
                    pe.wait_ge(t_free, 1 + t0 + k)
                    turn_rows(bankT, xhat[:, k % 2, :, :], len(pair_tiles(k))).then_inc(t_made, 1)
                if 5 <= slot < 7:
                    h = slot - 5
                    pe.wait_ge(t_free, 1 + t0 + 4)
                    pe.wait_ge(k_free, 1 + k0 + h)
                    for b in range(CB):
                        mm = T.matmul(bankK[0:GH, 0:HC], g.wg1f[:, b, :], turnedT[:, b, ds(h * HC, HC)],
                                      start=b == 0, stop=b == CB - 1)
                    mm.then_inc(k_made, 1)
                if 7 <= slot < 11:
                    j = slot - 7
                    h, f = j // CB, j % CB
                    pe.wait_ge(k_free, 1 + k0 + 2 + j)
                    T.matmul(bankK[:, 0:HC], g.wg2[:, ds(f * P, P)], hid[:, ds(h * HC, HC)],
                             start=True, stop=True).then_inc(k_made, 1)
                if 8 <= slot < 12:
                    j = slot - 8
                    h, f = j // CB, j % CB
                    pe.wait_ge(t_free, 1 + t0 + 4 + j)
                    for b in range(CB):
                        mm = T.matmul(bankT[:, 0:HC], g.wqm[:, b, ds(f * P, P)],
                                      g.xT[:, b, ds(s * GC + h * HC, HC)], start=b == 0, stop=b == CB - 1)
                    mm.then_inc(t_made, 1)
                if slot >= 12:
                    k = slot - 12
                    pe.wait_ge(t_free, 1 + t0 + 8)
                    pe.wait_ge(k_free, 1 + k0 + 6 + k)
                    for n, t in enumerate(pair_tiles(k)):
                        out = bankK[:, ds(n * C, C)]
                        T.matmul(out, g.ones2[:], g.bproj[:], start=True, stop=False)
                        for f in range(CB):
                            mm = T.matmul(out, gate[:, f, ds(t * P, P)], g.wproj[:, f, :],
                                          start=False, stop=f == CB - 1)
                    mm.then_inc(k_made, 1)

            pe.sem_inc(gram_made, 1)
            pe.wait_ge(wf1_ready, 2)
            hidden(0, 0, 0)
            hidden(0, 0, 1)
            along(pe, chunk, scores, gram, context, output)
            merge(NCH // 2 - 1, 1, 3)

        @block.scalar
        def _(act):
            A = nc.scalar

            def silu(i, p, h):
                c = 2 * i + p
                act.wait_ge(hid_made, 2 * c + h + 1)
                if not is_first(c):
                    act.wait_ge(filt_made, PAIRS * (c - 1) + 2 * h + 2)
                for f in range(CB):
                    A.activation(hidT[:, h, f, :], hps[f][:], ACT.Silu, bias=g.bf1[:, f:f + 1]).then_inc(hid_ready, 1)

            def copy_sums(i, p, j):
                c = 2 * i + p
                act.wait_ge(sum_made, PAIRS * c + j + 1)
                if not is_first(i):
                    for k in range(TABLES):
                        act.wait_ge(added[k], 16 * PER * (c - 1))
                A.activation(summed[p][:, ds(2 * j, 2), :], sps[:].rearrange("p (t c) -> p t c", c=C),
                             ACT.Copy).then_inc(sum_ready, 1)

            def chunk(i, p, last, work):
                if not is_first(2 * i + p):
                    copy_sums(i + p - 1, 1 - p, 3)
                work(0)
                if not last:
                    silu(i + p, 1 - p, 0)
                copy_sums(i, p, 0)
                work(1)
                copy_sums(i, p, 1)
                work(2)
                if not last:
                    silu(i + p, 1 - p, 1)
                copy_sums(i, p, 2)
                work(3)

            def copy_turned(dst, c0, n):
                A.activation(dst[:, :, ds(c0, n * P)].rearrange("p f (t n) -> p f t n", n=P),
                             bankT[:, 0:n * C].rearrange("p (t f n) -> p f t n", f=CB, n=P),
                             ACT.Copy).then_inc(t_free, 1)

            def scores(s, slot):
                if slot < 4:
                    act.wait_ge(t_made, T_SCORES + 4 * s + slot + 1)
                    copy_turned(g.xT, s * GC + slot * 2 * P, len(pair_tiles(slot)))
                if isinstance(s, int) and s == NG - 1 and slot == 14:
                    act.wait_ge(var_ready, 1)
                    A.activation(m.rstd[:], m.rstd[:], ACT.Sqrt).then_inc(std_ready, 1)

            def gram(s, slot):
                if slot < 4:
                    h, f = slot // CB, slot % CB
                    n = tail_cols(s, h) if isinstance(s, int) and s == NG - 1 else HC
                    if is_first(s):
                        act.wait_ge(maxed, CB)
                    act.wait_ge(k_made, K_GRAM + 4 * s + slot + 1)
                    act.wait_ge(t_made, T_GRAM + GT * s)
                    A.activation(turnedT[:, f, ds(h * HC, n)], bankK[:, 0:n], ACT.Exp, bias=g.neg_k_max[:, f:f + 1],
                                 accum_out=g.k_sum[:, f, ds(2 * s + h, 1)]).then_inc(k_free, 1)

            def output(s, slot):
                t0, k0 = T_OUT + T_OUT_PER * s, K_OUT + K_OUT_PER * s
                if 1 <= slot < 5:
                    k = slot - 1
                    act.wait_ge(t_made, t0 + k + 1)
                    act.wait_ge(k_made, k0 - K_OUT_PER + 2)
                    copy_turned(turnedT, k * 2 * P, len(pair_tiles(k)))
                if 5 <= slot < 7:
                    h = slot - 5
                    act.wait_ge(k_made, k0 + h + 1)
                    A.activation(hid[:, ds(h * HC, HC)], bankK[0:GH, 0:HC], ACT.Gelu,
                                 bias=g.bg1f[:, 0:1]).then_inc(k_free, 1)
                if 7 <= slot < 11:
                    j = slot - 7
                    h, f = j // CB, j % CB
                    act.wait_ge(k_made, k0 + 2 + j + 1)
                    A.activation(gate[:, f, ds(h * HC, HC)], bankK[:, 0:HC], ACT.Sigmoid,
                                 bias=g.bg2[:, f:f + 1]).then_inc(k_free, 1)

            silu(0, 0, 0)
            silu(0, 0, 1)
            along(act, chunk, scores, gram, None, output)
            copy_sums(NCH // 2 - 1, 1, 3)

        @block.vector
        def _(dve):
            V = nc.vector

            def split_attr(i, p, h):
                c = 2 * i + p
                dve.wait_ge(attr_in[h], 48 * (c + 1))
                if not is_first(c):
                    dve.wait_ge(hid_made, 2 * (c - 1) + h + 1)
                V.tensor_copy(attr_parts[:, h, :], attr[:, h, :]).then_inc(attr_rounded, 1)
                dve.wait_ge(attr_rounded, 2 * c + h + 1)
                V.tensor_tensor(attr_parts[64:SPAN, h, :], attr[64:SPAN, h, :],
                                attr_parts[64:SPAN, h, :].bitcast(F32), ALU.subtract).then_inc(attr_ready, 1)

            def dst_columns(i, p):
                V.tensor_copy(dst_idx[p][:], dst_all[:, ds((2 * i + p) * ET, ET)]).then_inc(idx_ready, 1)

            def equal(i, p, j):
                c = 2 * i + p
                if j == 0:
                    dve.wait_ge(row_in[p], 16 * i + 16)
                    if not is_first(i):
                        dve.wait_ge(sum_made, PAIRS * (c - 1))
                for t in range(2 * j, 2 * j + 2):
                    row = src_row[:, p, ds(t * P, P)]
                    col = src_f[:, ds(c * ET + t, 1)]
                    V.tensor_scalar(same[:, p, t, :], row, col, None, ALU.is_equal)
                    op = V.scalar_tensor_tensor(out=rank_scr[:, t, :], in0=row, scalar=col, in1=g.earlier[:],
                                                op0=ALU.is_equal, op1=ALU.mult, accum_out=rank[:, t:t + 1])
                op.then_inc(same_ready, 1)

            def out_rows(i, p):
                c = 2 * i + p
                dve.wait_ge(same_ready, PAIRS * c + PAIRS)
                V.scalar_tensor_tensor(out=redirect[:], in0=rank[:], scalar=0.0, in1=to_trash[:, ds(c * ET, ET)],
                                       op0=ALU.is_gt, op1=ALU.mult).then_inc(redirected, 1)
                dve.wait_ge(redirected, c + 1)
                if not is_first(i):
                    for k in range(TABLES):
                        dve.wait_ge(added[k], 16 * PER * (c - 1))
                V.tensor_tensor(out_idx[p][:], redirect[:], src_f[:, ds(c * ET, ET)], ALU.add).then_inc(out_ready, 1)

            def message(i, p, j):
                c = 2 * i + p
                if j % 2 == 0:
                    dve.wait_ge(rows_in[p][j // 2], 16 * PAIRS * (i + 1))
                dve.wait_ge(filt_made, PAIRS * c + j + 1)
                if not (is_first(c) and j < 2):
                    dve.wait_ge(sum_made, PAIRS * c + j - 1)
                V.tensor_tensor(msg[:, j % 2, :, :], fps[j % 2][:].rearrange("p (t c) -> p t c", c=C),
                                gathered[p][:, ds(2 * j, 2), :], ALU.mult).then_inc(msg_ready, 1)

            def chunk(i, p, last, work):
                for j in range(PAIRS):
                    message(i, p, j)
                    if j % 2 == 0 and not last:
                        split_attr(i + p, 1 - p, j // 2)
                    if j == 2 and not (isinstance(i, int) and i == NCH // 2 - 1):
                        dst_columns(i + 1, p)
                    if not last:
                        equal(i + p, 1 - p, j)
                    work(j)
                if not last:
                    out_rows(i + p, 1 - p)

            def scores(s, slot):
                if slot < 4:
                    if slot == 0:
                        dve.wait_ge(stage_in, 16 * (s + 1))
                    for t in pair_tiles(slot):
                        V.bn_stats(m.raw[:, s * GT + t, :], xn[:, t, :]).then_inc(stats, 1)
                if 5 <= slot < 9:
                    j = slot - 5
                    h, f = j // CB, j % CB
                    n = tail_cols(s, h) if isinstance(s, int) and s == NG - 1 else HC
                    dve.wait_ge(k_made, K_SCORES + 4 * s + j + 1)
                    V.tensor_reduce(g.k_max[:, f, ds(2 * s + h, 1)], bankK[:, 0:n], X, ALU.max).then_inc(k_free, 1)
                if not (isinstance(s, int) and s == NG - 1):
                    return
                if slot == 9:
                    dve.wait_ge(k_free, 1 + 4 * NG)
                    for f in range(CB):
                        V.tensor_reduce(g.neg_k_max[:, f:f + 1], g.k_max[:, f, :], X, ALU.max,
                                        negate=True).then_inc(maxed, 1)
                if slot == 10:
                    dve.wait_ge(k_made, K_FOLD + 1)
                    V.tensor_tensor(g.bg1f[:], bankK[0:GH, 0:1], g.bg1[:], ALU.add).then_inc(k_free, 1)
                    for b in range(CB):
                        V.tensor_scalar(g.wg1f[:, b, :], g.wg1[:, b, :], g.ln_g[:, b:b + 1], None,
                                        ALU.mult).then_inc(folded, 1)
                if slot == 12:
                    V.memset(g.head_mask[:], 0.0).then_inc(folded, 1)
                    dve.wait_ge(folded, CB + 1)
                    for h in range(P // MD):
                        V.memset(g.head_mask[ds(h * MD, MD), ds(h * MD, MD)], 1.0).then_inc(folded, 1)
                if slot == 13:
                    dve.wait_ge(stats, NT)
                    combine_moments(nc, dve, m, 0, NT, step, 0)
                    dve.wait_ge(step, MOMENT_STEPS)
                    dve.sem_inc(var_ready, 1)

            def gram(s, slot):
                if is_first(s) and slot == 0:
                    dve.wait_ge(std_ready, 1)
                if 4 <= slot < 4 + GT:
                    t = slot - 4
                    rows = rows_of(s * GT + t)
                    dve.wait_ge(t_made, T_GRAM + GT * s + t + 1)
                    dve.wait_ge(gram_made, 1 + GT * s + max(t - 1, 0))
                    V.tensor_copy(e_node[0:rows, t % 2, :], bankT[0:rows, 0:C]).then_inc(node_ready, 1)
                    dve.wait_ge(node_ready, GT * s + t + 1)
                    dve.sem_inc(t_free, 1)

            def context():
                dve.wait_ge(std_ready, 1)
                V.reciprocal(m.rstd[:], m.rstd[:]).then_inc(rstd_ready, 1)
                dve.wait_ge(gram_made, 1 + NT)
                V.tensor_copy(gramT[:].rearrange("p b n -> p (b n)"), bankG[:]).then_inc(stage, 1)
                dve.wait_ge(k_free, 1 + K_CTX)
                V.tensor_reduce(g.k_tot[:], g.k_sum[:], X, ALU.add).then_inc(stage, 1)
                dve.wait_ge(stage, 2)
                V.reciprocal(g.k_inv[:], g.k_tot[:]).then_inc(stage, 1)
                dve.wait_ge(stage, 3)
                dve.wait_ge(folded, CB + 1 + P // MD)
                dve.wait_ge(k_made, K_CTX + 1)
                for f in range(CB):
                    V.scalar_tensor_tensor(out=ctx_m[:, f, :], in0=bankK[:, ds(f * P, P)],
                                           scalar=g.k_inv[:, f:f + 1], in1=g.head_mask[:],
                                           op0=ALU.mult, op1=ALU.mult).then_inc(stage, 1)
                dve.wait_ge(stage, 3 + CB)
                dve.sem_inc(k_free, 1)
                dve.wait_ge(t_made, T_CTX + 1)
                V.tensor_copy(g.wqm[:], bankT[:].rearrange("p (b n) -> p b n", b=CB)).then_inc(t_free, 1)
                dve.wait_ge(rstd_ready, 1)

            def output(s, slot):
                t0, k0 = T_OUT + T_OUT_PER * s, K_OUT + K_OUT_PER * s
                if slot < 4:
                    if slot == 0:
                        dve.wait_ge(stage_in, 16 * (2 * NG + s + 1))
                    before = t0 + slot - 1 if slot >= 2 else t0 - T_OUT_PER + slot + 3
                    dve.wait_ge(t_made, before)
                    for n, t in enumerate(pair_tiles(slot)):
                        op = V.tensor_scalar(xhat[:, slot % 2, n, :], xn[:, t, :], m.mean[:, ds(s * GT + t, 1)],
                                             m.rstd[:, ds(s * GT + t, 1)], ALU.subtract, ALU.mult)
                    op.then_inc(xhat_ready, 1)
                if 4 <= slot < 8:
                    k = slot - 4
                    if k == 0:
                        dve.wait_ge(x_in, 16 * (s + 1) + (16 if isinstance(s, int) and s == NG - 1 else 0))
                    tiles = pair_tiles(k)
                    here = slice(tiles[0], tiles[-1] + 1)
                    V.tensor_tensor(res[:, here, :], res[:, here, :], xn[:, here, :], ALU.add).then_inc(presum_ready, 1)
                if 8 <= slot < 12:
                    j = slot - 8
                    h, f = j // CB, j % CB
                    dve.wait_ge(t_made, t0 + 4 + j + 1)
                    dve.wait_ge(k_free, 1 + k0 + 2 + j + 1)
                    cols = gate[:, f, ds(h * HC, HC)]
                    V.tensor_tensor(cols, bankT[:, 0:HC], cols, ALU.mult).then_inc(t_free, 1)
                if slot >= 12:
                    k = slot - 12
                    tiles = pair_tiles(k)
                    here = slice(tiles[0], tiles[-1] + 1)
                    dve.wait_ge(presum_ready, 4 * s + k + 1)
                    dve.wait_ge(k_made, k0 + 6 + k + 1)
                    V.tensor_tensor(res[:, here, :], bankK[:, 0:len(tiles) * C].rearrange("p (t c) -> p t c", c=C),
                                    res[:, here, :], ALU.add).then_inc(res_ready, 1)
                    dve.wait_ge(res_ready, 4 * s + k + 1)
                    dve.sem_inc(k_free, 1)

            dve.sem_inc(t_free, 1)
            dve.sem_inc(k_free, 1)
            V.memset(wf1_raw[:], 0.0).then_inc(cleared, 1)
            dve.wait_ge(cols_in, 32)
            V.tensor_copy(src_f[:], src_i).then_inc(cols_ready, 1)
            V.tensor_copy(trash_f[:], g.trash_i[:]).then_inc(cols_ready, 1)
            dve.wait_ge(cols_ready, 2)
            V.tensor_scalar(to_trash[:], src_f[:], trash_f[:, 0:1], -1.0, ALU.subtract, ALU.mult).then_inc(cols_ready, 1)
            dve.wait_ge(cols_ready, 3)
            dst_columns(0, 0)
            dst_columns(0, 1)
            dve.wait_ge(wf1_in, 48)
            V.tensor_copy(wf1_parts[:], wf1_raw[:]).then_inc(wf1_ready, 1)
            dve.wait_ge(wf1_ready, 1)
            V.tensor_tensor(wf1_parts[32:64, :], wf1_raw[32:64, :], wf1_parts[32:64, :].bitcast(F32),
                            ALU.subtract).then_inc(wf1_ready, 1)
            split_attr(0, 0, 0)
            split_attr(0, 0, 1)
            for j in range(PAIRS):
                equal(0, 0, j)
            out_rows(0, 0)
            along(dve, chunk, scores, gram, context, output)


def update_nodes(nc, sem, sb, g):
    parts_in = [sem(f"u_parts_in{p}") for p in range(2)]
    weights = update_weights(sb, g)
    weights_in = sem("u_weights_in")
    res_in = sem("u_res_in")
    agg_ready = sem("u_agg_ready")
    turned = sem("u_turned")
    turn_copied = sem("u_turn_copied")
    hid_made = sem("u_hid_made")
    hid_ready = sem("u_hid_ready")
    h_made = sem("u_h_made")
    h_ready = sem("u_h_ready")
    stats = sem("u_stats")
    chain = sem("u_chain")
    norm_ready = sem("u_norm_ready")
    back_made = sem("u_back_made")
    back_ready = sem("u_back_ready")
    part = [[sb(f"part{p}{k}", [P, GT, C], F32) for k in range(TABLES)] for p in range(2)]
    aggT = sb("aggT", [P, CB, GC], F32)
    hidT = sb("u_hidT", [P, CB, GC], F32)
    hT = sb("hT", [P, CB, NPAD], F32)
    raw = sb("bn_raw", [P, CB, 2 * NG, 6], F32)
    mv = sb("bn_mv", [P, CB, 2], F32)
    sd = sb("bn_sd", [P, CB], F32)
    scale = sb("bn_scale", [P, CB], F32)
    shift = sb("bn_shift", [P, CB], F32)
    turn = [g.ps[0], g.ps[1]]
    ups = [g.ps[2], g.ps[3]]
    hps = [g.ps[4], g.ps[5]]
    bps = [g.ps[6], g.ps[7]]

    with nc.Block() as block:
        @block.sync
        def _(sp):
            for s in range(NG):
                if s >= 2:
                    sp.wait_ge(turned, 4 * (s - 1))
                for k in range(TABLES):
                    sp.dma_start(part[s % 2][k][:], split_rows(g.sums_dram[k], s * GT, GT)).then_inc(parts_in[s % 2], 16)
            sp.dma_start(g.res[:], split_rows(g.res_dram, 0, NT)).then_inc(res_in, 16)

        @block.tensor
        def _(pe):
            pe.wait_ge(weights_in, 16 * len(weights))
            for s in range(NG):
                pe.wait_ge(agg_ready, s + 1)
                for k in range(4):
                    if 4 * s + k >= 2:
                        pe.wait_ge(turn_copied, 4 * s + k - 1)
                    for t in range(2 * k, min(2 * k + 2, GT)):
                        for b in range(CB):
                            mm = nc.tensor.transpose(turn[k % 2][:, ds((t % 2 * CB + b) * P, P)],
                                                     part[s % 2][0][:, t, ds(b * P, P)], g.ident[:])
                    mm.then_inc(turned, 1)
                pe.wait_ge(turn_copied, 4 * s + 4)
                for w, src, bank, made, ready in ((g.wu1, aggT, ups, hid_made, hid_ready),
                                                  (g.wu2, hidT, hps, h_made, h_ready)):
                    if w is g.wu2:
                        pe.wait_ge(hid_ready, 4 * s + 4)
                    for j in range(4):
                        h, f = j // CB, j % CB
                        if 4 * s + j >= 2:
                            pe.wait_ge(ready, 4 * s + j - 1)
                        for b in range(CB):
                            mm = nc.tensor.matmul(bank[f][:, 0:HC], w[:, b, ds(f * P, P)], src[:, b, ds(h * HC, HC)],
                                                  start=b == 0, stop=b == CB - 1)
                        mm.then_inc(made, 1)
            for s in range(NG):
                pe.wait_ge(norm_ready, CB * (s + 1))
                for k in range(4):
                    if 4 * s + k >= 2:
                        pe.wait_ge(back_ready, 4 * s + k - 1)
                    for t in range(2 * k, min(2 * k + 2, GT)):
                        for f in range(CB):
                            mm = nc.tensor.transpose(bps[k % 2][:, ds((t % 2 * CB + f) * P, P)],
                                                     hT[:, f, ds(s * GC + t * P, P)], g.ident[:])
                    mm.then_inc(back_made, 1)

        @block.scalar
        def _(act):
            with nc.allow_non_contiguous_dma(reason="bias columns: a few hundred elements"):
                for t, src in weights:
                    act.dma_start(t[:], src).then_inc(weights_in, 16)
            act.wait_ge(weights_in, 16 * len(weights))
            for s in range(NG):
                for k in range(4):
                    n = 2 if k < 3 else 1
                    act.wait_ge(turned, 4 * s + k + 1)
                    if s:
                        act.wait_ge(hid_made, 4 * s)
                    nc.scalar.activation(
                        aggT[:, :, ds(k * 2 * P, n * P)].rearrange("p f (t n) -> p f t n", n=P),
                        turn[k % 2][:, 0:n * C].rearrange("p (t f n) -> p f t n", f=CB, n=P),
                        ACT.Copy).then_inc(turn_copied, 1)
                for j in range(4):
                    h, f = j // CB, j % CB
                    act.wait_ge(hid_made, 4 * s + j + 1)
                    if s:
                        act.wait_ge(h_made, 4 * s)
                    nc.scalar.activation(hidT[:, f, ds(h * HC, HC)], ups[f][:, 0:HC], ACT.Silu,
                                         bias=g.bu1[:, f:f + 1]).then_inc(hid_ready, 1)
            act.wait_ge(chain, 3)
            nc.scalar.activation(sd[:], sd[:], ACT.Sqrt).then_inc(chain, 1)
            act.wait_ge(chain, 8)
            for s in range(NG):
                for f in range(CB):
                    cols = hT[:, f, ds(s * GC, GC)]
                    nc.scalar.activation(cols, cols, ACT.Identity, bias=shift[:, f:f + 1],
                                         scale=scale[:, f:f + 1]).then_inc(norm_ready, 1)

        @block.vector
        def _(dve):
            def gather_sums(s):
                dve.wait_ge(parts_in[s % 2], 32 * (s // 2 + 1))
                a, b = part[s % 2]
                nc.vector.tensor_tensor(a[:], a[:], b[:], ALU.add).then_inc(agg_ready, 1)

            dve.wait_ge(weights_in, 16 * len(weights))
            gather_sums(0)
            for s in range(NG):
                if s + 1 < NG:
                    gather_sums(s + 1)
                for j in range(4):
                    h, f = j // CB, j % CB
                    dve.wait_ge(h_made, 4 * s + j + 1)
                    nc.vector.tensor_scalar(hT[:, f, ds(s * GC + h * HC, HC)], hps[f][:, 0:HC],
                                            g.bu2[:, f:f + 1], None, ALU.add).then_inc(h_ready, 1)
                    dve.wait_ge(h_ready, 4 * s + j + 1)
                    n = HC if s < NG - 1 else tail_cols(s, h)
                    nc.vector.bn_stats(raw[:, f, 2 * s + h, :],
                                       hT[:, f, ds(s * GC + h * HC, n)]).then_inc(stats, 1)
            dve.wait_ge(stats, 4 * NG)
            for f in range(CB):
                nc.vector.bn_aggr(mv[:, f, :], raw[:, f, :, :]).then_inc(chain, 1)
            dve.wait_ge(chain, 2)
            nc.vector.tensor_scalar(sd[:], mv[:, :, 1], EPS, None, ALU.add).then_inc(chain, 1)
            dve.wait_ge(chain, 4)
            nc.vector.reciprocal(sd[:], sd[:]).then_inc(chain, 1)
            dve.wait_ge(chain, 5)
            nc.vector.tensor_tensor(scale[:], g.gamma[:], sd[:], ALU.mult).then_inc(chain, 1)
            dve.wait_ge(chain, 6)
            nc.vector.tensor_tensor(shift[:], mv[:, :, 0], scale[:], ALU.mult).then_inc(chain, 1)
            dve.wait_ge(chain, 7)
            nc.vector.tensor_tensor(shift[:], g.beta[:], shift[:], ALU.subtract).then_inc(chain, 1)
            dve.wait_ge(res_in, 16)
            for s in range(NG):
                for k in range(4):
                    n = 2 if k < 3 else 1
                    dve.wait_ge(back_made, 4 * s + k + 1)
                    here = g.res[:, ds(s * GT + 2 * k, n), :]
                    nc.vector.tensor_tensor(here, bps[k % 2][:, 0:n * C].rearrange("p (t c) -> p t c", c=C),
                                            here, ALU.add).then_inc(back_ready, 1)


def slice_weights(nc, sem, sb, g):
    w = g.w
    wx_t = sb("wx_t", [FD, FH, C], F32)
    w_slice = sb("w_slice", [FD, FG], F32)
    b_x = sb("b_x", [FD, FH], F32)
    b_slice = sb("b_slice", [1, FG], F32)
    temp = sb("temp", [P, FH], F32)
    inv_temp = sb("inv_temp", [P, FH], F32)
    bias = sb("slice_bias", [1, HG], F32)
    loaded = sem("f_loaded")
    chain = sem("f_chain")
    made = sem("f_made")
    stats = sem("f_stats")
    step = sem("f_step")
    m = g.mom

    with nc.Block() as block:
        @block.sync
        def _(sp):
            sp.dma_start(wx_t[:], w["ffn_W_xT"]).then_inc(loaded, 16)
            sp.dma_start(w_slice[:], w["ffn_W_slice"]).then_inc(loaded, 16)
            with nc.allow_non_contiguous_dma(reason="512 elements of bias"):
                sp.dma_start(b_x[:], w["ffn_b_x"].rearrange("(h d) -> d h", h=FH)).then_inc(loaded, 16)
            sp.dma_start(b_slice[:], w["ffn_b_slice"].rearrange("(a n) -> a n", a=1)).then_inc(loaded, 16)
            sp.dma_start(temp[:], w["ffn_temperature"].rearrange("a h b c -> (a b c) h").to_broadcast([P, FH]))\
              .then_inc(loaded, 16)

        @block.tensor
        def _(pe):
            pe.wait_ge(loaded, 80)
            for b in range(CB):
                for h in range(FH):
                    nc.tensor.matmul(g.ps[b][:, ds(h * FG, FG)], wx_t[:, h, ds(b * P, P)], w_slice[:],
                                     start=True, stop=True)
            for h in range(FH):
                mm = nc.tensor.matmul(g.ps[2][0:1, ds(h * FG, FG)], b_x[:, h:h + 1], w_slice[:], start=True, stop=True)
            mm.then_inc(made, 1)

        @block.scalar
        def _(act):
            act.wait_ge(step, MOMENT_STEPS)
            nc.scalar.activation(m.rstd[:], m.rstd[:], ACT.Sqrt).then_inc(step, 1)

        @block.vector
        def _(dve):
            heads = lambda ap: ap.rearrange("p (h n) -> p h n", h=FH)
            wide = lambda ap, n: ap.unsqueeze(2).to_broadcast([n, FH, FG])
            dve.wait_ge(loaded, 80)
            nc.vector.tensor_scalar(temp[:], temp[:], 0.1, 5.0, ALU.max, ALU.min).then_inc(chain, 1)
            dve.wait_ge(chain, 1)
            nc.vector.reciprocal(inv_temp[:], temp[:]).then_inc(chain, 1)
            dve.wait_ge(chain, 2)
            dve.wait_ge(made, 1)
            for b in range(CB):
                nc.vector.tensor_tensor(heads(g.w_logit[:, b, :]), heads(g.ps[b][:]), wide(inv_temp[:], P), ALU.mult)
            nc.vector.tensor_tensor(heads(bias[:]), heads(g.ps[2][0:1, :]),
                                    b_slice[:].unsqueeze(1).to_broadcast([1, FH, FG]), ALU.add).then_inc(chain, 1)
            dve.wait_ge(chain, 3)
            nc.vector.tensor_tensor(heads(bias[:]), heads(bias[:]), wide(inv_temp[0:1, :], 1), ALU.mult).then_inc(chain, 1)
            dve.wait_ge(chain, 4)
            nc.vector.tensor_copy(g.bias_parts[:, 0, :], bias[:]).then_inc(chain, 1)
            dve.wait_ge(chain, 5)
            nc.vector.tensor_tensor(g.bias_parts[:, 1, :], bias[:], g.bias_parts[:, 0, :].bitcast(F32), ALU.subtract)
            with dve.Fori(0, NT) as t:
                nc.vector.bn_stats(m.raw[:, t, :], g.res[:, t, :]).then_inc(stats, 1)
            dve.wait_ge(stats, NT)
            combine_moments(nc, dve, m, 0, NT, step, 0)
            dve.wait_ge(step, MOMENT_STEPS + 1)
            nc.vector.reciprocal(m.rstd[:], m.rstd[:])


def slice_tokens(nc, sem, sb, g):
    x2_ready = sem("h_x2_ready")
    turned = sem("h_turned")
    x2T_ready = sem("h_x2T_ready")
    logit_made = sem("h_logit_made")
    max_ready = sem("h_max_ready")
    shifted = sem("h_shifted")
    exp_ready = sem("h_exp_ready")
    sum_ready = sem("h_sum_ready")
    inv_ready = sem("h_inv_ready")
    w_ready = sem("h_w_ready")
    w_turned = sem("h_w_turned")
    wT_ready = sem("h_wT_ready")
    tok_made = sem("h_tok_made")
    ones_ready = sem("h_ones_ready")
    x2 = [sb(f"x2_{p}", [P, XW], F32) for p in range(2)]
    x2T = [sb(f"x2T_{p}", [P, CB, P], F32) for p in range(2)]
    ex = [sb(f"ex_{p}", [P, HG], F32) for p in range(2)]
    neg_max = [sb(f"neg_max{p}", [P, FH], F32) for p in range(2)]
    tot = [sb(f"tot{p}", [P, FH], F32) for p in range(2)]
    m = g.mom
    tps = g.ps[0]
    lps = g.ps[1]
    wps = [g.ps[2], g.ps[3]]
    acc = g.ps[4:8]
    heads = lambda ap: ap.rearrange("p (h n) -> p h n", h=FH)
    wide = lambda ap: ap.unsqueeze(2).to_broadcast([P, FH, FG])

    def over_tiles(eng, step):
        step(0, 0)
        step(1, 1)
        with eng.Fori(1, NT // 2) as i:
            step(2 * i, 0)
            step(2 * i + 1, 1)
        step(NT - 1, 0)

    with nc.Block() as block:
        @block.tensor
        def _(pe):
            def turn_x(t, p):
                pe.wait_ge(x2_ready, t + 1)
                pe.wait_ge(x2T_ready, t + 1)
                for b in range(CB):
                    mm = nc.tensor.transpose(tps[:, ds(b * P, P)], x2[p][:, ds(b * P, P)], g.ident[:])
                mm.then_inc(turned, 1)

            def logits(t, p):
                pe.wait_ge(x2T_ready, t + 2)
                pe.wait_ge(shifted, t + 1)
                nc.tensor.matmul(lps[:], g.ones2[0:1, :], g.bias_parts[:, 0, :], start=True, stop=False)
                nc.tensor.matmul(lps[:], g.ones2[0:1, :], g.bias_parts[:, 1, :], start=False, stop=False)
                for b in range(CB):
                    mm = nc.tensor.matmul(lps[:], x2T[p][:, b, :], g.w_logit[:, b, :], start=False, stop=b == CB - 1)
                mm.then_inc(logit_made, 1)

            def use(t, p):
                pe.wait_ge(w_ready, t + 1)
                pe.wait_ge(wT_ready, t + 1)
                for q in range(HGB):
                    mm = nc.tensor.transpose(wps[p][:, ds(q * P, P)], ex[p][:, ds(q * P, P)], g.ident[:])
                mm.then_inc(w_turned, 1)
                rows = rows_of(t)
                for q in range(HGB):
                    mm = nc.tensor.matmul(acc[q][:, 0:XW], ex[p][0:rows, ds(q * P, P)], x2[p][0:rows, :],
                                          start=isinstance(t, int) and t == 0, stop=isinstance(t, int) and t == NT - 1)
                mm.then_inc(tok_made, 1)

            def step(t, p):
                turn_x(t, p)
                logits(t, p)
                if not (isinstance(t, int) and t == 0):
                    use(t - 1, 1 - p)

            over_tiles(pe, step)
            use(NT - 1, 0)

        @block.scalar
        def _(act):
            act.sem_inc(x2T_ready, 1)
            act.sem_inc(wT_ready, 2)

            def copy_x(t, p):
                act.wait_ge(turned, t + 1)
                if not (isinstance(t, int) and t < 2):
                    act.wait_ge(logit_made, t - 1)
                nc.scalar.activation(x2T[p][:], tps[:, 0:C].rearrange("p (b n) -> p b n", b=CB),
                                     ACT.Copy).then_inc(x2T_ready, 1)

            def expo(t, p):
                act.wait_ge(shifted, t + 2)
                nc.scalar.activation(ex[p][:], ex[p][:], ACT.Exp).then_inc(exp_ready, 1)

            def copy_w(t, p):
                act.wait_ge(w_turned, t + 1)
                nc.scalar.activation(g.wT[:, :, ds(t * P, P)], wps[p][:].rearrange("p (q n) -> p q n", q=HGB),
                                     ACT.Copy).then_inc(wT_ready, 1)

            def step(t, p):
                copy_x(t, p)
                if not (isinstance(t, int) and t == 0):
                    copy_w(t - 1, 1 - p)
                expo(t, p)

            over_tiles(act, step)
            copy_w(NT - 1, 0)

        @block.vector
        def _(dve):
            for p in range(2):
                nc.vector.memset(x2[p][:, C:C + 1], 1.0)
                nc.vector.memset(x2[p][:, C + 1:XW], 0.0)
            dve.sem_inc(shifted, 1)

            def normalise(t, p):
                if not (isinstance(t, int) and t < 2):
                    dve.wait_ge(tok_made, t - 1)
                nc.vector.tensor_scalar(x2[p][:, 0:C], g.res[:, t, :], m.mean[:, ds(t, 1)], m.rstd[:, ds(t, 1)],
                                        ALU.subtract, ALU.mult).then_inc(x2_ready, 1)

            def softmax(t, p):
                dve.wait_ge(logit_made, t + 1)
                nc.vector.tensor_reduce(neg_max[p][:], heads(lps[:]), X, ALU.max, negate=True).then_inc(max_ready, 1)
                dve.wait_ge(max_ready, t + 1)
                nc.vector.tensor_tensor(heads(ex[p][:]), heads(lps[:]), wide(neg_max[p][:]), ALU.add).then_inc(shifted, 1)
                dve.wait_ge(exp_ready, t + 1)
                nc.vector.tensor_reduce(tot[p][:], heads(ex[p][:]), X, ALU.add).then_inc(sum_ready, 1)
                dve.wait_ge(sum_ready, t + 1)
                nc.vector.reciprocal(tot[p][:], tot[p][:]).then_inc(inv_ready, 1)
                dve.wait_ge(inv_ready, t + 1)
                nc.vector.tensor_tensor(heads(ex[p][:]), heads(ex[p][:]), wide(tot[p][:]), ALU.mult).then_inc(w_ready, 1)

            def step(t, p):
                if not (isinstance(t, int) and t == NT - 1):
                    normalise(t + 1, 1 - p)
                softmax(t, p)

            normalise(0, 0)
            over_tiles(dve, step)


def slice_attention(nc, sem, sb, g):
    w = g.w
    w_fx = sb("w_fx", [P, CB, FH * FD], F32)
    b_fx = sb("b_fx", [1, FH * FD], F32)
    w_q = sb("w_q", [FD, FD], F32)
    w_k = sb("w_k", [FD, FD], F32)
    w_v = sb("w_v", [FD, FD], F32)
    w_out = sb("w_out", [FD, FH, C], F32)
    norm = sb("norm", [P, HGB, 2], F32)
    tok = sb("tok", [P, HGB, XW], F32)
    tokT = sb("tokT", [P, CB, HG], F32)
    share = sb("share", [1, HG], F32)
    fxT = sb("fxT", [FD, HG], F32)
    qT = sb("qT", [FD, HG], F32)
    kT = sb("kT", [FD, HG], F32)
    v = sb("v", [FG, FH * FD], F32)
    at = sb("at", [FG, HG], F32)
    atT = sb("atT", [FG, HG], F32)
    neg = sb("neg", [FG, FH], F32)
    tot = sb("a_tot", [FG, FH], F32)
    oT = sb("oT", [FD, HG], F32)
    loaded = sem("i_loaded")
    vec = sem("i_vec")
    mat = sem("i_mat")
    expo = sem("i_exp")
    acc = g.ps[4:8]
    heads = lambda ap: ap.rearrange("p (h n) -> p h n", h=FH)
    wide = lambda ap: ap.unsqueeze(2).to_broadcast([FG, FH, FG])

    with nc.Block() as block:
        @block.sync
        def _(sp):
            for t, src in ((w_fx, w["ffn_W_fx"].rearrange("(b p) n -> p b n", p=P)),
                           (b_fx, w["ffn_b_fx"].rearrange("(a n) -> a n", a=1)),
                           (w_q, w["ffn_W_q"]), (w_k, w["ffn_W_k"]), (w_v, w["ffn_W_v"]),
                           (w_out, w["ffn_W_out"].rearrange("(h d) n -> d h n", h=FH))):
                sp.dma_start(t[:], src).then_inc(loaded, 16)

        @block.vector
        def _(dve):
            V = nc.vector
            for q in range(HGB):
                V.tensor_scalar(norm[:, q, 0:1], acc[q][:, C:C + 1], EPS, None, ALU.add).then_inc(vec, 1)
            dve.wait_ge(vec, 4)
            V.reciprocal(norm[:, :, 1], norm[:, :, 0]).then_inc(vec, 1)
            dve.wait_ge(vec, 5)
            for q in range(HGB):
                V.tensor_scalar(tok[:, q, :], acc[q][:, 0:XW], norm[:, q, 1:2], None, ALU.mult).then_inc(vec, 1)
            dve.wait_ge(mat, 1)
            for b in range(CB):
                V.tensor_copy(tokT[:, b, :], g.ps[b][:]).then_inc(vec, 1)
            V.tensor_copy(share[:], g.ps[2][0:1, :]).then_inc(vec, 1)
            dve.wait_ge(mat, 2)
            V.tensor_copy(fxT[:], g.ps[3][0:FD, :]).then_inc(vec, 1)
            dve.wait_ge(mat, 3)
            V.tensor_copy(qT[:], g.ps[4][0:FD, :]).then_inc(vec, 1)
            V.tensor_copy(kT[:], g.ps[5][0:FD, :]).then_inc(vec, 1)
            V.tensor_copy(v[:], g.ps[6][0:FG, :]).then_inc(vec, 1)
            dve.wait_ge(mat, 4)
            V.tensor_reduce(neg[:], heads(g.ps[7][0:FG, :]), X, ALU.max, negate=True).then_inc(vec, 1)
            dve.wait_ge(vec, 17)
            V.tensor_tensor(heads(at[:]), heads(g.ps[7][0:FG, :]), wide(neg[:]), ALU.add).then_inc(vec, 1)
            dve.wait_ge(expo, 1)
            V.tensor_reduce(tot[:], heads(at[:]), X, ALU.add).then_inc(vec, 1)
            dve.wait_ge(vec, 19)
            V.reciprocal(tot[:], tot[:]).then_inc(vec, 1)
            dve.wait_ge(vec, 20)
            V.tensor_tensor(heads(at[:]), heads(at[:]), wide(tot[:]), ALU.mult).then_inc(vec, 1)
            dve.wait_ge(mat, 5)
            V.tensor_copy(atT[:], g.ps[0][0:FG, :]).then_inc(vec, 1)
            dve.wait_ge(mat, 6)
            V.tensor_copy(oT[:], g.ps[1][0:FD, :]).then_inc(vec, 1)
            dve.wait_ge(mat, 7)
            for q in range(HGB):
                V.tensor_copy(g.m_out[:, q, :], g.ps[2 + q][:, 0:C])

        @block.scalar
        def _(act):
            act.wait_ge(vec, 18)
            nc.scalar.activation(at[:], at[:], ACT.Exp, scale=float(FD) ** -0.5).then_inc(expo, 1)

        @block.tensor
        def _(pe):
            T = nc.tensor
            for q in range(HGB):
                pe.wait_ge(vec, 5 + q + 1)
                for b in range(CB):
                    T.transpose(g.ps[b][:, ds(q * P, P)], tok[:, q, ds(b * P, P)], g.ident[:])
                mm = T.transpose(g.ps[2][0:1, ds(q * P, P)], tok[:, q, C:C + 1], g.ident[:])
            mm.then_inc(mat, 1)
            pe.wait_ge(loaded, 96)
            pe.wait_ge(vec, 12)
            for h in range(FH):
                out = g.ps[3][0:FD, ds(h * FG, FG)]
                for b in range(CB):
                    T.matmul(out, w_fx[:, b, ds(h * FD, FD)], tokT[:, b, ds(h * FG, FG)], start=b == 0, stop=False)
                mm = T.matmul(out, b_fx[:, ds(h * FD, FD)], share[:, ds(h * FG, FG)], start=False, stop=True)
            mm.then_inc(mat, 1)
            pe.wait_ge(vec, 13)
            T.matmul(g.ps[4][0:FD, :], w_q[:], fxT[:], start=True, stop=True)
            T.matmul(g.ps[5][0:FD, :], w_k[:], fxT[:], start=True, stop=True)
            for h in range(FH):
                mm = T.matmul(g.ps[6][0:FG, ds(h * FD, FD)], fxT[:, ds(h * FG, FG)], w_v[:], start=True, stop=True)
            mm.then_inc(mat, 1)
            pe.wait_ge(vec, 16)
            for h in range(FH):
                mm = T.matmul(g.ps[7][0:FG, ds(h * FG, FG)], qT[:, ds(h * FG, FG)], kT[:, ds(h * FG, FG)],
                              start=True, stop=True)
            mm.then_inc(mat, 1)
            pe.wait_ge(vec, 21)
            for h in range(FH):
                mm = T.transpose(g.ps[0][0:FG, ds(h * FG, FG)], at[:, ds(h * FG, FG)], g.ident[0:FG, 0:FG])
            mm.then_inc(mat, 1)
            pe.wait_ge(vec, 22)
            for h in range(FH):
                mm = T.matmul(g.ps[1][0:FD, ds(h * FG, FG)], v[:, ds(h * FD, FD)], atT[:, ds(h * FG, FG)],
                              start=True, stop=True)
            mm.then_inc(mat, 1)
            pe.wait_ge(vec, 23)
            for h in range(FH):
                mm = T.matmul(g.ps[2 + h // 2][ds(h % 2 * FG, FG), 0:C], oT[:, ds(h * FG, FG)], w_out[:, h, :],
                              start=True, stop=True)
            mm.then_inc(mat, 1)


def slice_output(nc, sem, sb, g):
    made = sem("j_made")
    ready = sem("j_ready")
    stored = [sem(f"j_stored{p}") for p in range(2)]
    y = [sb(f"y{p}", [P, GT, C], F32) for p in range(2)]
    yps = g.ps[0:4]

    with nc.Block() as block:
        @block.tensor
        def _(pe):
            for u in range(NT):
                if u % 2 == 0 and u >= 8:
                    pe.wait_ge(ready, u // 2 - 3)
                out = yps[u // 2 % 4][:, ds(u % 2 * C, C)]
                nc.tensor.matmul(out, g.ones2[:], g.b_out[:], start=True, stop=False)
                for q in range(HGB):
                    mm = nc.tensor.matmul(out, g.wT[:, q, ds(u * P, P)], g.m_out[:, q, :], start=False, stop=q == HGB - 1)
                if u % 2 or u == NT - 1:
                    mm.then_inc(made, 1)

        @block.vector
        def _(dve):
            for k in range(-(-NT // 2)):
                n = min(2, NT - 2 * k)
                dve.wait_ge(made, k + 1)
                here = g.res[:, ds(2 * k, n), :]
                nc.vector.tensor_tensor(here, yps[k % 4][:, 0:n * C].rearrange("p (t c) -> p t c", c=C), here,
                                        ALU.add).then_inc(ready, 1)

        @block.sync
        def _(sp):
            done = 0
            whole = NT - 1
            for t0 in range(0, whole, 8):
                sp.wait_ge(ready, t0 // 2 + 4)
                sp.dma_start(split_rows(g.out_dram, t0, 8), g.res[:, t0:t0 + 8, :]).then_inc(stored[0], 16)
                done += 16
            sp.wait_ge(ready, -(-NT // 2))
            sp.dma_start(g.out_dram[whole * P:NODES, :], g.res[0:TAIL, whole, :]).then_inc(stored[1], 16)
            sp.wait_ge(stored[0], done)
            sp.wait_ge(stored[1], 16)


def gps_layer(nc, w, x, attr_T, src_rows, src_cols, dst_cols, out):
    with ExitStack() as ctx:
        def sem(name):
            return ctx.enter_context(nc.semaphore(name))

        def sb(name, shape, dt):
            return ctx.enter_context(nc.sbuf_tensor(name, shape, dt))

        def scoped(stage, *args):
            with ExitStack() as inner:
                stage(nc, sem, lambda *a: inner.enter_context(nc.sbuf_tensor(*a)), *args)

        g = Shared()
        g.w, g.x_dram, g.attr_T, g.out_dram = w, x, attr_T, out
        g.src_rows, g.src_cols, g.dst_cols = src_rows, src_cols, dst_cols
        g.xn_dram = nc.dram_tensor("xn_rows", [NPAD, C], F32).ap()
        g.res_dram = nc.dram_tensor("res_rows", [NPAD, C], F32).ap()
        g.sums_dram = [nc.dram_tensor(f"sums{k}", [ROWS, C], F32).ap() for k in range(TABLES)]
        g.ps = [ctx.enter_context(nc.psum_tensor(f"bank{b}", [P, 512], F32)) for b in range(8)]
        g.ident = sb("ident", [P, P], F32)
        g.earlier = sb("earlier", [P, P], F32)
        g.trash_i = sb("trash_i", [P, 1], I32)
        g.mom = Moments(sb, "mom")
        g.ones2 = sb("ones2", [BIAS_ROWS, P], F32R)
        g.biases = []
        g.bf2, g.bproj, g.b_out = (bias_row(sb, g, name) for name in ("gnn_bf2", "mix_bproj", "ffn_b_out"))
        with ExitStack() as mixing:
            sb_mix = lambda *a: mixing.enter_context(nc.sbuf_tensor(*a))
            g.weights = mixing_weights(sb_mix, g)
            g.zeros = sb_mix("zeros", [P, 1600], F32)
            g.tables_clear = sem("tables_clear")
            g.clear_count = 16 * TABLES * (ROWS // P * C // g.zeros.shape[1])
            scoped(first_layernorm, g)
            g.xT = sb_mix("xT", [P, CB, NPAD], F32)
            g.k_max = sb_mix("k_max", [P, CB, 2 * NG], F32)
            g.neg_k_max = sb_mix("neg_k_max", [P, CB], F32)
            g.k_sum = sb_mix("k_sum", [P, CB, 2 * NG], F32)
            g.k_tot = sb_mix("k_tot", [P, CB], F32)
            g.k_inv = sb_mix("k_inv", [P, CB], F32)
            g.bg1f = sb_mix("bg1f", [GH, 1], F32)
            g.wg1f = sb_mix("wg1f", [P, CB, GH], F32)
            g.head_mask = sb_mix("head_mask", [P, P], F32)
            g.wqm = sb_mix("wqm", [P, CB, C], F32)
            scoped(messages_and_attention, g)
        g.res = sb("res", [P, NT, C], F32)
        scoped(update_nodes, g)
        with ExitStack() as late:
            sb_late = lambda *a: late.enter_context(nc.sbuf_tensor(*a))
            g.w_logit = sb_late("w_logit", [P, CB, HG], F32)
            g.bias_parts = sb_late("bias_parts", [1, 2, HG], F32R)
            g.m_out = sb_late("m_out", [P, HGB, C], F32)
            g.wT = sb_late("wT", [P, HGB, NPAD], F32)
            scoped(slice_weights, g)
            scoped(slice_tokens, g)
            scoped(slice_attention, g)
            scoped(slice_output, g)


def kernel(**inputs):
    import numpy as np
    from concourse import bacc
    from concourse.bass_utils import run_bass_kernel_spmd

    a = {k: np.asarray(v) for k, v in inputs.items()}
    attr_T = np.zeros((EF, EPAD), np.float32)
    attr_T[:, :EDGES] = a["edge_attr_20"].T
    src = np.full((EPAD,), PAD_SRC, np.int32)
    src[:EDGES] = a["src"]
    dst = np.zeros((EPAD,), np.int32)
    dst[:EDGES] = a["dst"]
    arrays = {
        "x": a["x"], "attr_T": attr_T, "src_rows": src.reshape(NCH, EC),
        "src_cols": np.ascontiguousarray(src.reshape(-1, P).T),
        "dst_cols": np.ascontiguousarray(dst.reshape(-1, P).T),
    }
    weights = {k[3:]: v for k, v in a.items() if k.startswith("L0_")}
    weights["mix_WqT"] = np.ascontiguousarray(weights["mix_Wqkv"][:, :C].T)
    weights["ffn_W_xT"] = np.ascontiguousarray(weights.pop("ffn_W_x").reshape(C, FH, FD).transpose(2, 1, 0))

    nc = bacc.Bacc("TRN2", target_bir_lowering=False, num_devices=1)
    declare = lambda name, v: nc.dram_tensor(name, v.shape, mybir.dt.from_np(v.dtype), kind="ExternalInput").ap()
    io = {k: declare(k, v) for k, v in arrays.items()}
    w = {k: declare("w_" + k, v) for k, v in weights.items()}
    arrays.update({"w_" + k: v for k, v in weights.items()})
    out = nc.dram_tensor("out", (NODES, C), F32, kind="ExternalOutput").ap()
    gps_layer(nc, w, out=out, **io)
    r = run_bass_kernel_spmd(nc, [arrays], core_ids=[0])
    return r.results[0]["out"]
```

```python
from contextlib import ExitStack

import concourse.bass as bass
from concourse import mybir
from concourse.alu_op_type import AluOpType as ALU

F32 = mybir.dt.float32
F32R = mybir.dt.float32r
I32 = mybir.dt.int32
ACT = mybir.ActivationFunctionType
X = mybir.AxisListType.X
ds = bass.ds

P = 128
NODES, C = 6250, 256
CB = C // P
NT = -(-NODES // P)
TAIL = NODES - (NT - 1) * P
NPAD = NT * P
GT = 7
NG = NT // GT
GC = GT * P
HC = GC // 2
EDGES, EF = 100000, 20
ET = 8
EC = ET * P
NCH = 2 * -(-EDGES // (2 * EC))
EPAD = NCH * EC
TRASH = NODES
PAD_SRC = NODES + P
ROWS = -(-(PAD_SRC + 1) // P) * P
CLEARS = 8
TABLES = 2
WINDOWED = 2
NW = NCH * WINDOWED
MH, MD = 8, 32
GH = C // 4
FH, FD, FG = 8, 64, 64
HG = FH * FG
HGB = HG // P
EPS = 1e-5
BIAS_ROWS = 33
XW = C + 2


def tail_cols(s, h):
    return max(0, min(HC, NODES - (NG - 1) * GC - h * HC))


def rows_of(t):
    return TAIL if is_known(t, NT - 1) else P


def split_rows(dram, t0, n):
    return dram[ds(t0 * P, n * P), :].rearrange("(t p) c -> p t c", p=P)


class Shared:
    pass


class Moments:

    def __init__(self, sb, name):
        self.raw = sb(name + "_raw", [P, NT, 6], F32)
        self.mean = sb(name + "_mean", [P, NT], F32)
        self.rstd = sb(name + "_rstd", [P, NT], F32)
        self.tmp = sb(name + "_tmp", [P, 3, NT], F32)


def combine_moments(nc, dve, m, t0, n, step, base):
    half = lambda k: m.raw[:, ds(t0, n), k]
    cut = lambda b: b[:, ds(t0, n)]
    s, d, q = (m.tmp[:, k, ds(t0, n)] for k in range(3))
    nc.vector.tensor_tensor(s, half(1), half(4), ALU.add).then_inc(step, 1)
    nc.vector.tensor_tensor(d, half(1), half(4), ALU.subtract).then_inc(step, 1)
    nc.vector.tensor_tensor(q, half(2), half(5), ALU.add).then_inc(step, 1)
    dve.wait_ge(step, base + 3)
    nc.vector.tensor_scalar(cut(m.mean), s, 0.5, None, ALU.mult).then_inc(step, 1)
    nc.vector.scalar_tensor_tensor(out=d, in0=d, scalar=0.25, in1=d, op0=ALU.mult,
                                   op1=ALU.mult).then_inc(step, 1)
    nc.vector.tensor_scalar(q, q, 1.0 / C, EPS, ALU.mult, ALU.add).then_inc(step, 1)
    dve.wait_ge(step, base + 6)
    nc.vector.tensor_tensor(cut(m.rstd), q, d, ALU.add).then_inc(step, 1)


MOMENT_STEPS = 7


def clear_table(eng, g, k):
    flat = g.sums_dram[k].rearrange("(p r) c -> p (r c)", p=P)
    width = g.zeros.shape[1]
    for n in range(CLEARS):
        eng.dma_start(flat[:, n * width:(n + 1) * width], g.zeros).then_inc(g.table_clear[k], 16)


def first_layernorm(nc, sem, sb, g):
    parts = [(12 * k, 12) for k in range(4)] + [(NT - 1, 1)]
    x = sb("x_rows_a", [P, NT, C], F32)
    xn = sb("xn_a", [P, NT, C], F32)
    ones_f = sb("ones_f", [BIAS_ROWS, P], F32)
    x_in = [sem(f"x_in{k}") for k in range(len(parts))]
    tail_clear = sem("a_tail_clear")
    stats = sem("a_stats")
    step = sem("a_step")
    var_ready = sem("a_var_ready")
    std_ready = sem("a_std_ready")
    rstd_ready = sem("a_rstd_ready")
    xn_ready = sem("a_xn_ready")
    xn_out = sem("a_xn_out")
    zero_ready = sem("a_zero_ready")
    filled = sem("a_filled")
    ones_filled = sem("a_ones_filled")
    weights_in = sem("a_weights_in")
    bias_clear = sem("a_bias_clear")
    bias_in = sem("a_bias_in")
    halved = sem("a_halved")
    m = g.mom
    last = len(parts) - 1

    with nc.Block() as block:
        @block.sync
        def _(sp):
            for k, (t0, n) in enumerate(parts[:-1]):
                sp.dma_start(x[:, t0:t0 + n, :], split_rows(g.x_dram, t0, n)).then_inc(x_in[k], 16)
            sp.wait_ge(tail_clear, 1)
            sp.dma_start(x[0:TAIL, NT - 1, :], g.x_dram[(NT - 1) * P:NODES, :]).then_inc(x_in[last], 16)
            for k, (t0, n) in enumerate(parts):
                sp.wait_ge(xn_ready, t0 + n)
                sp.dma_start(split_rows(g.xn_dram, t0, n), xn[:, t0:t0 + n, :]).then_inc(xn_out, 16)
            sp.wait_ge(xn_out, 16 * len(parts))

        @block.gpsimd
        def _(pool):
            nc.gpsimd.memset(g.zeros, 0.0).then_inc(zero_ready, 1)
            nc.gpsimd.memset(g.ident[:], 0.0).then_inc(filled, 1)
            nc.gpsimd.memset(g.earlier[:], 1.0).then_inc(filled, 1)
            pool.wait_ge(filled, 2)
            nc.gpsimd.affine_select(out=g.ident[:], in_=g.ident[:], compare_op=ALU.not_equal, fill=1.0,
                                    base=0, pattern=[[-1, P]], channel_multiplier=1)
            nc.gpsimd.affine_select(out=g.earlier[:], in_=g.earlier[:], compare_op=ALU.is_gt, fill=0.0,
                                    base=0, pattern=[[-1, P]], channel_multiplier=1)
            nc.gpsimd.iota(g.trash_i[:], pattern=[[0, 1]], base=TRASH, channel_multiplier=1)

        @block.scalar
        def _(act):
            with nc.allow_non_contiguous_dma(reason="bias columns: a few hundred elements"):
                for t, src in g.weights:
                    act.dma_start(t[:], src).then_inc(weights_in, 16)
            act.wait_ge(bias_clear, len(g.biases))
            for whole, _, row in g.biases:
                for k in (0, BIAS_ROWS - 1):
                    act.dma_start(whole[k:k + 1, :], row).then_inc(bias_in, 16)
            act.wait_ge(zero_ready, 1)
            clear_table(act, g, 0)
            for k in range(len(parts)):
                t0, n = parts[k]
                act.wait_ge(var_ready, k + 1)
                nc.scalar.activation(m.rstd[:, t0:t0 + n], m.rstd[:, t0:t0 + n], ACT.Sqrt).then_inc(std_ready, 1)
            act.wait_ge(weights_in, 16 * len(g.weights))

        @block.vector
        def _(dve):
            nc.vector.memset(x[:, NT - 1, :], 0.0).then_inc(tail_clear, 1)
            for whole, _, _ in g.biases:
                nc.vector.memset(whole[:], 0.0).then_inc(bias_clear, 1)
            nc.vector.memset(ones_f[:], 1.0).then_inc(ones_filled, 1)
            dve.wait_ge(ones_filled, 1)
            nc.vector.tensor_copy(g.ones2[:], ones_f[:])

            def gather_stats(k):
                t0, n = parts[k]
                dve.wait_ge(x_in[k], 16)
                for t in range(t0, t0 + n):
                    nc.vector.bn_stats(m.raw[:, t, :], x[:, t, :]).then_inc(stats, 1)
                dve.wait_ge(stats, t0 + n)
                combine_moments(nc, dve, m, t0, n, step, MOMENT_STEPS * k)
                dve.wait_ge(step, MOMENT_STEPS * (k + 1))
                dve.sem_inc(var_ready, 1)

            def normalise(k):
                t0, n = parts[k]
                dve.wait_ge(std_ready, k + 1)
                nc.vector.reciprocal(m.rstd[:, t0:t0 + n], m.rstd[:, t0:t0 + n]).then_inc(rstd_ready, 1)
                dve.wait_ge(rstd_ready, k + 1)
                for t in range(t0, t0 + n):
                    nc.vector.tensor_scalar(xn[:, t, :], x[:, t, :], m.mean[:, t:t + 1],
                                            m.rstd[:, t:t + 1], ALU.subtract, ALU.mult).then_inc(xn_ready, 1)

            for k in range(len(parts)):
                gather_stats(k)
                if k:
                    normalise(k - 1)
            normalise(last)
            dve.wait_ge(bias_in, 32 * len(g.biases))
            for k, (whole, halves, _) in enumerate(g.biases):
                low = slice(BIAS_ROWS - 1, BIAS_ROWS)
                nc.vector.tensor_copy(halves[:], whole[:]).then_inc(halved, 1)
                dve.wait_ge(halved, k + 1)
                nc.vector.tensor_tensor(halves[low, :], whole[low, :], halves[low, :].bitcast(F32), ALU.subtract)


def in_blocks(a):
    return a.rearrange("(b p) n -> p b n", p=P)


def as_columns(a):
    return a.rearrange("(b p) -> p b", p=P)


def as_row(a):
    return a.rearrange("(a n) -> a n", a=1)


def mixing_weights(sb, g):
    w = g.w
    g.wqkv = sb("wqkv", [P, CB, 3 * C], F32)
    g.wq_t = sb("wq_t", [P, CB, C], F32)
    g.wproj = sb("wproj", [P, CB, C], F32)
    g.wg1 = sb("wg1", [P, CB, GH], F32)
    g.wg2 = sb("wg2", [GH, C], F32)
    g.ln_g = sb("ln_g", [P, CB], F32)
    g.ln_b = sb("ln_b", [P, CB], F32)
    g.bg1 = sb("bg1", [GH, 1], F32)
    g.bg2 = sb("bg2", [P, CB], F32)
    g.wf2 = sb("wf2", [P, CB, C], F32)
    g.bf1 = sb("bf1", [P, CB], F32)
    return [
        (g.wqkv, in_blocks(w["mix_Wqkv"])), (g.wq_t, in_blocks(w["mix_WqT"])), (g.wproj, in_blocks(w["mix_Wproj"])),
        (g.wg1, in_blocks(w["mix_Wg1"])), (g.wg2, w["mix_Wg2"]), (g.ln_g, as_columns(w["mix_ln_g"])),
        (g.ln_b, as_columns(w["mix_ln_b"])), (g.bg1, w["mix_bg1"].rearrange("(p a) -> p a", a=1)),
        (g.bg2, as_columns(w["mix_bg2"])), (g.wf2, in_blocks(w["gnn_Wf2"])), (g.bf1, as_columns(w["gnn_bf1"]))]


def update_weights(sb, g):
    w = g.w
    g.wu1 = sb("wu1", [P, CB, C], F32)
    g.wu2 = sb("wu2", [P, CB, C], F32)
    g.bu1 = sb("bu1", [P, CB], F32)
    g.bu2 = sb("bu2", [P, CB], F32)
    g.gamma = sb("gamma", [P, CB], F32)
    g.beta = sb("beta", [P, CB], F32)
    return [
        (g.wu1, in_blocks(w["gnn_Wu1"])), (g.bu1, as_columns(w["gnn_bu1"])), (g.wu2, in_blocks(w["gnn_Wu2"])),
        (g.bu2, as_columns(w["gnn_bu2"])), (g.gamma, as_columns(w["gnn_gamma"])), (g.beta, as_columns(w["gnn_beta"]))]


def bias_row(sb, g, name):
    whole = sb(name + "_row", [BIAS_ROWS, C], F32)
    halves = sb(name + "_halves", [BIAS_ROWS, C], F32R)
    g.biases.append((whole, halves, as_row(g.w[name])))
    return halves


T_SCORES, K_SCORES = 0, 0
K_FOLD = K_SCORES + 4 * NG
T_GRAM, K_GRAM = T_SCORES + 4 * NG, K_FOLD + 1
T_CTX, K_CTX = T_GRAM + NT, K_GRAM + 4 * NG
T_OUT, K_OUT = T_CTX + 1, K_CTX + 1
T_OUT_PER, K_OUT_PER = 8, 10
SLOTS = 16
EXP_SLOTS = (1, 2, 5, 6)
GRAM_SLOT = 7
PASS_CHUNKS = (4, 4, 6)
PASS_START = (0, 2 * NG, 4 * NG)
assert 7 * NG == NCH // 2


def is_first(v):
    return isinstance(v, int) and v == 0


def is_known(v, value):
    return isinstance(v, int) and v == value


def pair_tiles(k):
    return range(2 * k, min(2 * k + 2, GT))


def messages_and_attention(nc, sem, sb, g):
    HE = EC // 2
    PAIRS = ET // 2
    PER = ET // TABLES
    SPAN = 2 * 32 + EF
    attr = sb("attr", [SPAN, 2, HE], F32)
    attr_parts = sb("attr_parts", [SPAN, 2, HE], F32R)
    wf1_raw = sb("wf1_raw", [SPAN, C], F32)
    wf1_parts = sb("wf1_parts", [SPAN, C], F32R)
    src_row = sb("src_row", [P, 2, EC], I32)
    src_f = sb("src_f", [P, NCH * ET], F32)
    to_trash = sb("to_trash", [P, NCH * ET], F32)
    trash_f = sb("trash_f", [P, 1], F32)
    dst_all = sb("dst_all", [P, NCH * ET], I32)
    dst_idx = [sb(f"dst_idx{p}", [P, ET - WINDOWED], I32) for p in range(2)]
    late_idx = [sb(f"late_idx{p}", [P, WINDOWED], I32) for p in range(2)]
    dst_row = sb("dst_row", [P, WINDOWED * P], I32)
    window = sb("window", [P, WINDOWED, C], F32)
    spread = sb("spread", [P, WINDOWED, P], F32)
    window_row = sb("window_row", [P, NW], F32)
    base_i = sb("base_i", [1, NW], I32)
    wide_i = sb("wide_i", [1, 1], I32)
    out_idx = [sb(f"out_idx{p}", [P, ET], I32) for p in range(2)]
    hidT = sb("hidT", [P, 2, CB, HE], F32)
    gathered = [sb(f"gathered{p}", [P, ET, C], F32) for p in range(2)]
    msg = sb("msg", [P, 2, 2, C], F32)
    msg_high = sb("msg_high", [P, 2, 2, C], F32R)
    msg_low = sb("msg_low", [P, 2, 2, C], F32R)
    same = sb("same", [P, 2, ET, P], F32R)
    rank = sb("rank", [P, ET], F32)
    rank_scr = sb("rank_scr", [P, ET, P], mybir.dt.bfloat16)
    redirect = sb("redirect", [P, ET], F32)
    summed = [sb(f"summed{p}", [P, ET, C], F32) for p in range(2)]
    src_i = summed[0][:].rearrange("p t c -> p (t c)")[:, 0:NCH * ET].bitcast(I32)
    dst_w = gathered[1][:].rearrange("p t c -> p (t c)")[:, 0:NW]
    extremes = sb("extremes", [NCH, 2, WINDOWED], F32)
    ends_all = gathered[1][:].rearrange("p t c -> p (t c)")[:, NW:3 * NW].rearrange("p (k n) -> p k n", k=2)
    hps = [g.ps[0], g.ps[1]]
    fps = [g.ps[2], g.ps[3]]
    sps = g.ps[4]

    cols_in = sem("e_cols_in")
    cols_ready = sem("e_cols_ready")
    cleared = sem("e_cleared")
    wf1_in = sem("e_wf1_in")
    wf1_ready = sem("e_wf1_ready")
    attr_in = [sem(f"e_attr_in{h}") for h in range(2)]
    attr_rounded = sem("e_attr_rounded")
    attr_ready = sem("e_attr_ready")
    row_in = [sem(f"e_row_in{p}") for p in range(2)]
    hid_made = sem("e_hid_made")
    hid_ready = sem("e_hid_ready")
    filt_made = sem("e_filt_made")
    idx_ready = sem("e_idx_ready")
    rows_in = [[sem(f"e_rows_in{p}{h}") for h in range(2)] for p in range(2)]
    WIN_ENDS, WIN_DONE = 5, 9
    widest = sb("widest", [1, 1], F32)
    late_in = sem("e_late_in")
    late_ready = sem("e_late_ready")
    window_in = sem("e_window_in")
    dst_row_in = sem("e_dst_row_in")
    spread_ready = sem("e_spread_ready")
    spread_made = sem("e_spread_made")
    spread_out = sem("e_spread_out")
    high_ready = sem("e_high_ready")
    low_ready = sem("e_low_ready")
    win_turned = sem("e_win_turned")
    win_step = sem("e_win_step")
    ends_out = sem("e_ends_out")
    ends_in = sem("e_ends_in")
    msg_ready = sem("e_msg_ready")
    same_ready = sem("e_same_ready")
    redirected = sem("e_redirected")
    out_ready = sem("e_out_ready")
    sum_made = sem("e_sum_made")
    sum_ready = sem("e_sum_ready")
    added = [sem(f"e_added{k}") for k in range(TABLES)]
    passed = sem("e_passed")

    xn = sb("xn_stage", [P, GT, C], F32)
    res = sb("res_stage", [P, GT, C], F32)
    turnedT = sb("turnedT", [P, CB, GC], F32)
    ctx_m = sb("ctx_m", [P, CB, P], F32)
    xhat = sb("xhat", [P, 2, 2, C], F32)
    e_node, gramT = xhat[:, 0, :, :], xhat[:, 1, :, :]
    hid = sb("hid", [GH, GC], F32)
    gate = g.gate
    bankT, bankK, bankG = g.ps[5], g.ps[6], g.ps[7]
    m = g.mom

    stage_in = sem("m_stage_in")
    t_made, t_free = sem("m_t_made"), sem("m_t_free")
    k_made, k_free = sem("m_k_made"), sem("m_k_free")
    stats = sem("m_stats")
    step = sem("m_step")
    var_ready = sem("m_var_ready")
    std_ready = sem("m_std_ready")
    rstd_ready = sem("m_rstd_ready")
    maxed = sem("m_maxed")
    folded = sem("m_folded")
    node_ready = sem("m_node_ready")
    gram_made = sem("m_gram_made")
    stage = sem("m_stage")
    x_in = sem("m_x_in")
    xhat_ready = sem("m_xhat_ready")
    presum_ready = sem("m_presum_ready")
    res_ready = sem("m_res_ready")
    res_out = sem("m_res_out")

    def along(eng, chunk, scores=None, gram=None, output=None):
        def group(k, s, share):
            places = 4 * PASS_CHUNKS[k]

            def step(place):
                for slot in range(-(-SLOTS * place // places), -(-SLOTS * (place + 1) // places)):
                    share(s, slot)

            for n in range(PASS_CHUNKS[k]):
                i = PASS_START[k] + PASS_CHUNKS[k] // 2 * s + n // 2
                chunk(i, n % 2, is_known(i, NCH // 2 - 1) and n % 2 == 1,
                      (lambda q: step(4 * n + q)) if share else (lambda q: None))

        def groups(k, share):
            group(k, 0, share)
            with eng.Fori(1, NG - 1) as s:
                group(k, s, share)
            group(k, NG - 1, share)

        groups(0, scores)
        groups(1, gram)
        groups(2, output)

    with nc.Block() as block:
        @block.sync
        def _(sp):
            def load_stage(s):
                sp.dma_start(xn[:], split_rows(g.xn_dram, s * GT, GT)).then_inc(stage_in, 16)

            def load_window(c):
                if not is_first(c):
                    sp.wait_ge(spread_ready, c)
                sp.dma_start(dst_row[:], g.dst_late[ds(c, 1), :].to_broadcast([P, WINDOWED * P]))\
                  .then_inc(dst_row_in, 16)
                if is_first(c):
                    sp.wait_ge(win_step, WIN_DONE)
                else:
                    sp.wait_ge(spread_made, c)
                for k in range(WINDOWED):
                    base = sp.value_load(base_i[0:1, ds(WINDOWED * c + k, 1)], min_val=0, max_val=NPAD - P)
                    sp.dma_start(window[:, k, :], g.xn_dram[ds(base, P), :]).then_inc(window_in, 16)

            def chunk(i, p, last, work):
                c = 2 * i + p
                if not is_first(i):
                    sp.wait_ge(same_ready, PAIRS * (c - 1))
                sp.dma_start(src_row[:, p, :],
                             g.src_rows[ds(c, 1), :].to_broadcast([P, EC])).then_inc(row_in[p], 16)
                for h in range(2):
                    if not is_first(c):
                        sp.wait_ge(attr_ready, 2 * (c - 1) + h + 1)
                    for copy in range(3):
                        sp.dma_start(attr[32 * copy:32 * copy + EF, h, :],
                                     g.attr_T[:, ds(c * EC + h * HE, HE)]).then_inc(attr_in[h], 16)
                load_window(c)
                for q in range(PAIRS):
                    work(q)

            def scores(s, slot):
                if slot == 12 and not is_known(s, NG - 1):
                    sp.wait_ge(t_made, T_SCORES + 4 * s + 4)
                    sp.wait_ge(stats, GT * s + GT)
                    load_stage(s + 1)

            def gram(s, slot):
                if slot == 0:
                    if is_first(s):
                        sp.wait_ge(t_made, T_SCORES + 4 * NG)
                        sp.wait_ge(stats, NT)
                    else:
                        sp.wait_ge(gram_made, 1 + GT * s)
                    load_stage(s)

            def store_res(s):
                sp.wait_ge(res_ready, 4 * s + 4)
                sp.dma_start(split_rows(g.res_dram, s * GT, GT), res[:]).then_inc(res_out, 16)

            def load_x(s):
                if not is_first(s):
                    sp.wait_ge(res_out, 16 * s)
                if is_known(s, NG - 1):
                    sp.dma_start(res[:, 0:GT - 1, :], split_rows(g.x_dram, s * GT, GT - 1)).then_inc(x_in, 16)
                    sp.dma_start(res[0:TAIL, GT - 1, :], g.x_dram[(NT - 1) * P:NODES, :]).then_inc(x_in, 16)
                else:
                    sp.dma_start(res[:], split_rows(g.x_dram, s * GT, GT)).then_inc(x_in, 16)

            def output(s, slot):
                if slot == 0 and is_first(s):
                    sp.wait_ge(gram_made, 1 + NT)
                    load_stage(0)
                if slot == 4:
                    if not is_first(s):
                        store_res(s - 1)
                    load_x(s)
                if slot == 12 and not is_known(s, NG - 1):
                    sp.wait_ge(presum_ready, 4 * s + 4)
                    load_stage(s + 1)

            sp.dma_start(src_i, g.src_cols).then_inc(cols_in, 16)
            sp.dma_start(dst_all[:], g.dst_cols).then_inc(cols_in, 16)
            sp.wait_ge(cleared, 2)
            for copy in range(3):
                sp.dma_start(wf1_raw[32 * copy:32 * copy + EF, :], g.w["gnn_Wf1"]).then_inc(wf1_in, 16)
            load_stage(0)
            along(sp, chunk, scores, gram, output)
            store_res(NG - 1)
            sp.wait_ge(res_out, 16 * NG)

        @block.gpsimd
        def _(pool):
            def gather(c, p, t):
                if t == 0:
                    pool.wait_ge(idx_ready, c + 1)
                if not (isinstance(c, int) and c < 2):
                    pool.wait_ge(msg_ready, PAIRS * (c - 2) + t // 2 + 1)
                pool.sem_inc(passed, 1)
                nc.gpsimd.indirect_dma_start(
                    gathered[p][:, t, :], None, g.xn_dram,
                    bass.IndirectOffsetOnAxis(ap=dst_idx[p][:, t:t + 1], axis=0)).then_inc(rows_in[p][t // PAIRS], 16)

            def late_rows(i, p, narrow):
                c = 2 * i + p
                pool.wait_ge(spread_out, c + 1)
                if narrow:
                    pool.sem_inc(late_in, 16 * WINDOWED)
                    return
                pool.wait_ge(late_ready, c + 1)
                pool.sem_inc(passed, 1)
                for k in range(WINDOWED):
                    nc.gpsimd.indirect_dma_start(
                        gathered[p][:, ET - WINDOWED + k, :], None, g.xn_dram,
                        bass.IndirectOffsetOnAxis(ap=late_idx[p][:, k:k + 1], axis=0)).then_inc(late_in, 16)

            REST, AHEAD = {0: 3, 1: 4, 3: 5}, {5: 0, 7: 1, ET: 2}

            def chunk(narrow, i, p, last, work):
                c = 2 * i + p
                goes_on = not is_known(i, NCH // 2 - 1)
                for t in range(ET):
                    if not last and t in REST:
                        gather(c + 1, 1 - p, REST[t])
                    if goes_on and t in AHEAD:
                        gather(c + 2, p, AHEAD[t])
                    if t == 0:
                        pool.wait_ge(out_ready, c + 1)
                    if t % 2 == 0:
                        pool.wait_ge(sum_ready, PAIRS * c + t // 2 + 1)
                    k = t % TABLES
                    if is_first(c) and t < TABLES:
                        pool.wait_ge(g.table_clear[k], 16 * CLEARS)
                    else:
                        pool.wait_ge(added[k], 16 * (PER * c + t // TABLES))
                    pool.sem_inc(passed, 1)
                    nc.gpsimd.indirect_dma_start(
                        g.sums_dram[k], bass.IndirectOffsetOnAxis(ap=out_idx[p][:, t:t + 1], axis=0),
                        summed[p][:, t, :], None, compute_op=ALU.add).then_inc(added[k], 16)
                if goes_on:
                    gather(c + 2, p, AHEAD[ET])
                if not last:
                    late_rows(i + p, 1 - p, narrow)

            nc.gpsimd.memset(attr[:], 0.0).then_inc(cleared, 1)
            for t in range(ET - WINDOWED):
                gather(0, 0, t)
            pool.wait_ge(win_step, WIN_DONE)
            is_wide = pool.value_load(wide_i[0:1, 0:1], min_val=0, max_val=1)
            for t in range(len(AHEAD)):
                gather(1, 1, t)
            with pool.If(is_wide > 0):
                late_rows(0, 0, False)
                along(pool, lambda *a: chunk(False, *a))
            with pool.Else():
                late_rows(0, 0, True)
                along(pool, lambda *a: chunk(True, *a))
            for k in range(TABLES):
                pool.wait_ge(added[k], 16 * PER * NCH)

        @block.tensor
        def _(pe):
            T = nc.tensor

            def hidden(i, p, h):
                c = 2 * i + p
                pe.wait_ge(attr_ready, 2 * c + h + 1)
                for f in range(CB):
                    if not (is_first(c) and h == 0):
                        pe.wait_ge(hid_ready, 2 * (2 * c + h) - 1 + f)
                    mm = T.matmul(hps[f][:], wf1_parts[:, ds(f * P, P)], attr_parts[:, h, :], start=True, stop=True)
                mm.then_inc(hid_made, 1)

            def filt(i, p, j):
                c = 2 * i + p
                h = j // 2
                if j % 2 == 0:
                    pe.wait_ge(hid_ready, 4 * c + 2 * h + 2)
                if not (is_first(c) and j < 2):
                    pe.wait_ge(msg_ready, PAIRS * c + j - 1)
                for t in range(2):
                    out = fps[j % 2][:, ds(t * C, C)]
                    T.matmul(out, g.ones2[:], g.bf2[:], start=True, stop=False)
                    for f in range(CB):
                        mm = T.matmul(out, hidT[:, h, f, ds((2 * (j % 2) + t) * P, P)], g.wf2[:, f, :],
                                      start=False, stop=f == CB - 1)
                mm.then_inc(filt_made, 1)

            def merge(i, p, j):
                c = 2 * i + p
                pe.wait_ge(low_ready, PAIRS * c + j + 1)
                pe.wait_ge(same_ready, PAIRS * c + j + 1)
                if j == 2:
                    if isinstance(c, int) and c == NCH - 1:
                        pe.wait_ge(sum_ready, PAIRS * c + j)
                    else:
                        pe.wait_ge(spread_out, c + 2)
                elif not (is_first(c) and j == 0):
                    pe.wait_ge(sum_ready, PAIRS * c + j)
                for t in range(2):
                    for k, half in enumerate((msg_high, msg_low)):
                        mm = T.matmul(sps[:, ds(t * C, C)], same[:, p, 2 * j + t, :], half[:, j % 2, t, :],
                                      start=k == 0, stop=k == 1)
                mm.then_inc(sum_made, 1)

            def spread_rows(c):
                pe.wait_ge(spread_ready, c + 1)
                pe.wait_ge(window_in, 16 * WINDOWED * (c + 1))
                if not is_first(c):
                    pe.wait_ge(sum_ready, PAIRS * (c - 1) + 2)
                for k in range(WINDOWED):
                    mm = T.matmul(sps[:, ds(k * C, C)], spread[:, k, :], window[:, k, :], start=True, stop=True)
                mm.then_inc(spread_made, 1)

            def chunk(i, p, last, work):
                filt(i, p, 0)
                if not is_first(2 * i + p):
                    merge(i + p - 1, 1 - p, 3)
                work(0)
                filt(i, p, 1)
                merge(i, p, 0)
                if not last:
                    hidden(i + p, 1 - p, 0)
                work(1)
                filt(i, p, 2)
                merge(i, p, 1)
                work(2)
                if not last:
                    spread_rows(2 * i + p + 1)
                filt(i, p, 3)
                merge(i, p, 2)
                if not last:
                    hidden(i + p, 1 - p, 1)
                work(3)

            def turn_rows(out, rows, n_tiles):
                for t in range(n_tiles):
                    for b in range(CB):
                        mm = T.transpose(out[:, ds((t * CB + b) * P, P)], rows[:, t, ds(b * P, P)], g.ident[:])
                return mm

            def k_product(s, j):
                h, f = j // CB, j % CB
                for b in range(CB):
                    mm = T.matmul(bankK[:, 0:HC], g.wqkv[:, b, ds(C + f * P, P)],
                                  g.xT[:, b, ds(s * GC + h * HC, HC)], start=b == 0, stop=b == CB - 1)
                mm.then_inc(k_made, 1)

            def scores(s, slot):
                if slot < 4:
                    if slot == 0:
                        pe.wait_ge(stage_in, 16 * (s + 1))
                    pe.wait_ge(t_free, 1 + T_SCORES + 4 * s + slot)
                    tiles = pair_tiles(slot)
                    turn_rows(bankT, xn[:, tiles[0]:tiles[-1] + 1, :], len(tiles)).then_inc(t_made, 1)
                elif 5 <= slot < 9:
                    j = slot - 5
                    pe.wait_ge(t_free, 1 + T_SCORES + 4 * s + 4)
                    pe.wait_ge(k_free, 1 + K_SCORES + 4 * s + j)
                    k_product(s, j)
                if is_known(s, NG - 1) and slot == 10:
                    pe.wait_ge(k_free, 1 + K_FOLD)
                    for b in range(CB):
                        mm = T.matmul(bankK[0:GH, 0:1], g.wg1[:, b, :], g.ln_b[:, b:b + 1],
                                      start=b == 0, stop=b == CB - 1)
                    mm.then_inc(k_made, 1)

            def gram(s, slot):
                if slot in EXP_SLOTS:
                    j = EXP_SLOTS.index(slot)
                    pe.wait_ge(k_free, 1 + K_GRAM + 4 * s + j)
                    k_product(s, j)
                if GRAM_SLOT <= slot < GRAM_SLOT + GT:
                    t = slot - GRAM_SLOT
                    pe.wait_ge(k_free, 1 + K_GRAM + 4 * s + 4)
                    pe.wait_ge(t_free, 1 + T_GRAM + GT * s + t)
                    rows = rows_of(s * GT + t)
                    for f in range(CB):
                        mm = T.transpose(bankT[0:rows, ds(f * P, P)], turnedT[:, f, ds(t * P, rows)], g.ident[:])
                    mm.then_inc(t_made, 1)
                if GRAM_SLOT < slot <= GRAM_SLOT + GT:
                    t = slot - GRAM_SLOT - 1
                    if t == 0:
                        pe.wait_ge(stage_in, 16 * (NG + s + 1))
                    pe.wait_ge(node_ready, GT * s + t + 1)
                    rows = rows_of(s * GT + t)
                    for b in range(CB):
                        mm = T.matmul(bankG[:, ds(b * C, C)], xn[0:rows, t, ds(b * P, P)], e_node[0:rows, t % 2, :],
                                      start=is_first(s) and t == 0 and b == 0,
                                      stop=is_known(s, NG - 1) and t == GT - 1 and b == CB - 1,
                                      skip_group_check=True)
                    mm.then_inc(gram_made, 1)

            def context():
                pe.wait_ge(stage, 1)
                pe.wait_ge(k_free, 1 + K_CTX)
                for f in range(CB):
                    for b in range(CB):
                        mm = T.matmul(bankK[:, ds(f * P, P)], gramT[:, b, ds(f * P, P)],
                                      g.wqkv[:, b, ds(2 * C + f * P, P)], start=b == 0, stop=b == CB - 1)
                mm.then_inc(k_made, 1)

            def queries():
                pe.wait_ge(k_free, 1 + K_OUT)
                pe.wait_ge(t_free, 1 + T_CTX)
                for b in range(CB):
                    for f in range(CB):
                        mm = T.matmul(bankT[:, ds(b * C + f * P, P)], g.wq_t[:, f, ds(b * P, P)],
                                      ctx_m[:, f, :], start=True, stop=True)
                mm.then_inc(t_made, 1)

            def output(s, slot):
                t0, k0 = T_OUT + T_OUT_PER * s, K_OUT + K_OUT_PER * s
                if is_first(s) and slot == 0:
                    context()
                if is_first(s) and slot == 1:
                    queries()
                if 1 <= slot < 5:
                    k = slot - 1
                    pe.wait_ge(xhat_ready, 4 * s + k + 1)
                    pe.wait_ge(t_free, 1 + t0 + k)
                    turn_rows(bankT, xhat[:, k % 2, :, :], len(pair_tiles(k))).then_inc(t_made, 1)
                if 5 <= slot < 7:
                    h = slot - 5
                    pe.wait_ge(t_free, 1 + t0 + 4)
                    pe.wait_ge(k_free, 1 + k0 + h)
                    for b in range(CB):
                        mm = T.matmul(bankK[0:GH, 0:HC], g.wg1f[:, b, :], turnedT[:, b, ds(h * HC, HC)],
                                      start=b == 0, stop=b == CB - 1)
                    mm.then_inc(k_made, 1)
                if 7 <= slot < 11:
                    j = slot - 7
                    h, f = j // CB, j % CB
                    pe.wait_ge(k_free, 1 + k0 + 2 + j)
                    T.matmul(bankK[:, 0:HC], g.wg2[:, ds(f * P, P)], hid[:, ds(h * HC, HC)],
                             start=True, stop=True).then_inc(k_made, 1)
                if 8 <= slot < 12:
                    j = slot - 8
                    h, f = j // CB, j % CB
                    pe.wait_ge(t_free, 1 + t0 + 4 + j)
                    for b in range(CB):
                        mm = T.matmul(bankT[:, 0:HC], g.wqm[:, b, ds(f * P, P)],
                                      g.xT[:, b, ds(s * GC + h * HC, HC)], start=b == 0, stop=b == CB - 1)
                    mm.then_inc(t_made, 1)
                if slot >= 12:
                    k = slot - 12
                    pe.wait_ge(t_free, 1 + t0 + 8)
                    pe.wait_ge(k_free, 1 + k0 + 6 + k)
                    for n, t in enumerate(pair_tiles(k)):
                        out = bankK[:, ds(n * C, C)]
                        T.matmul(out, g.ones2[:], g.bproj[:], start=True, stop=False)
                        for f in range(CB):
                            mm = T.matmul(out, gate[:, f, ds(t * P, P)], g.wproj[:, f, :],
                                          start=False, stop=f == CB - 1)
                    mm.then_inc(k_made, 1)

            pe.sem_inc(gram_made, 1)
            pe.wait_ge(win_step, 1)
            for k in range(WINDOWED):
                mm = T.transpose(bankT[0:NCH, ds(k * P, P)], dst_w.rearrange("p (c t) -> p t c", t=WINDOWED)[:, k, :],
                                 g.ident[:])
            mm.then_inc(win_turned, 1)
            pe.wait_ge(wf1_ready, 2)
            hidden(0, 0, 0)
            hidden(0, 0, 1)
            spread_rows(0)
            along(pe, chunk, scores, gram, output)
            merge(NCH // 2 - 1, 1, 3)

        @block.scalar
        def _(act):
            A = nc.scalar

            def silu(i, p, h):
                c = 2 * i + p
                act.wait_ge(hid_made, 2 * c + h + 1)
                if not is_first(c):
                    act.wait_ge(filt_made, PAIRS * (c - 1) + 2 * h + 2)
                for f in range(CB):
                    A.activation(hidT[:, h, f, :], hps[f][:], ACT.Silu, bias=g.bf1[:, f:f + 1]).then_inc(hid_ready, 1)

            def copy_sums(i, p, j):
                c = 2 * i + p
                act.wait_ge(sum_made, PAIRS * c + j + 1)
                if not is_first(i):
                    for k in range(TABLES):
                        act.wait_ge(added[k], 16 * PER * (c - 1))
                A.activation(summed[p][:, ds(2 * j, 2), :], sps[:].rearrange("p (t c) -> p t c", c=C),
                             ACT.Copy).then_inc(sum_ready, 1)

            def high_attr(i, p, h):
                c = 2 * i + p
                act.wait_ge(attr_in[h], 48 * (c + 1))
                if not is_first(c):
                    act.wait_ge(hid_made, 2 * (c - 1) + h + 1)
                A.activation(attr_parts[:, h, :], attr[:, h, :], ACT.Copy).then_inc(attr_rounded, 1)

            def high_half(i, p, j):
                c = 2 * i + p
                act.wait_ge(msg_ready, PAIRS * c + j + 1)
                A.activation(msg_high[:, j % 2, :, :], msg[:, j % 2, :, :], ACT.Copy).then_inc(high_ready, 1)

            def copy_rows(c, p):
                act.wait_ge(spread_made, c + 1)
                if not (isinstance(c, int) and c < 2):
                    act.wait_ge(msg_ready, PAIRS * (c - 1))
                A.activation(gathered[p][:, ds(ET - WINDOWED, WINDOWED), :],
                             sps[:].rearrange("p (t c) -> p t c", c=C), ACT.Copy).then_inc(spread_out, 1)

            def chunk(i, p, last, work):
                if not is_first(2 * i + p):
                    copy_sums(i + p - 1, 1 - p, 3)
                if not last:
                    high_attr(i + p, 1 - p, 0)
                high_half(i, p, 0)
                work(0)
                copy_sums(i, p, 0)
                high_half(i, p, 1)
                if not last:
                    silu(i + p, 1 - p, 0)
                work(1)
                copy_sums(i, p, 1)
                if not last:
                    high_attr(i + p, 1 - p, 1)
                high_half(i, p, 2)
                work(2)
                if not last:
                    copy_rows(2 * i + p + 1, 1 - p)
                copy_sums(i, p, 2)
                high_half(i, p, 3)
                if not last:
                    silu(i + p, 1 - p, 1)
                work(3)

            def copy_turned(dst, c0, n):
                A.activation(dst[:, :, ds(c0, n * P)].rearrange("p f (t n) -> p f t n", n=P),
                             bankT[:, 0:n * C].rearrange("p (t f n) -> p f t n", f=CB, n=P),
                             ACT.Copy).then_inc(t_free, 1)

            def scores(s, slot):
                if slot < 4:
                    act.wait_ge(t_made, T_SCORES + 4 * s + slot + 1)
                    copy_turned(g.xT, s * GC + slot * 2 * P, len(pair_tiles(slot)))
                if is_known(s, NG - 1) and slot == 14:
                    act.wait_ge(var_ready, 1)
                    A.activation(m.rstd[:], m.rstd[:], ACT.Sqrt).then_inc(std_ready, 1)

            def gram(s, slot):
                if slot in EXP_SLOTS:
                    j = EXP_SLOTS.index(slot)
                    h, f = j // CB, j % CB
                    n = tail_cols(s, h) if is_known(s, NG - 1) else HC
                    if is_first(s):
                        act.wait_ge(maxed, CB)
                    act.wait_ge(k_made, K_GRAM + 4 * s + j + 1)
                    act.wait_ge(t_made, T_GRAM + GT * s)
                    A.activation(turnedT[:, f, ds(h * HC, n)], bankK[:, 0:n], ACT.Exp, bias=g.neg_k_max[:, f:f + 1],
                                 accum_out=g.k_sum[:, f, ds(2 * s + h, 1)]).then_inc(k_free, 1)

            def output(s, slot):
                t0, k0 = T_OUT + T_OUT_PER * s, K_OUT + K_OUT_PER * s
                if 1 <= slot < 5:
                    k = slot - 1
                    act.wait_ge(t_made, t0 + k + 1)
                    act.wait_ge(k_made, k0 - K_OUT_PER + 2)
                    copy_turned(turnedT, k * 2 * P, len(pair_tiles(k)))
                if 5 <= slot < 7:
                    h = slot - 5
                    act.wait_ge(k_made, k0 + h + 1)
                    A.activation(hid[:, ds(h * HC, HC)], bankK[0:GH, 0:HC], ACT.Gelu,
                                 bias=g.bg1f[:, 0:1]).then_inc(k_free, 1)
                if 7 <= slot < 11:
                    j = slot - 7
                    h, f = j // CB, j % CB
                    act.wait_ge(k_made, k0 + 2 + j + 1)
                    A.activation(gate[:, f, ds(h * HC, HC)], bankK[:, 0:HC], ACT.Sigmoid,
                                 bias=g.bg2[:, f:f + 1]).then_inc(k_free, 1)

            act.wait_ge(win_step, WIN_ENDS)
            with nc.allow_non_contiguous_dma(reason="four hundred numbers"):
                act.dma_start(g.ends_dram.rearrange("k (c t) -> c k t", t=WINDOWED), extremes[:]).then_inc(ends_out, 16)
            act.wait_ge(ends_out, 16)
            act.dma_start(ends_all.rearrange("p k n -> p (k n)"),
                         g.ends_dram.rearrange("(a k) n -> a (k n)", a=1).to_broadcast([P, 2 * NW])).then_inc(ends_in, 16)
            high_attr(0, 0, 0)
            high_attr(0, 0, 1)
            act.wait_ge(window_in, 16 * WINDOWED)
            for k in range(1, TABLES):
                clear_table(act, g, k)
            silu(0, 0, 0)
            silu(0, 0, 1)
            copy_rows(0, 0)
            along(act, chunk, scores, gram, output)
            copy_sums(NCH // 2 - 1, 1, 3)

        @block.vector
        def _(dve):
            V = nc.vector

            def low_attr(i, p, h):
                c = 2 * i + p
                dve.wait_ge(attr_rounded, 2 * c + h + 1)
                V.tensor_tensor(attr_parts[64:SPAN, h, :], attr[64:SPAN, h, :],
                                attr_parts[64:SPAN, h, :].bitcast(F32), ALU.subtract).then_inc(attr_ready, 1)

            def dst_columns(i, p):
                V.tensor_copy(dst_idx[p][:], dst_all[:, ds((2 * i + p) * ET, ET - WINDOWED)]).then_inc(idx_ready, 1)

            def late_columns(i, p):
                V.tensor_copy(late_idx[p][:], dst_all[:, ds((2 * i + p) * ET + ET - WINDOWED, WINDOWED)])\
                 .then_inc(late_ready, 1)

            def indicate(c):
                dve.wait_ge(dst_row_in, 16 * (c + 1))
                if not is_first(c):
                    dve.wait_ge(spread_made, c)
                for k in range(WINDOWED):
                    op = V.tensor_scalar(spread[:, k, :], dst_row[:, ds(k * P, P)],
                                         window_row[:, ds(WINDOWED * c + k, 1)], None, ALU.is_equal)
                op.then_inc(spread_ready, 1)

            def low_half(i, p, j):
                c = 2 * i + p
                dve.wait_ge(high_ready, PAIRS * c + j + 1)
                V.tensor_tensor(msg_low[:, j % 2, :, :], msg[:, j % 2, :, :], msg_high[:, j % 2, :, :].bitcast(F32),
                                ALU.subtract).then_inc(low_ready, 1)

            def equal(i, p, t):
                c = 2 * i + p
                if t == 0:
                    dve.wait_ge(row_in[p], 16 * i + 16)
                    if not is_first(i):
                        dve.wait_ge(sum_made, PAIRS * (c - 1))
                row = src_row[:, p, ds(t * P, P)]
                col = src_f[:, ds(c * ET + t, 1)]
                V.tensor_scalar(same[:, p, t, :], row, col, None, ALU.is_equal)
                op = V.scalar_tensor_tensor(out=rank_scr[:, t, :], in0=row, scalar=col, in1=g.earlier[:],
                                            op0=ALU.is_equal, op1=ALU.mult, accum_out=rank[:, t:t + 1])
                if t % 2:
                    op.then_inc(same_ready, 1)

            def out_rows(i, p):
                c = 2 * i + p
                dve.wait_ge(same_ready, PAIRS * c + PAIRS)
                V.scalar_tensor_tensor(out=redirect[:], in0=rank[:], scalar=0.0, in1=to_trash[:, ds(c * ET, ET)],
                                       op0=ALU.is_gt, op1=ALU.mult).then_inc(redirected, 1)
                dve.wait_ge(redirected, c + 1)
                if not is_first(i):
                    for k in range(TABLES):
                        dve.wait_ge(added[k], 16 * PER * (c - 1))
                V.tensor_tensor(out_idx[p][:], redirect[:], src_f[:, ds(c * ET, ET)], ALU.add).then_inc(out_ready, 1)

            def message(i, p, j):
                c = 2 * i + p
                if j == 0:
                    dve.wait_ge(rows_in[p][0], 16 * 4 * (i + 1))
                if j == 2:
                    dve.wait_ge(rows_in[p][1], 16 * 2 * (i + 1))
                if j == 3:
                    dve.wait_ge(late_in, 16 * WINDOWED * (c + 1))
                dve.wait_ge(filt_made, PAIRS * c + j + 1)
                if not (is_first(c) and j < 2):
                    dve.wait_ge(sum_made, PAIRS * c + j - 1)
                V.tensor_tensor(msg[:, j % 2, :, :], fps[j % 2][:].rearrange("p (t c) -> p t c", c=C),
                                gathered[p][:, ds(2 * j, 2), :], ALU.mult).then_inc(msg_ready, 1)

            def chunk(i, p, last, work):
                for j in range(PAIRS):
                    message(i, p, j)
                    if not last:
                        equal(i + p, 1 - p, 2 * j)
                        if j % 2 == 0:
                            low_attr(i + p, 1 - p, j // 2)
                    low_half(i, p, j)
                    if not last:
                        equal(i + p, 1 - p, 2 * j + 1)
                        if j == 0:
                            indicate(2 * i + p + 1)
                    if not is_known(i, NCH // 2 - 1):
                        if j == 2:
                            dst_columns(i + 1, p)
                        if j == 3:
                            late_columns(i + 1, p)
                    work(j)
                if not last:
                    out_rows(i + p, 1 - p)

            def scores(s, slot):
                if slot < 4:
                    if slot == 0:
                        dve.wait_ge(stage_in, 16 * (s + 1))
                    for t in pair_tiles(slot):
                        V.bn_stats(m.raw[:, s * GT + t, :], xn[:, t, :]).then_inc(stats, 1)
                if 5 <= slot < 9:
                    j = slot - 5
                    h, f = j // CB, j % CB
                    n = tail_cols(s, h) if is_known(s, NG - 1) else HC
                    dve.wait_ge(k_made, K_SCORES + 4 * s + j + 1)
                    V.tensor_reduce(g.k_max[:, f, ds(2 * s + h, 1)], bankK[:, 0:n], X, ALU.max).then_inc(k_free, 1)
                if not is_known(s, NG - 1):
                    return
                if slot == 9:
                    dve.wait_ge(k_free, 1 + 4 * NG)
                    for f in range(CB):
                        V.tensor_reduce(g.neg_k_max[:, f:f + 1], g.k_max[:, f, :], X, ALU.max,
                                        negate=True).then_inc(maxed, 1)
                if slot == 10:
                    dve.wait_ge(k_made, K_FOLD + 1)
                    V.tensor_tensor(g.bg1f[:], bankK[0:GH, 0:1], g.bg1[:], ALU.add).then_inc(k_free, 1)
                    for b in range(CB):
                        V.tensor_scalar(g.wg1f[:, b, :], g.wg1[:, b, :], g.ln_g[:, b:b + 1], None,
                                        ALU.mult).then_inc(folded, 1)
                if slot == 12:
                    V.memset(g.head_mask[:], 0.0).then_inc(folded, 1)
                    dve.wait_ge(folded, CB + 1)
                    for h in range(P // MD):
                        V.memset(g.head_mask[ds(h * MD, MD), ds(h * MD, MD)], 1.0).then_inc(folded, 1)
                if slot == 13:
                    dve.wait_ge(stats, NT)
                    combine_moments(nc, dve, m, 0, NT, step, 0)
                    dve.wait_ge(step, MOMENT_STEPS)
                    dve.sem_inc(var_ready, 1)

            def gram(s, slot):
                if is_first(s) and slot == 0:
                    dve.wait_ge(std_ready, 1)
                if GRAM_SLOT <= slot < GRAM_SLOT + GT:
                    t = slot - GRAM_SLOT
                    rows = rows_of(s * GT + t)
                    dve.wait_ge(t_made, T_GRAM + GT * s + t + 1)
                    dve.wait_ge(gram_made, 1 + GT * s + max(t - 1, 0))
                    V.tensor_copy(e_node[0:rows, t % 2, :], bankT[0:rows, 0:C]).then_inc(node_ready, 1)
                    dve.wait_ge(node_ready, GT * s + t + 1)
                    dve.sem_inc(t_free, 1)

            def context():
                dve.wait_ge(std_ready, 1)
                V.reciprocal(m.rstd[:], m.rstd[:]).then_inc(rstd_ready, 1)
                dve.wait_ge(gram_made, 1 + NT)
                V.tensor_copy(gramT.rearrange("p b n -> p (b n)"), bankG[:]).then_inc(stage, 1)
                dve.wait_ge(k_free, 1 + K_CTX)
                V.tensor_reduce(g.k_tot[:], g.k_sum[:], X, ALU.add).then_inc(stage, 1)
                dve.wait_ge(stage, 2)
                V.reciprocal(g.k_inv[:], g.k_tot[:]).then_inc(stage, 1)
                dve.wait_ge(stage, 3)
                dve.wait_ge(folded, CB + 1 + P // MD)
                dve.wait_ge(k_made, K_CTX + 1)
                for f in range(CB):
                    V.scalar_tensor_tensor(out=ctx_m[:, f, :], in0=bankK[:, ds(f * P, P)],
                                           scalar=g.k_inv[:, f:f + 1], in1=g.head_mask[:],
                                           op0=ALU.mult, op1=ALU.mult).then_inc(stage, 1)
                dve.wait_ge(stage, 3 + CB)
                dve.sem_inc(k_free, 1)
                dve.wait_ge(rstd_ready, 1)

            def queries():
                dve.wait_ge(t_made, T_CTX + 1)
                V.tensor_copy(g.wqm[:], bankT[:].rearrange("p (b n) -> p b n", b=CB)).then_inc(t_free, 1)

            def output(s, slot):
                t0, k0 = T_OUT + T_OUT_PER * s, K_OUT + K_OUT_PER * s
                if is_first(s) and slot == 0:
                    context()
                if is_first(s) and slot == 1:
                    queries()
                if slot < 4:
                    if slot == 0:
                        dve.wait_ge(stage_in, 16 * (2 * NG + s + 1))
                    before = t0 + slot - 1 if slot >= 2 else t0 - T_OUT_PER + slot + 3
                    dve.wait_ge(t_made, before)
                    for n, t in enumerate(pair_tiles(slot)):
                        op = V.tensor_scalar(xhat[:, slot % 2, n, :], xn[:, t, :], m.mean[:, ds(s * GT + t, 1)],
                                             m.rstd[:, ds(s * GT + t, 1)], ALU.subtract, ALU.mult)
                    op.then_inc(xhat_ready, 1)
                if 4 <= slot < 8:
                    k = slot - 4
                    if k == 0:
                        dve.wait_ge(x_in, 16 * (s + 1) + (16 if is_known(s, NG - 1) else 0))
                    tiles = pair_tiles(k)
                    here = slice(tiles[0], tiles[-1] + 1)
                    V.tensor_tensor(res[:, here, :], res[:, here, :], xn[:, here, :], ALU.add).then_inc(presum_ready, 1)
                if 8 <= slot < 12:
                    j = slot - 8
                    h, f = j // CB, j % CB
                    dve.wait_ge(t_made, t0 + 4 + j + 1)
                    dve.wait_ge(k_free, 1 + k0 + 2 + j + 1)
                    cols = gate[:, f, ds(h * HC, HC)]
                    V.tensor_tensor(cols, bankT[:, 0:HC], cols, ALU.mult).then_inc(t_free, 1)
                if slot >= 12:
                    k = slot - 12
                    tiles = pair_tiles(k)
                    here = slice(tiles[0], tiles[-1] + 1)
                    dve.wait_ge(presum_ready, 4 * s + k + 1)
                    dve.wait_ge(k_made, k0 + 6 + k + 1)
                    V.tensor_tensor(res[:, here, :], bankK[:, 0:len(tiles) * C].rearrange("p (t c) -> p t c", c=C),
                                    res[:, here, :], ALU.add).then_inc(res_ready, 1)
                    dve.wait_ge(res_ready, 4 * s + k + 1)
                    dve.sem_inc(k_free, 1)

            dve.sem_inc(t_free, 1)
            dve.sem_inc(k_free, 1)
            V.memset(wf1_raw[:], 0.0).then_inc(cleared, 1)
            dve.wait_ge(cols_in, 32)
            V.tensor_copy(dst_w.rearrange("p (c t) -> p c t", t=WINDOWED),
                          dst_all[:].rearrange("p (c t) -> p c t", t=ET)[:, :, ET - WINDOWED:ET]).then_inc(win_step, 1)
            for p in range(2):
                dst_columns(0, p)
                late_columns(0, p)
            V.tensor_copy(src_f[:], src_i).then_inc(cols_ready, 1)
            V.tensor_copy(trash_f[:], g.trash_i[:]).then_inc(cols_ready, 1)
            dve.wait_ge(cols_ready, 2)
            V.tensor_scalar(to_trash[:], src_f[:], trash_f[:, 0:1], -1.0, ALU.subtract, ALU.mult).then_inc(cols_ready, 1)
            dve.wait_ge(cols_ready, 3)
            dve.wait_ge(win_turned, 1)
            turned = bankT[0:NCH, 0:WINDOWED * P].rearrange("c (t e) -> c t e", e=P)
            V.tensor_reduce(extremes[:, 0, :], turned, X, ALU.min).then_inc(win_step, 1)
            V.tensor_reduce(extremes[:, 1, :], turned, X, ALU.max).then_inc(win_step, 1)
            dve.wait_ge(win_step, 3)
            V.tensor_scalar(extremes[:, 0, :], extremes[:, 0, :], float(NPAD - P), None, ALU.min).then_inc(win_step, 1)
            dve.wait_ge(win_step, 4)
            V.tensor_tensor(extremes[:, 1, :], extremes[:, 1, :], extremes[:, 0, :], ALU.subtract).then_inc(win_step, 1)
            dve.wait_ge(wf1_in, 48)
            V.tensor_copy(wf1_parts[:], wf1_raw[:]).then_inc(wf1_ready, 1)
            dve.wait_ge(wf1_ready, 1)
            V.tensor_tensor(wf1_parts[32:64, :], wf1_raw[32:64, :], wf1_parts[32:64, :].bitcast(F32),
                            ALU.subtract).then_inc(wf1_ready, 1)
            low_attr(0, 0, 0)
            low_attr(0, 0, 1)
            dve.wait_ge(ends_in, 16)
            V.tensor_copy(base_i[:], ends_all[0:1, 0, :]).then_inc(win_step, 1)
            V.tensor_reduce(widest[:], ends_all[0:1, 1, :], X, ALU.max).then_inc(win_step, 1)
            V.tensor_scalar(window_row[:], ends_all[:, 0, :], trash_f[:, 0:1], float(-TRASH), ALU.add,
                            ALU.add).then_inc(win_step, 1)
            dve.wait_ge(win_step, 8)
            V.tensor_scalar(wide_i[:], widest[:], float(P), None, ALU.is_ge).then_inc(win_step, 1)
            for t in range(ET):
                equal(0, 0, t)
            indicate(0)
            out_rows(0, 0)
            along(dve, chunk, scores, gram, output)


def update_nodes(nc, sem, sb, g):
    w = g.w
    wx_t = sb("wx_t", [FD, FH, C], F32)
    w_slice = sb("w_slice", [FD, FG], F32)
    b_x = sb("b_x", [FD, FH], F32)
    b_slice = sb("b_slice", [1, FG], F32)
    temp = sb("temp", [P, FH], F32)
    inv_temp = sb("inv_temp", [P, FH], F32)
    bias = sb("slice_bias", [1, HG], F32)
    ends = sb("slice_bias_ends", [1, BIAS_ROWS], F32)
    logit_w = sem("u_logit_w")
    fold = sem("u_fold")
    folded = sem("u_folded")
    row_stats = sem("u_row_stats")
    step = sem("u_step")
    root = sem("u_root")
    slice_in = sem("u_slice_in")
    m = g.mom
    parts_in = [sem(f"u_parts_in{p}") for p in range(2)]
    weights = update_weights(sb, g)
    weights_in = sem("u_weights_in")
    res_in = sem("u_res_in")
    agg_ready = sem("u_agg_ready")
    turned = sem("u_turned")
    turn_copied = sem("u_turn_copied")
    hid_made = sem("u_hid_made")
    hid_ready = sem("u_hid_ready")
    h_made = sem("u_h_made")
    h_ready = sem("u_h_ready")
    stats = sem("u_stats")
    chain = sem("u_chain")
    norm_ready = sem("u_norm_ready")
    back_made = sem("u_back_made")
    back_ready = sem("u_back_ready")
    part = [[sb(f"part{p}{k}", [P, GT, C], F32) for k in range(TABLES)] for p in range(2)]
    agg_high, agg_low = sb("agg_high", [P, CB, GC], F32R), sb("agg_low", [P, CB, GC], F32R)
    hid_high, hid_low = sb("hid_high", [P, CB, GC], F32R), sb("hid_low", [P, CB, GC], F32R)
    hidT = [part[p][1][:].rearrange("p t c -> p (t c)").rearrange("p (b n) -> p b n", b=CB) for p in range(2)]
    wu1h, wu1l = sb("wu1h", [P, CB, C], F32R), sb("wu1l", [P, CB, C], F32R)
    wu2h, wu2l = sb("wu2h", [P, CB, C], F32R), sb("wu2l", [P, CB, C], F32R)
    wu_high, wu_low = sem("u_wu_high"), sem("u_wu_low")
    turn_low = sem("u_turn_low")
    hid_rounded, hid_lowered = sem("u_hid_rounded"), sem("u_hid_lowered")
    hT = sb("hT", [P, CB, NPAD], F32)
    raw = sb("bn_raw", [P, CB, 2 * NG, 6], F32)
    mv = sb("bn_mv", [P, CB, 2], F32)
    sd = sb("bn_sd", [P, CB], F32)
    scale = sb("bn_scale", [P, CB], F32)
    shift = sb("bn_shift", [P, CB], F32)
    flat = [part[p][0][:].rearrange("p t c -> p (t c)") for p in range(2)]
    w_logit = flat[0][:, 0:CB * HG].rearrange("p (b n) -> p b n", b=CB)
    spread = flat[1][0:BIAS_ROWS, 0:HG]
    turn = [g.ps[0], g.ps[1]]
    ups = [g.ps[2], g.ps[3]]
    hps = [g.ps[4], g.ps[5]]
    bps = [g.ps[6], g.ps[7]]

    FOLD_BIAS = 7
    heads = lambda ap: ap.rearrange("p (h n) -> p h n", h=FH)
    wide = lambda ap, n: ap.unsqueeze(2).to_broadcast([n, FH, FG])

    with nc.Block() as block:
        @block.sync
        def _(sp):
            for s in range(NG):
                if s >= 2:
                    sp.wait_ge(turned, 4 * (s - 1))
                    sp.wait_ge(hid_lowered, 4 * (s - 1))
                for k in range(TABLES):
                    sp.dma_start(part[s % 2][k][:], split_rows(g.sums_dram[k], s * GT, GT)).then_inc(parts_in[s % 2], 16)
            sp.dma_start(g.res[:], split_rows(g.res_dram, 0, NT)).then_inc(res_in, 16)

        @block.tensor
        def _(pe):
            def turn_sums(s, pairs):
                pe.wait_ge(agg_ready, s + 1)
                for k in pairs:
                    if 4 * s + k >= 2:
                        pe.wait_ge(turn_low, 4 * s + k - 1)
                    for t in range(2 * k, min(2 * k + 2, GT)):
                        for b in range(CB):
                            mm = nc.tensor.transpose(turn[k % 2][:, ds((t % 2 * CB + b) * P, P)],
                                                     part[s % 2][0][:, t, ds(b * P, P)], g.ident[:])
                    mm.then_inc(turned, 1)

            def product(s, h, wh, wl, high, low, bank, made, ready):
                for f in range(CB):
                    j = CB * h + f
                    if 4 * s + j >= 2:
                        pe.wait_ge(ready, 4 * s + j - 1)
                    for b in range(CB):
                        for k, (x, y) in enumerate(((wh, high), (wh, low), (wl, high))):
                            mm = nc.tensor.matmul(bank[f][:, 0:HC], x[:, b, ds(f * P, P)],
                                                  y[:, b, ds(h * HC, HC)], start=b == 0 and k == 0,
                                                  stop=b == CB - 1 and k == 2)
                    mm.then_inc(made, 1)

            turn_sums(0, range(4))
            pe.wait_ge(wu_low, 2)
            for s in range(NG):
                for h in range(2):
                    pe.wait_ge(turn_low, 4 * s + 2 + 2 * h)
                    product(s, h, wu1h, wu1l, agg_high, agg_low, ups, hid_made, hid_ready)
                for h in range(2):
                    if s + 1 < NG:
                        turn_sums(s + 1, range(2 * h, 2 * h + 2))
                    pe.wait_ge(hid_lowered, 4 * s + 2 + 2 * h)
                    product(s, h, wu2h, wu2l, hid_high, hid_low, hps, h_made, h_ready)
            pe.wait_ge(slice_in, 80)
            pe.wait_ge(turn_low, 4 * NG)
            pe.wait_ge(hid_ready, 4 * NG)
            for b in range(CB):
                for h in range(FH):
                    nc.tensor.matmul(g.ps[b][:, ds(h * FG, FG)], wx_t[:, h, ds(b * P, P)], w_slice[:],
                                     start=True, stop=True)
            for h in range(FH):
                mm = nc.tensor.matmul(g.ps[2][0:1, ds(h * FG, FG)], b_x[:, h:h + 1], w_slice[:], start=True, stop=True)
            mm.then_inc(folded, 1)
            pe.wait_ge(fold, FOLD_BIAS)
            nc.tensor.matmul(g.ps[3][0:BIAS_ROWS, :], ends[:], bias[:], start=True, stop=True).then_inc(folded, 1)
            for s in range(NG):
                pe.wait_ge(norm_ready, CB * (s + 1))
                for k in range(4):
                    if 4 * s + k >= 2:
                        pe.wait_ge(back_ready, 4 * s + k - 1)
                    for t in range(2 * k, min(2 * k + 2, GT)):
                        for f in range(CB):
                            mm = nc.tensor.transpose(bps[k % 2][:, ds((t % 2 * CB + f) * P, P)],
                                                     hT[:, f, ds(s * GC + t * P, P)], g.ident[:])
                    mm.then_inc(back_made, 1)

        @block.scalar
        def _(act):
            with nc.allow_non_contiguous_dma(reason="bias columns: a few hundred elements"):
                for t, src in weights:
                    act.dma_start(t[:], src).then_inc(weights_in, 16)
                act.dma_start(wx_t[:], w["ffn_W_xT"]).then_inc(slice_in, 16)
                act.dma_start(w_slice[:], w["ffn_W_slice"]).then_inc(slice_in, 16)
                act.dma_start(b_x[:], w["ffn_b_x"].rearrange("(h d) -> d h", h=FH)).then_inc(slice_in, 16)
                act.dma_start(b_slice[:], as_row(w["ffn_b_slice"])).then_inc(slice_in, 16)
                act.dma_start(temp[:], w["ffn_temperature"].rearrange("a h b c -> (a b c) h").to_broadcast([P, FH]))\
                  .then_inc(slice_in, 16)
            def copy_sums(s):
                for k in range(4):
                    n = 2 if k < 3 else 1
                    act.wait_ge(turned, 4 * s + k + 1)
                    if s:
                        act.wait_ge(hid_made, 4 * s)
                    nc.scalar.activation(
                        agg_high[:, :, ds(k * 2 * P, n * P)].rearrange("p f (t n) -> p f t n", n=P),
                        turn[k % 2][:, 0:n * C].rearrange("p (t f n) -> p f t n", f=CB, n=P),
                        ACT.Copy).then_inc(turn_copied, 1)

            def round_hidden(s, j):
                cols = ds(j // CB * HC, HC)
                act.wait_ge(hid_ready, 4 * s + j + 1)
                if s:
                    act.wait_ge(h_made, 4 * s)
                nc.scalar.activation(hid_high[:, j % CB, cols], hidT[s % 2][:, j % CB, cols],
                                     ACT.Copy).then_inc(hid_rounded, 1)

            copy_sums(0)
            for s in range(NG):
                for j in range(4):
                    h, f = j // CB, j % CB
                    act.wait_ge(hid_made, 4 * s + j + 1)
                    nc.scalar.activation(hidT[s % 2][:, f, ds(h * HC, HC)], ups[f][:, 0:HC], ACT.Silu,
                                         bias=g.bu1[:, f:f + 1]).then_inc(hid_ready, 1)
                    if j:
                        round_hidden(s, j - 1)
                round_hidden(s, 3)
                if s + 1 < NG:
                    copy_sums(s + 1)
            act.wait_ge(chain, 3)
            nc.scalar.activation(sd[:], sd[:], ACT.Sqrt).then_inc(chain, 1)
            act.wait_ge(chain, 8)
            for s in range(NG):
                for f in range(CB):
                    cols = hT[:, f, ds(s * GC, GC)]
                    nc.scalar.activation(cols, cols, ACT.Identity, bias=shift[:, f:f + 1],
                                         scale=scale[:, f:f + 1]).then_inc(norm_ready, 1)
            act.wait_ge(step, MOMENT_STEPS)
            nc.scalar.activation(m.rstd[:], m.rstd[:], ACT.Sqrt).then_inc(root, 1)

        @block.gpsimd
        def _(pool):
            for s in range(NG):
                for j in range(4):
                    cols = ds(j // CB * HC, HC)
                    pool.wait_ge(hid_rounded, 4 * s + j + 1)
                    nc.gpsimd.tensor_tensor(hid_low[:, j % CB, cols], hidT[s % 2][:, j % CB, cols],
                                            hid_high[:, j % CB, cols].bitcast(F32),
                                            ALU.subtract).then_inc(hid_lowered, 1)

        @block.vector
        def _(dve):
            def low_sums(s):
                for k in range(4):
                    n = 2 if k < 3 else 1
                    dve.wait_ge(turn_copied, 4 * s + k + 1)
                    cols = ds(k * 2 * P, n * P)
                    tiles = lambda ap: ap.rearrange("p f (t n) -> p f t n", n=P)
                    nc.vector.tensor_tensor(
                        tiles(agg_low[:, :, cols]),
                        turn[k % 2][:, 0:n * C].rearrange("p (t f n) -> p f t n", f=CB, n=P),
                        tiles(agg_high[:, :, cols].bitcast(F32)), ALU.subtract).then_inc(turn_low, 1)

            def fold_slices():
                dve.wait_ge(fold, 5)
                dve.wait_ge(folded, 1)
                nc.vector.tensor_tensor(heads(bias[:]), heads(g.ps[2][0:1, :]),
                                        b_slice[:].unsqueeze(1).to_broadcast([1, FH, FG]), ALU.add).then_inc(fold, 1)
                dve.wait_ge(fold, 6)
                nc.vector.tensor_tensor(heads(bias[:]), heads(bias[:]), wide(inv_temp[0:1, :], 1),
                                        ALU.mult).then_inc(fold, 1)
                for b in range(CB):
                    nc.vector.tensor_tensor(heads(w_logit[:, b, :]), heads(g.ps[b][:]), wide(inv_temp[:], P),
                                            ALU.mult).then_inc(logit_w, 1)
                dve.wait_ge(logit_w, CB)
                nc.vector.tensor_copy(g.logit_high[:], w_logit).then_inc(logit_w, 1)
                dve.wait_ge(logit_w, CB + 1)
                nc.vector.tensor_tensor(g.logit_low[:], w_logit, g.logit_high[:].bitcast(F32), ALU.subtract)
                dve.wait_ge(folded, 2)
                nc.vector.tensor_copy(spread, g.ps[3][0:BIAS_ROWS, :]).then_inc(fold, 1)
                dve.wait_ge(fold, 8)
                nc.vector.tensor_copy(g.logit_bias[:], spread).then_inc(fold, 1)
                dve.wait_ge(fold, 9)
                low = slice(BIAS_ROWS - 1, BIAS_ROWS)
                nc.vector.tensor_tensor(g.logit_bias[low, :], spread[low, :], g.logit_bias[low, :].bitcast(F32),
                                        ALU.subtract)

            def gather_sums(s):
                dve.wait_ge(parts_in[s % 2], 32 * (s // 2 + 1))
                a, b = part[s % 2]
                nc.vector.tensor_tensor(a[:], a[:], b[:], ALU.add).then_inc(agg_ready, 1)

            gather_sums(0)
            dve.wait_ge(weights_in, 16 * len(weights))
            for k, (w_f, high, low) in enumerate(((g.wu1, wu1h, wu1l), (g.wu2, wu2h, wu2l))):
                nc.vector.tensor_copy(high[:], w_f[:]).then_inc(wu_high, 1)
                dve.wait_ge(wu_high, k + 1)
                nc.vector.tensor_tensor(low[:], w_f[:], high[:].bitcast(F32), ALU.subtract).then_inc(wu_low, 1)
            low_sums(0)
            nc.vector.memset(ends[:], 0.0).then_inc(fold, 1)
            dve.wait_ge(fold, 1)
            for k in (0, BIAS_ROWS - 1):
                nc.vector.memset(ends[:, k:k + 1], 1.0).then_inc(fold, 1)
            dve.wait_ge(slice_in, 80)
            nc.vector.tensor_scalar(temp[:], temp[:], 0.1, 5.0, ALU.max, ALU.min).then_inc(fold, 1)
            dve.wait_ge(fold, 4)
            nc.vector.reciprocal(inv_temp[:], temp[:]).then_inc(fold, 1)
            for s in range(NG):
                if s + 1 < NG:
                    gather_sums(s + 1)
                    low_sums(s + 1)
                for j in range(4):
                    h, f = j // CB, j % CB
                    dve.wait_ge(h_made, 4 * s + j + 1)
                    nc.vector.tensor_scalar(hT[:, f, ds(s * GC + h * HC, HC)], hps[f][:, 0:HC],
                                            g.bu2[:, f:f + 1], None, ALU.add).then_inc(h_ready, 1)
                    dve.wait_ge(h_ready, 4 * s + j + 1)
                    n = HC if s < NG - 1 else tail_cols(s, h)
                    nc.vector.bn_stats(raw[:, f, 2 * s + h, :],
                                       hT[:, f, ds(s * GC + h * HC, n)]).then_inc(stats, 1)
            dve.wait_ge(stats, 4 * NG)
            for f in range(CB):
                nc.vector.bn_aggr(mv[:, f, :], raw[:, f, :, :]).then_inc(chain, 1)
            dve.wait_ge(chain, 2)
            nc.vector.tensor_scalar(sd[:], mv[:, :, 1], EPS, None, ALU.add).then_inc(chain, 1)
            fold_slices()
            dve.wait_ge(chain, 4)
            nc.vector.reciprocal(sd[:], sd[:]).then_inc(chain, 1)
            dve.wait_ge(chain, 5)
            nc.vector.tensor_tensor(scale[:], g.gamma[:], sd[:], ALU.mult).then_inc(chain, 1)
            dve.wait_ge(chain, 6)
            nc.vector.tensor_tensor(shift[:], mv[:, :, 0], scale[:], ALU.mult).then_inc(chain, 1)
            dve.wait_ge(chain, 7)
            nc.vector.tensor_tensor(shift[:], g.beta[:], shift[:], ALU.subtract).then_inc(chain, 1)
            dve.wait_ge(res_in, 16)
            for s in range(NG):
                for k in range(4):
                    n = 2 if k < 3 else 1
                    dve.wait_ge(back_made, 4 * s + k + 1)
                    here = g.res[:, ds(s * GT + 2 * k, n), :]
                    nc.vector.tensor_tensor(here, bps[k % 2][:, 0:n * C].rearrange("p (t c) -> p t c", c=C),
                                            here, ALU.add).then_inc(back_ready, 1)
                    dve.wait_ge(back_ready, 4 * s + k + 1)
                    for t in range(s * GT + 2 * k, s * GT + 2 * k + n):
                        nc.vector.bn_stats(m.raw[:, t, :], g.res[:, t, :]).then_inc(row_stats, 1)
            dve.wait_ge(row_stats, NT)
            combine_moments(nc, dve, m, 0, NT, step, 0)
            dve.wait_ge(root, 1)
            nc.vector.reciprocal(m.rstd[:], m.rstd[:])


def slice_tokens(nc, sem, sb, g):
    RING = 4
    LAG = 2
    x2_ready = sem("h_x2_ready")
    turned = sem("h_turned")
    xT_high = sem("h_xT_high")
    xT_low = sem("h_xT_low")
    logit_made = sem("h_logit_made")
    max_ready = sem("h_max_ready")
    shifted = sem("h_shifted")
    exp_ready = sem("h_exp_ready")
    sum_ready = sem("h_sum_ready")
    inv_ready = sem("h_inv_ready")
    w_ready = sem("h_w_ready")
    w_turned = sem("h_w_turned")
    wT_ready = sem("h_wT_ready")
    tok_made = sem("h_tok_made")
    x_high, x_low = sem("h_x_high"), sem("h_x_low")
    w_high, w_low = sem("h_w_high"), sem("h_w_low")
    ones_ready = sem("h_ones_ready")
    x2 = [sb(f"x2_{p}", [P, XW], F32) for p in range(RING)]
    x2h = [sb(f"x2h_{p}", [P, XW], F32R) for p in range(2)]
    x2l = [sb(f"x2l_{p}", [P, XW], F32R) for p in range(2)]
    xTh = [sb(f"xTh_{p}", [P, CB, P], F32R) for p in range(2)]
    xTl = [sb(f"xTl_{p}", [P, CB, P], F32R) for p in range(2)]
    ex = [sb(f"ex_{p}", [P, HG], F32) for p in range(RING)]
    wh = [sb(f"wh_{p}", [P, HG], F32R) for p in range(2)]
    wl = [sb(f"wl_{p}", [P, HG], F32R) for p in range(2)]
    neg_max = [sb(f"neg_max{p}", [P, FH], F32) for p in range(2)]
    tot = [sb(f"tot{p}", [P, FH], F32) for p in range(2)]
    m = g.mom
    tps = g.ps[0]
    lps = [g.ps[1], g.ps[2]]
    wps = g.ps[3]
    acc = g.ps[4:8]
    heads = lambda ap: ap.rearrange("p (h n) -> p h n", h=FH)
    wide = lambda ap: ap.unsqueeze(2).to_broadcast([P, FH, FG])
    blocks = lambda ap: ap.rearrange("p (b n) -> p b n", b=CB)

    def is_before(t, bound):
        return isinstance(t, int) and t < bound

    def exists(t):
        return not (isinstance(t, int) and t >= NT)

    def over_tiles(eng, step):
        for t in range(RING):
            step(t, t)
        whole = (NT - 2) // RING
        with eng.Fori(1, whole) as i:
            for r in range(RING):
                step(RING * i + r, r)
        for t in range(RING * whole, NT):
            step(t, t % RING)

    with nc.Block() as block:
        @block.tensor
        def _(pe):
            def turn_x(t, r):
                pe.wait_ge(x2_ready, t + 1)
                if not is_before(t, 1):
                    pe.wait_ge(xT_low, t)
                for b in range(CB):
                    mm = nc.tensor.transpose(tps[:, ds(b * P, P)], x2[r][:, ds(b * P, P)], g.ident[:])
                mm.then_inc(turned, 1)

            def logits(t, r):
                bank = lps[r % 2][:]
                pe.wait_ge(xT_low, t + 1)
                if not is_before(t, 2):
                    pe.wait_ge(shifted, t - 1)
                nc.tensor.matmul(bank, g.ones2[:], g.logit_bias[:], start=True, stop=False)
                for b in range(CB):
                    for x, y in ((xTh, g.logit_high), (xTh, g.logit_low), (xTl, g.logit_high)):
                        mm = nc.tensor.matmul(bank, x[r % 2][:, b, :], y[:, b, :], start=False,
                                              stop=b == CB - 1 and x is xTl)
                mm.then_inc(logit_made, 1)

            def turn_w(t, r):
                pe.wait_ge(w_ready, t + 1)
                if not is_before(t, 1):
                    pe.wait_ge(wT_ready, t)
                for q in range(HGB):
                    mm = nc.tensor.transpose(wps[:, ds(q * P, P)], ex[r][:, ds(q * P, P)], g.ident[:])
                mm.then_inc(w_turned, 1)

            def tokens(t, r):
                rows = rows_of(t)
                pe.wait_ge(x_low, t + 1)
                pe.wait_ge(w_high, 2 * t + 2)
                for x, y in ((wh, x2h), (wh, x2l), (wl, x2h)):
                    if x is wl:
                        pe.wait_ge(w_low, 2 * t + 2)
                    for q in range(HGB):
                        mm = nc.tensor.matmul(acc[q][:, 0:XW], x[r % 2][0:rows, ds(q * P, P)], y[r % 2][0:rows, :],
                                              start=is_before(t, 1) and x is wh and y is x2h,
                                              stop=is_known(t, NT - 1) and x is wl)
                mm.then_inc(tok_made, 1)

            def step(t, r):
                logits(t, r)
                if not is_before(t, LAG):
                    turn_w(t - LAG, (r - LAG) % RING)
                if exists(t + 1):
                    turn_x(t + 1, (r + 1) % RING)
                if not is_before(t, LAG):
                    tokens(t - LAG, (r - LAG) % RING)

            turn_x(0, 0)
            over_tiles(pe, step)
            for t in range(NT - LAG, NT):
                turn_w(t, t % RING)
                tokens(t, t % RING)

        @block.scalar
        def _(act):
            A = nc.scalar

            def copy_xT(t, r):
                act.wait_ge(turned, t + 1)
                A.activation(xTh[r % 2][:], blocks(tps[:, 0:C]), ACT.Copy).then_inc(xT_high, 1)

            def expo(t, r):
                act.wait_ge(shifted, t + 1)
                A.activation(ex[r][:], ex[r][:], ACT.Exp).then_inc(exp_ready, 1)

            def copy_w(t):
                act.wait_ge(w_turned, t + 1)
                A.activation(g.wT[:, :, ds(t * P, P)], wps[:].rearrange("p (q n) -> p q n", q=HGB),
                             ACT.Copy).then_inc(wT_ready, 1)

            def round_both(t, r):
                act.wait_ge(x2_ready, t + 1)
                if is_known(t, NT - 1):
                    act.wait_ge(tok_made, t - 1)
                A.activation(x2h[r % 2][:], x2[r][:], ACT.Copy).then_inc(x_high, 1)
                act.wait_ge(w_ready, t + 1)
                for k in range(2):
                    cols = ds(k * HG // 2, HG // 2)
                    A.activation(wh[r % 2][:, cols], ex[r][:, cols], ACT.Copy).then_inc(w_high, 1)

            def step(t, r):
                if not is_before(t, LAG):
                    copy_w(t - LAG)
                if exists(t + 1):
                    copy_xT(t + 1, (r + 1) % RING)
                expo(t, r)
                if not is_before(t, 1):
                    round_both(t - 1, (r - 1) % RING)

            copy_xT(0, 0)
            over_tiles(act, step)
            round_both(NT - 1, (NT - 1) % RING)
            for t in range(NT - LAG, NT):
                copy_w(t)

        @block.gpsimd
        def _(pool):
            G = nc.gpsimd

            def low_halves(t, r):
                pool.wait_ge(x_high, t + 1)
                G.tensor_tensor(x2l[r % 2][:], x2[r][:], x2h[r % 2][:].bitcast(F32), ALU.subtract).then_inc(x_low, 1)
                for k in range(2):
                    cols = ds(k * HG // 2, HG // 2)
                    pool.wait_ge(w_high, 2 * t + k + 1)
                    G.tensor_tensor(wl[r % 2][:, cols], ex[r][:, cols], wh[r % 2][:, cols].bitcast(F32),
                                    ALU.subtract).then_inc(w_low, 1)

            def step(t, r):
                if not is_before(t, 1):
                    low_halves(t - 1, (r - 1) % RING)

            over_tiles(pool, step)
            low_halves(NT - 1, (NT - 1) % RING)

        @block.vector
        def _(dve):
            V = nc.vector

            def normalise(t, r):
                if not is_before(t, RING):
                    dve.wait_ge(x_low, t - RING + 1)
                V.tensor_scalar(x2[r][:, 0:C], g.res[:, t, :], m.mean[:, ds(t, 1)], m.rstd[:, ds(t, 1)],
                                ALU.subtract, ALU.mult).then_inc(x2_ready, 1)

            def low_xT(t, r):
                dve.wait_ge(xT_high, t + 1)
                V.tensor_tensor(xTl[r % 2][:], blocks(tps[:, 0:C]), xTh[r % 2][:].bitcast(F32),
                                ALU.subtract).then_inc(xT_low, 1)

            def shift(t, r):
                dve.wait_ge(logit_made, t + 1)
                V.tensor_reduce(neg_max[r % 2][:], heads(lps[r % 2][:]), X, ALU.max, negate=True).then_inc(max_ready, 1)
                dve.wait_ge(max_ready, t + 1)
                V.tensor_tensor(heads(ex[r][:]), heads(lps[r % 2][:]), wide(neg_max[r % 2][:]),
                                ALU.add).then_inc(shifted, 1)

            def divide(t, r):
                dve.wait_ge(exp_ready, t + 1)
                V.tensor_reduce(tot[r % 2][:], heads(ex[r][:]), X, ALU.add).then_inc(sum_ready, 1)
                dve.wait_ge(sum_ready, t + 1)
                V.reciprocal(tot[r % 2][:], tot[r % 2][:]).then_inc(inv_ready, 1)
                dve.wait_ge(inv_ready, t + 1)
                V.tensor_tensor(heads(ex[r][:]), heads(ex[r][:]), wide(tot[r % 2][:]), ALU.mult).then_inc(w_ready, 1)

            def step(t, r):
                if exists(t + 2):
                    normalise(t + 2, (r + 2) % RING)
                shift(t, r)
                if exists(t + 1):
                    low_xT(t + 1, (r + 1) % RING)
                if not is_before(t, 1):
                    divide(t - 1, (r - 1) % RING)

            for r in range(RING):
                V.memset(x2[r][:, C:C + 1], 1.0).then_inc(ones_ready, 1)
                V.memset(x2[r][:, C + 1:XW], 0.0).then_inc(ones_ready, 1)
            dve.wait_ge(ones_ready, 2 * RING)
            normalise(0, 0)
            normalise(1, 1)
            low_xT(0, 0)
            over_tiles(dve, step)
            divide(NT - 1, (NT - 1) % RING)


def slice_attention(nc, sem, sb, g):
    w = g.w
    w_fx = sb("w_fx", [P, CB, FH * FD], F32)
    b_fx = sb("b_fx", [1, FH * FD], F32)
    w_q = sb("w_q", [FD, FD], F32)
    w_k = sb("w_k", [FD, FD], F32)
    w_v = sb("w_v", [FD, FD], F32)
    w_out = sb("w_out", [FD, FH, C], F32)
    norm = sb("norm", [P, HGB, 2], F32)
    tok = sb("tok", [P, HGB, XW], F32)
    tokT = sb("tokT", [P, CB, HG], F32)
    share = sb("share", [1, HG], F32)
    fxT = sb("fxT", [FD, HG], F32)
    qT = sb("qT", [FD, HG], F32)
    kT = sb("kT", [FD, HG], F32)
    v = sb("v", [FG, FH * FD], F32)
    at = sb("at", [FG, HG], F32)
    atT = sb("atT", [FG, HG], F32)
    neg = sb("neg", [FG, FH], F32)
    tot = sb("a_tot", [FG, FH], F32)
    oT = qT
    loaded = sem("i_loaded")
    vec = sem("i_vec")
    mat = sem("i_mat")
    expo = sem("i_exp")
    acc = g.ps[4:8]
    heads = lambda ap: ap.rearrange("p (h n) -> p h n", h=FH)
    wide = lambda ap: ap.unsqueeze(2).to_broadcast([FG, FH, FG])

    with nc.Block() as block:
        @block.sync
        def _(sp):
            for t, src in ((w_fx, w["ffn_W_fx"].rearrange("(b p) n -> p b n", p=P)),
                           (b_fx, w["ffn_b_fx"].rearrange("(a n) -> a n", a=1)),
                           (w_q, w["ffn_W_q"]), (w_k, w["ffn_W_k"]), (w_v, w["ffn_W_v"]),
                           (w_out, w["ffn_W_out"].rearrange("(h d) n -> d h n", h=FH))):
                sp.dma_start(t[:], src).then_inc(loaded, 16)

        @block.vector
        def _(dve):
            V = nc.vector
            for q in range(HGB):
                V.tensor_scalar(norm[:, q, 0:1], acc[q][:, C:C + 1], EPS, None, ALU.add).then_inc(vec, 1)
            dve.wait_ge(vec, 4)
            V.reciprocal(norm[:, :, 1], norm[:, :, 0]).then_inc(vec, 1)
            dve.wait_ge(vec, 5)
            for q in range(HGB):
                V.tensor_scalar(tok[:, q, :], acc[q][:, 0:XW], norm[:, q, 1:2], None, ALU.mult).then_inc(vec, 1)
            dve.wait_ge(mat, 1)
            for b in range(CB):
                V.tensor_copy(tokT[:, b, :], g.ps[b][:]).then_inc(vec, 1)
            V.tensor_copy(share[:], g.ps[2][0:1, :]).then_inc(vec, 1)
            dve.wait_ge(mat, 2)
            V.tensor_copy(fxT[:], g.ps[3][0:FD, :]).then_inc(vec, 1)
            dve.wait_ge(mat, 3)
            V.tensor_copy(qT[:], g.ps[4][0:FD, :]).then_inc(vec, 1)
            V.tensor_copy(kT[:], g.ps[5][0:FD, :]).then_inc(vec, 1)
            V.tensor_copy(v[:], g.ps[6][0:FG, :]).then_inc(vec, 1)
            dve.wait_ge(mat, 4)
            V.tensor_reduce(neg[:], heads(g.ps[7][0:FG, :]), X, ALU.max, negate=True).then_inc(vec, 1)
            dve.wait_ge(vec, 17)
            V.tensor_tensor(heads(at[:]), heads(g.ps[7][0:FG, :]), wide(neg[:]), ALU.add).then_inc(vec, 1)
            dve.wait_ge(expo, 1)
            V.tensor_reduce(tot[:], heads(at[:]), X, ALU.add).then_inc(vec, 1)
            dve.wait_ge(vec, 19)
            V.reciprocal(tot[:], tot[:]).then_inc(vec, 1)
            dve.wait_ge(vec, 20)
            V.tensor_tensor(heads(at[:]), heads(at[:]), wide(tot[:]), ALU.mult).then_inc(vec, 1)
            dve.wait_ge(mat, 5)
            V.tensor_copy(atT[:], g.ps[0][0:FG, :]).then_inc(vec, 1)
            dve.wait_ge(mat, 6)
            V.tensor_copy(oT[:], g.ps[1][0:FD, :]).then_inc(vec, 1)
            dve.wait_ge(mat, 7)
            for q in range(HGB):
                V.tensor_copy(g.m_out[:, q, :], g.ps[2 + q][:, 0:C])

        @block.scalar
        def _(act):
            act.wait_ge(vec, 18)
            nc.scalar.activation(at[:], at[:], ACT.Exp, scale=float(FD) ** -0.5).then_inc(expo, 1)

        @block.tensor
        def _(pe):
            T = nc.tensor
            for q in range(HGB):
                pe.wait_ge(vec, 5 + q + 1)
                for b in range(CB):
                    T.transpose(g.ps[b][:, ds(q * P, P)], tok[:, q, ds(b * P, P)], g.ident[:])
                mm = T.transpose(g.ps[2][0:1, ds(q * P, P)], tok[:, q, C:C + 1], g.ident[:])
            mm.then_inc(mat, 1)
            pe.wait_ge(loaded, 96)
            pe.wait_ge(vec, 12)
            for h in range(FH):
                out = g.ps[3][0:FD, ds(h * FG, FG)]
                for b in range(CB):
                    T.matmul(out, w_fx[:, b, ds(h * FD, FD)], tokT[:, b, ds(h * FG, FG)], start=b == 0, stop=False)
                mm = T.matmul(out, b_fx[:, ds(h * FD, FD)], share[:, ds(h * FG, FG)], start=False, stop=True)
            mm.then_inc(mat, 1)
            pe.wait_ge(vec, 13)
            T.matmul(g.ps[4][0:FD, :], w_q[:], fxT[:], start=True, stop=True)
            T.matmul(g.ps[5][0:FD, :], w_k[:], fxT[:], start=True, stop=True)
            for h in range(FH):
                mm = T.matmul(g.ps[6][0:FG, ds(h * FD, FD)], fxT[:, ds(h * FG, FG)], w_v[:], start=True, stop=True)
            mm.then_inc(mat, 1)
            pe.wait_ge(vec, 16)
            for h in range(FH):
                mm = T.matmul(g.ps[7][0:FG, ds(h * FG, FG)], qT[:, ds(h * FG, FG)], kT[:, ds(h * FG, FG)],
                              start=True, stop=True)
            mm.then_inc(mat, 1)
            pe.wait_ge(vec, 21)
            for h in range(FH):
                mm = T.transpose(g.ps[0][0:FG, ds(h * FG, FG)], at[:, ds(h * FG, FG)], g.ident[0:FG, 0:FG])
            mm.then_inc(mat, 1)
            pe.wait_ge(vec, 22)
            for h in range(FH):
                mm = T.matmul(g.ps[1][0:FD, ds(h * FG, FG)], v[:, ds(h * FD, FD)], atT[:, ds(h * FG, FG)],
                              start=True, stop=True)
            mm.then_inc(mat, 1)
            pe.wait_ge(vec, 23)
            for h in range(FH):
                mm = T.matmul(g.ps[2 + h // 2][ds(h % 2 * FG, FG), 0:C], oT[:, ds(h * FG, FG)], w_out[:, h, :],
                              start=True, stop=True)
            mm.then_inc(mat, 1)


def slice_output(nc, sem, sb, g):
    ready = sem("j_ready")
    stored = [sem(f"j_stored{p}") for p in range(2)]
    m_ready = sem("j_m_ready")
    high_ready = sem("j_high_ready")
    low_ready = sem("j_low_ready")
    m_high = sb("m_high", [P, HGB, C], F32R)
    m_low = sb("m_low", [P, HGB, C], F32R)
    w_high = [sb(f"w_high{p}", [P, HGB, P], F32R) for p in range(2)]
    w_low = [sb(f"w_low{p}", [P, HGB, P], F32R) for p in range(2)]
    multiplied = sem("j_multiplied")
    yps = g.ps

    with nc.Block() as block:
        @block.tensor
        def _(pe):
            pe.wait_ge(m_ready, 2)
            for u in range(NT):
                if u % 2 == 0 and u >= 16:
                    pe.wait_ge(ready, u // 2 - 7)
                out = yps[u // 2 % 8][:, ds(u % 2 * C, C)]
                nc.tensor.matmul(out, g.ones2[:], g.b_out[:], start=True, stop=False)
                pe.wait_ge(high_ready, u + 1)
                for x, y in ((w_high, m_high), (w_high, m_low), (w_low, m_high)):
                    if x is w_low:
                        pe.wait_ge(low_ready, u + 1)
                    for q in range(HGB):
                        mm = nc.tensor.matmul(out, x[u % 2][:, q, :], y[:, q, :], start=False,
                                              stop=x is w_low and q == HGB - 1)
                mm.then_inc(multiplied, 1)

        @block.scalar
        def _(act):
            for u in range(NT):
                if u >= 2:
                    act.wait_ge(multiplied, u - 1)
                nc.scalar.activation(w_high[u % 2][:], g.wT[:, :, ds(u * P, P)], ACT.Copy).then_inc(high_ready, 1)

        @block.vector
        def _(dve):
            nc.vector.tensor_copy(m_high[:], g.m_out[:]).then_inc(m_ready, 1)
            dve.wait_ge(m_ready, 1)
            nc.vector.tensor_tensor(m_low[:], g.m_out[:], m_high[:].bitcast(F32), ALU.subtract).then_inc(m_ready, 1)

            def low(u):
                dve.wait_ge(high_ready, u + 1)
                if u >= 2:
                    dve.wait_ge(multiplied, u - 1)
                nc.vector.tensor_tensor(w_low[u % 2][:], g.wT[:, :, ds(u * P, P)], w_high[u % 2][:].bitcast(F32),
                                        ALU.subtract).then_inc(low_ready, 1)

            def add(k):
                n = min(2, NT - 2 * k)
                dve.wait_ge(multiplied, 2 * k + n)
                here = g.res[:, ds(2 * k, n), :]
                nc.vector.tensor_tensor(here, yps[k % 8][:, 0:n * C].rearrange("p (t c) -> p t c", c=C), here,
                                        ALU.add).then_inc(ready, 1)

            for u in range(NT):
                low(u)
                if u % 2 and u >= 3:
                    add(u // 2 - 1)
            add(NT // 2 - 1)
            add(NT // 2)

        @block.sync
        def _(sp):
            done = 0
            whole = NT - 1
            for t0 in range(0, whole, 8):
                sp.wait_ge(ready, t0 // 2 + 4)
                sp.dma_start(split_rows(g.out_dram, t0, 8), g.res[:, t0:t0 + 8, :]).then_inc(stored[0], 16)
                done += 16
            sp.wait_ge(ready, -(-NT // 2))
            sp.dma_start(g.out_dram[whole * P:NODES, :], g.res[0:TAIL, whole, :]).then_inc(stored[1], 16)
            sp.wait_ge(stored[0], done)
            sp.wait_ge(stored[1], 16)


def gps_layer(nc, w, x, attr_T, src_rows, src_cols, dst_cols, dst_late, out):
    with ExitStack() as ctx:
        def sem(name):
            return ctx.enter_context(nc.semaphore(name))

        def sb(name, shape, dt):
            return ctx.enter_context(nc.sbuf_tensor(name, shape, dt))

        def scoped(stage, *args):
            with ExitStack() as inner:
                stage(nc, sem, lambda *a: inner.enter_context(nc.sbuf_tensor(*a)), *args)

        g = Shared()
        g.w, g.x_dram, g.attr_T, g.out_dram = w, x, attr_T, out
        g.src_rows, g.src_cols, g.dst_cols, g.dst_late = src_rows, src_cols, dst_cols, dst_late
        g.xn_dram = nc.dram_tensor("xn_rows", [NPAD, C], F32).ap()
        g.res_dram = nc.dram_tensor("res_rows", [NPAD, C], F32).ap()
        g.ends_dram = nc.dram_tensor("window_ends", [2, NW], F32).ap()
        g.sums_dram = [nc.dram_tensor(f"sums{k}", [ROWS, C], F32).ap() for k in range(TABLES)]
        g.ps = [ctx.enter_context(nc.psum_tensor(f"bank{b}", [P, 512], F32)) for b in range(8)]
        g.ident = sb("ident", [P, P], F32)
        g.earlier = sb("earlier", [P, P], F32)
        g.trash_i = sb("trash_i", [P, 1], I32)
        g.mom = Moments(sb, "mom")
        g.ones2 = sb("ones2", [BIAS_ROWS, P], F32R)
        g.biases = []
        g.bf2, g.bproj, g.b_out = (bias_row(sb, g, name) for name in ("gnn_bf2", "mix_bproj", "ffn_b_out"))
        with ExitStack() as mixing:
            sb_mix = lambda *a: mixing.enter_context(nc.sbuf_tensor(*a))
            g.weights = mixing_weights(sb_mix, g)
            g.gate = sb_mix("gate", [P, CB, GC], F32)
            g.zeros = g.gate[:].rearrange("p f n -> p (f n)")[:, 0:ROWS // P * C // CLEARS]
            g.table_clear = [sem(f"table_clear{k}") for k in range(TABLES)]
            scoped(first_layernorm, g)
            g.xT = sb_mix("xT", [P, CB, NPAD], F32)
            g.k_max = sb_mix("k_max", [P, CB, 2 * NG], F32)
            g.neg_k_max = sb_mix("neg_k_max", [P, CB], F32)
            g.k_sum = sb_mix("k_sum", [P, CB, 2 * NG], F32)
            g.k_tot = sb_mix("k_tot", [P, CB], F32)
            g.k_inv = sb_mix("k_inv", [P, CB], F32)
            g.bg1f = sb_mix("bg1f", [GH, 1], F32)
            g.wg1f = sb_mix("wg1f", [P, CB, GH], F32)
            g.head_mask = sb_mix("head_mask", [P, P], F32)
            g.wqm = sb_mix("wqm", [P, CB, C], F32)
            scoped(messages_and_attention, g)
        g.res = sb("res", [P, NT, C], F32)
        g.logit_high = sb("logit_high", [P, CB, HG], F32R)
        g.logit_low = sb("logit_low", [P, CB, HG], F32R)
        g.logit_bias = sb("logit_bias", [BIAS_ROWS, HG], F32R)
        scoped(update_nodes, g)
        with ExitStack() as late:
            sb_late = lambda *a: late.enter_context(nc.sbuf_tensor(*a))
            g.m_out = sb_late("m_out", [P, HGB, C], F32)
            g.wT = sb_late("wT", [P, HGB, NPAD], F32)
            scoped(slice_tokens, g)
            scoped(slice_attention, g)
            scoped(slice_output, g)


def kernel(**inputs):
    import numpy as np
    from concourse import bacc
    from concourse.bass_utils import run_bass_kernel_spmd

    a = {k: np.asarray(v) for k, v in inputs.items()}
    attr_T = np.zeros((EF, EPAD), np.float32)
    attr_T[:, :EDGES] = a["edge_attr_20"].T
    src = np.full((EPAD,), PAD_SRC, np.int32)
    src[:EDGES] = a["src"]
    dst = np.zeros((EPAD,), np.int32)
    dst[:EDGES] = a["dst"]
    arrays = {
        "x": a["x"], "attr_T": attr_T, "src_rows": src.reshape(NCH, EC),
        "src_cols": np.ascontiguousarray(src.reshape(-1, P).T),
        "dst_cols": np.ascontiguousarray(dst.reshape(-1, P).T),
        "dst_late": np.ascontiguousarray(dst.reshape(NCH, EC)[:, EC - WINDOWED * P:]),
    }
    weights = {k[3:]: v for k, v in a.items() if k.startswith("L0_")}
    weights["mix_WqT"] = np.ascontiguousarray(weights["mix_Wqkv"][:, :C].T)
    weights["ffn_W_xT"] = np.ascontiguousarray(weights.pop("ffn_W_x").reshape(C, FH, FD).transpose(2, 1, 0))

    nc = bacc.Bacc("TRN2", target_bir_lowering=False, num_devices=1)
    declare = lambda name, v: nc.dram_tensor(name, v.shape, mybir.dt.from_np(v.dtype), kind="ExternalInput").ap()
    io = {k: declare(k, v) for k, v in arrays.items()}
    w = {k: declare("w_" + k, v) for k, v in weights.items()}
    arrays.update({"w_" + k: v for k, v in weights.items()})
    out = nc.dram_tensor("out", (NODES, C), F32, kind="ExternalOutput").ap()
    gps_layer(nc, w, out=out, **io)
    r = run_bass_kernel_spmd(nc, [arrays], core_ids=[0])
    return r.results[0]["out"]
```
